# Optimizing a Trainium2 kernel written in Bass

```python
import numpy as np
import jax
import jax.numpy as jnp

def _softmax(x, axis=-1):
    return jax.nn.softmax(x, axis=axis)

def _gelu(x):
    return jax.nn.gelu(x, approximate=True)

def _silu(x):
    return jax.nn.silu(x)

def _sigmoid(x):
    return jax.nn.sigmoid(x)

def _layernorm(x, axis=-1, eps=1e-05):
    m = jnp.mean(x, axis=axis, keepdims=True)
    v = jnp.var(x, axis=axis, keepdims=True)
    return (x - m) / jnp.sqrt(v + eps)

def _scatter_add(tgt, idx, src, axis=0):
    return tgt.at[idx].add(src)

def _segment_sum(src, seg, n):
    return jax.ops.segment_sum(src, seg, n)
kernel_name = 'mk_decoder_preln_d2_seqx_r8_ee2adb'

def setup_inputs(seed: int=0):
    np.random.seed(seed)
    _w = jnp.asarray

    def _rec_inputs():
        import jax
        import jax.numpy as jnp
        _rk = jax.random.key(seed)
        x = -0.0002928 + 1 * jax.random.normal(jax.random.fold_in(_rk, 1), (8, 128, 256), jnp.float32)
        _lenS = 128 - jax.random.randint(jax.random.fold_in(_rk, 7), (8,), 0, max(1, 128 // 4) + 1, jnp.int32)
        _lenS2 = 128 - jax.random.randint(jax.random.fold_in(_rk, 8), (8,), 0, max(1, 128 // 4) + 1, jnp.int32)
        fside_S2_0 = -0.00337071 + 1.01897 * jax.random.normal(jax.random.fold_in(_rk, 11), (128,), jnp.float32)
        _ctx_2048P = jax.random.normal(jax.random.fold_in(_rk, 12), (8, 16, 256), jnp.float32)
        _ctx_2048c = jax.random.dirichlet(jax.random.fold_in(_rk, 512), 0.3 * jnp.ones((16,), jnp.float32), (8, 128))
        _ctx_2048t = jnp.einsum('bsk,bkd->bsd', _ctx_2048c, _ctx_2048P)
        _ctx_2048t = _ctx_2048t * jax.lax.rsqrt(jnp.mean(jnp.square(_ctx_2048t)) + 1e-12) * 0.953939
        ctx_2048 = 0.000675642 + 1.00031 * (_ctx_2048t + 0.3 * jax.random.normal(jax.random.fold_in(_rk, 612), (8, 128, 256), jnp.float32))
        return (x, fside_S2_0, ctx_2048)
    x, fside_S2_0, ctx_2048 = _rec_inputs()

    def _L0_attn_setup():
        import jax, jax.numpy as jnp
        import numpy as np
        NQ, NKV, HD, SW = (32, 8, 64, 64)
        QM = NQ // NKV

        def _rope_tables(L):
            inv_freq = (1.0 / 1024.0) ** jnp.linspace(0.0, 1.0, HD // 4)
            inv_freq = jnp.concatenate([inv_freq, jnp.zeros(HD // 4)])
            theta = jnp.arange(L, dtype=jnp.float32)[:, None] * inv_freq[None, :]
            return (jnp.cos(theta), jnp.sin(theta))

        def _apply_rope(x, cos, sin):
            x1, x2 = jnp.split(x, 2, axis=-1)
            return jnp.concatenate([x1 * cos + x2 * sin, -x1 * sin + x2 * cos], axis=-1)
        key = jax.random.key(seed)
        k1, k2, k3 = jax.random.split(key, 3)
        B, L, D = (1, 256, 256)
        x = jax.random.normal(k1, (B, L, D), jnp.float32)
        W_qkv = jax.random.normal(k2, (D, (NQ + 2 * NKV) * HD), jnp.float32) * 0.02
        W_out = jax.random.normal(k3, (NQ * HD, D), jnp.float32) * 0.02
        s = jnp.zeros((1, NKV, QM), jnp.float32)
        return {'x': x, 'W_qkv': W_qkv, 'W_out': W_out, 's': s}
    _L0_attn_all = _L0_attn_setup()
    _L0_attn_in = {k: v for k, v in _L0_attn_all.items() if k in ('W_qkv', 'W_out', 's')}
    del _L0_attn_all

    def _L0_xattn_setup():
        import jax, jax.numpy as jnp
        import numpy as np
        key = jax.random.key(seed)
        ks = jax.random.split(key, 5)
        B, D, L, NH = (2, 128, 256, 8)
        H = D // NH
        return {'v': jax.random.normal(ks[0], (B, D, L), jnp.float32), 'k': jax.random.normal(ks[1], (H, L), jnp.float32) * 0.1, 'bias': jax.random.normal(ks[2], (D,), jnp.float32), 'x1': jax.random.normal(ks[3], (B, D, L), jnp.float32), 'x2': jax.random.normal(ks[4], (B, D, L), jnp.float32), 'num_heads': NH}
    _L0_xattn_all = _L0_xattn_setup()
    _L0_xattn_in = {k: v for k, v in _L0_xattn_all.items() if k in ('k',)}
    del _L0_xattn_all

    def _L0_ffn_setup():
        import jax, jax.numpy as jnp
        import numpy as np
        H, I, E, K = (256, 512, 8, 2)
        B, S = (1, 256)

        def _silu_mul(gu):
            d = gu.shape[-1] // 2
            return jax.nn.silu(gu[..., :d]) * gu[..., d:]
        key = jax.random.key(seed)
        ks = jax.random.split(key, 6)
        w_scale = 0.02
        return {'x': jax.random.normal(ks[0], (B, S, H), jnp.float32), 'gate_w': jax.random.normal(ks[1], (H, E), jnp.float32) * w_scale, 'base_gate_up': jax.random.normal(ks[2], (H, 2 * I), jnp.float32) * w_scale, 'base_down': jax.random.normal(ks[3], (I, H), jnp.float32) * w_scale, 'expert_gate_up': jax.random.normal(ks[4], (E, H, 2 * I), jnp.float32) * w_scale, 'expert_down': jax.random.normal(ks[5], (E, I, H), jnp.float32) * w_scale}
    _L0_ffn_all = _L0_ffn_setup()
    _L0_ffn_in = {k: v for k, v in _L0_ffn_all.items() if k in ('gate_w', 'base_gate_up', 'base_down', 'expert_gate_up', 'expert_down')}
    del _L0_ffn_all

    def _L1_attn_setup():
        import jax, jax.numpy as jnp
        import numpy as np
        EMBED_DIM = 256
        NUM_HEADS = 16
        HEAD_DIM = EMBED_DIM // NUM_HEADS
        SCALE = HEAD_DIM ** (-0.5)
        NEG = -9000000000000000.0

        def _act_quant(x):
            s = 127.0 / jnp.clip(jnp.max(jnp.abs(x), axis=-1, keepdims=True), 1e-05)
            return jnp.clip(jnp.round(x * s), -128.0, 127.0) / s

        def _weight_quant(w):
            s = 1.0 / jnp.clip(jnp.mean(jnp.abs(w)), 1e-05)
            return jnp.clip(jnp.round(w * s), -1.0, 1.0) / s

        def _bitlinear(x, w):
            xq = x + jax.lax.stop_gradient(_act_quant(x) - x)
            wq = w + jax.lax.stop_gradient(_weight_quant(w) - w)
            return jnp.einsum('bnc,oc->bno', xq, wq)
        key = jax.random.key(seed)
        k1, k2, k3 = jax.random.split(key, 3)
        x = jax.random.normal(k1, (2, 256, EMBED_DIM), dtype=jnp.float32)
        w_qkv = jax.random.normal(k2, (3 * EMBED_DIM, EMBED_DIM), dtype=jnp.float32) * EMBED_DIM ** (-0.5)
        w_proj = jax.random.normal(k3, (EMBED_DIM, EMBED_DIM), dtype=jnp.float32) * EMBED_DIM ** (-0.5)
        return {'x': x, 'w_qkv': w_qkv, 'w_proj': w_proj}
    _L1_attn_all = _L1_attn_setup()
    _L1_attn_in = {k: v for k, v in _L1_attn_all.items() if k in ('w_qkv', 'w_proj')}
    del _L1_attn_all

    def _L1_xattn_setup():
        import jax, jax.numpy as jnp
        import numpy as np

        def _wkv(time_decay, time_first, k, v):
            w = -jnp.exp(time_decay)
            u = time_first
            B, T, C = k.shape
            aa = jnp.zeros((B, C), dtype=k.dtype)
            bb = jnp.zeros((B, C), dtype=k.dtype)
            pp = jnp.full((B, C), -1e+38, dtype=k.dtype)

            def step(carry, kv_t):
                aa, bb, pp = carry
                kt, vt = kv_t
                ww = u + kt
                q = jnp.maximum(pp, ww)
                e1 = jnp.exp(pp - q)
                e2 = jnp.exp(ww - q)
                y_t = (e1 * aa + e2 * vt) / (e1 * bb + e2)
                ww2 = pp + w
                q2 = jnp.maximum(ww2, kt)
                e1b = jnp.exp(ww2 - q2)
                e2b = jnp.exp(kt - q2)
                new_carry = (e1b * aa + e2b * vt, e1b * bb + e2b, q2)
                return (new_carry, y_t)
            ks = jnp.transpose(k, (1, 0, 2))
            vs = jnp.transpose(v, (1, 0, 2))
            _, ys = jax.lax.scan(step, (aa, bb, pp), (ks, vs))
            return jnp.transpose(ys, (1, 0, 2))
        key = jax.random.key(seed)
        k1, k2, k3, k4 = jax.random.split(key, 4)
        B, T, C = (8, 128, 256)
        return {'batch_size': B, 'seq_len': T, 'embedding_dim': C, 'time_decay': jax.random.normal(k1, (C,), dtype=jnp.float32), 'time_first': jax.random.normal(k2, (C,), dtype=jnp.float32), 'k': jax.random.normal(k3, (B, T, C), dtype=jnp.float32), 'v': jax.random.normal(k4, (B, T, C), dtype=jnp.float32)}
    _L1_xattn_all = _L1_xattn_setup()
    _L1_xattn_in = {k: v for k, v in _L1_xattn_all.items() if k in ('time_decay', 'time_first')}
    del _L1_xattn_all

    def _L1_ffn_setup():
        import jax, jax.numpy as jnp
        import numpy as np
        HIDDEN = 256
        INTER = 1024
        BATCH, LOCAL_SEQ = (2, 512)
        key = jax.random.key(seed)
        k1, k2, k3 = jax.random.split(key, 3)
        h_shard = jax.random.normal(k1, (BATCH, LOCAL_SEQ, HIDDEN), dtype=jnp.float32)
        w_gate_up = jax.random.normal(k2, (2 * INTER, HIDDEN), dtype=jnp.float32) * 0.02
        w_down = jax.random.normal(k3, (HIDDEN, INTER), dtype=jnp.float32) * 0.02
        return {'h_shard': h_shard, 'w_gate_up': w_gate_up, 'w_down': w_down}
    _L1_ffn_all = _L1_ffn_setup()
    _L1_ffn_in = {k: v for k, v in _L1_ffn_all.items() if k in ('w_gate_up', 'w_down')}
    del _L1_ffn_all
    return {'x': x, 'fside_S2_0': fside_S2_0, 'ctx_2048': ctx_2048, 'L0_attn_W_qkv': _L0_attn_in['W_qkv'], 'L0_attn_W_out': _L0_attn_in['W_out'], 'L0_attn_s': _L0_attn_in['s'], 'L0_xattn_k': _L0_xattn_in['k'], 'L0_ffn_gate_w': _L0_ffn_in['gate_w'], 'L0_ffn_base_gate_up': _L0_ffn_in['base_gate_up'], 'L0_ffn_base_down': _L0_ffn_in['base_down'], 'L0_ffn_expert_gate_up': _L0_ffn_in['expert_gate_up'], 'L0_ffn_expert_down': _L0_ffn_in['expert_down'], 'L1_attn_w_qkv': _L1_attn_in['w_qkv'], 'L1_attn_w_proj': _L1_attn_in['w_proj'], 'L1_xattn_time_decay': _L1_xattn_in['time_decay'], 'L1_xattn_time_first': _L1_xattn_in['time_first'], 'L1_ffn_w_gate_up': _L1_ffn_in['w_gate_up'], 'L1_ffn_w_down': _L1_ffn_in['w_down']}

def reference(x, fside_S2_0, ctx_2048, L0_attn_W_qkv, L0_attn_W_out, L0_attn_s, L0_xattn_k, L0_ffn_gate_w, L0_ffn_base_gate_up, L0_ffn_base_down, L0_ffn_expert_gate_up, L0_ffn_expert_down, L1_attn_w_qkv, L1_attn_w_proj, L1_xattn_time_decay, L1_xattn_time_first, L1_ffn_w_gate_up, L1_ffn_w_down):
    import jax
    import jax.numpy as jnp

    def _L0_attn_ref(x, W_qkv, W_out, s):
        import jax, jax.numpy as jnp
        import numpy as np
        NQ, NKV, HD, SW = (32, 8, 64, 64)
        QM = NQ // NKV

        def _rope_tables(L):
            inv_freq = (1.0 / 1024.0) ** jnp.linspace(0.0, 1.0, HD // 4)
            inv_freq = jnp.concatenate([inv_freq, jnp.zeros(HD // 4)])
            theta = jnp.arange(L, dtype=jnp.float32)[:, None] * inv_freq[None, :]
            return (jnp.cos(theta), jnp.sin(theta))

        def _apply_rope(x, cos, sin):
            x1, x2 = jnp.split(x, 2, axis=-1)
            return jnp.concatenate([x1 * cos + x2 * sin, -x1 * sin + x2 * cos], axis=-1)
        B, L, D = x.shape
        proj = x @ W_qkv
        q, k, v = jnp.split(proj, (NQ * HD, (NQ + NKV) * HD), axis=-1)
        cos, sin = _rope_tables(L)
        q = _apply_rope(q.reshape(B, L, NKV, QM, HD), cos[None, :, None, None, :], sin[None, :, None, None, :])
        k = _apply_rope(k.reshape(B, L, NKV, HD), cos[None, :, None, :], sin[None, :, None, :])
        v = v.reshape(B, L, NKV, HD)
        sm_scale = 1.0 / jnp.sqrt(jnp.float32(HD))
        attn = jnp.einsum('bqhmd,bkhd->bhmqk', q, k) * sm_scale
        q_pos = jnp.arange(L)[:, None]
        k_pos = jnp.arange(L)[None, :]
        mask = (q_pos >= k_pos) & (q_pos < k_pos + SW)
        attn = jnp.where(mask, -jnp.inf, attn)
        sink = jnp.broadcast_to(s[:, :, :, None, None], attn.shape[:-1] + (1,))
        w = jax.nn.softmax(jnp.concatenate([attn, sink], axis=-1), axis=-1)[..., :-1]
        out = jnp.einsum('bhmqk,bkhd->bqhmd', w, v).reshape(B, L, NQ * HD)
        return out @ W_out

    def _L0_xattn_ref(v, k, bias, x1, x2, num_heads):
        import jax, jax.numpy as jnp
        import numpy as np
        B, D, L = v.shape
        H = D // num_heads
        fft_size = 2 * L
        vr = v.reshape(B, H, num_heads, L)
        x1r = x1.reshape(B, H, num_heads, L)
        x2r = x2.reshape(B, H, num_heads, L)
        kv = vr[:, :, :, None, :] * x2r[:, :, None, :, :]
        k_f = jnp.fft.rfft(k.astype(jnp.float32), n=fft_size)
        y = jnp.fft.irfft(jnp.fft.rfft(kv, n=fft_size) * k_f[None, :, None, None, :], n=fft_size)[..., :L]
        skip = bias.astype(jnp.float32).reshape(H, num_heads)[None, :, :, None, None]
        y = y + kv * skip
        out = jnp.einsum('bhijl,bhil->bhjl', y, x1r)
        return out.reshape(B, D, L)

    def _L0_ffn_ref(x, gate_w, base_gate_up, base_down, expert_gate_up, expert_down):
        import jax, jax.numpy as jnp
        import numpy as np
        H, I, E, K = (256, 512, 8, 2)
        B, S = (1, 256)

        def _silu_mul(gu):
            d = gu.shape[-1] // 2
            return jax.nn.silu(gu[..., :d]) * gu[..., d:]
        base_y = _silu_mul(x @ base_gate_up) @ base_down
        b, s, h = x.shape
        xf = x.reshape(-1, h)
        n = xf.shape[0]
        n_exp = gate_w.shape[1]
        probs = jax.nn.softmax((xf @ gate_w).astype(jnp.float32), axis=-1)
        w, idx = jax.lax.top_k(probs, K)
        w = (w / w.sum(axis=-1, keepdims=True)).astype(x.dtype)
        comb = jnp.zeros((n, n_exp), x.dtype).at[jnp.arange(n)[:, None], idx].add(w)
        out = jnp.zeros_like(xf)
        for e in range(n_exp):
            y = _silu_mul(xf @ expert_gate_up[e]) @ expert_down[e]
            out = out + comb[:, e:e + 1] * y
        return out.reshape(b, s, h) + base_y

    def _L1_attn_ref(x, w_qkv, w_proj):
        import jax, jax.numpy as jnp
        import numpy as np
        EMBED_DIM = 256
        NUM_HEADS = 16
        HEAD_DIM = EMBED_DIM // NUM_HEADS
        SCALE = HEAD_DIM ** (-0.5)
        NEG = -9000000000000000.0

        def _act_quant(x):
            s = 127.0 / jnp.clip(jnp.max(jnp.abs(x), axis=-1, keepdims=True), 1e-05)
            return jnp.clip(jnp.round(x * s), -128.0, 127.0) / s

        def _weight_quant(w):
            s = 1.0 / jnp.clip(jnp.mean(jnp.abs(w)), 1e-05)
            return jnp.clip(jnp.round(w * s), -1.0, 1.0) / s

        def _bitlinear(x, w):
            xq = x + jax.lax.stop_gradient(_act_quant(x) - x)
            wq = w + jax.lax.stop_gradient(_weight_quant(w) - w)
            return jnp.einsum('bnc,oc->bno', xq, wq)
        B, N, C = x.shape
        H, D = (NUM_HEADS, HEAD_DIM)
        qkv = _bitlinear(x, w_qkv).reshape(B, N, 3, H, D)
        q, k, v = (qkv[:, :, 0], qkv[:, :, 1], qkv[:, :, 2])
        attn = jnp.einsum('bnhd,bmhd->bhnm', q, k) * SCALE
        causal = jnp.tril(jnp.ones((N, N), dtype=bool))
        attn = jnp.where(causal, attn, NEG)
        attn = jax.nn.softmax(attn, axis=-1)
        out = jnp.einsum('bhnm,bmhd->bnhd', attn, v).reshape(B, N, C)
        return _bitlinear(out, w_proj)

    def _L1_xattn_ref(batch_size, seq_len, embedding_dim, time_decay, time_first, k, v):
        import jax, jax.numpy as jnp
        import numpy as np

        def _wkv(time_decay, time_first, k, v):
            w = -jnp.exp(time_decay)
            u = time_first
            B, T, C = k.shape
            aa = jnp.zeros((B, C), dtype=k.dtype)
            bb = jnp.zeros((B, C), dtype=k.dtype)
            pp = jnp.full((B, C), -1e+38, dtype=k.dtype)

            def step(carry, kv_t):
                aa, bb, pp = carry
                kt, vt = kv_t
                ww = u + kt
                q = jnp.maximum(pp, ww)
                e1 = jnp.exp(pp - q)
                e2 = jnp.exp(ww - q)
                y_t = (e1 * aa + e2 * vt) / (e1 * bb + e2)
                ww2 = pp + w
                q2 = jnp.maximum(ww2, kt)
                e1b = jnp.exp(ww2 - q2)
                e2b = jnp.exp(kt - q2)
                new_carry = (e1b * aa + e2b * vt, e1b * bb + e2b, q2)
                return (new_carry, y_t)
            ks = jnp.transpose(k, (1, 0, 2))
            vs = jnp.transpose(v, (1, 0, 2))
            _, ys = jax.lax.scan(step, (aa, bb, pp), (ks, vs))
            return jnp.transpose(ys, (1, 0, 2))
        assert seq_len <= 128
        return _wkv(time_decay, time_first, k, v)

    def _L1_ffn_ref(h_shard, w_gate_up, w_down):
        import jax, jax.numpy as jnp
        import numpy as np
        HIDDEN = 256
        INTER = 1024
        BATCH, LOCAL_SEQ = (2, 512)
        batch, local_seq, hidden = h_shard.shape
        gate_up = jnp.einsum('bsh,oh->bso', h_shard, w_gate_up)
        gate, up = jnp.split(gate_up, 2, axis=-1)
        h = jax.nn.silu(gate) * up
        out = jnp.einsum('bsi,hi->bsh', h, w_down)
        return out
    x = x + _L0_attn_ref(_layernorm(x, axis=-1), L0_attn_W_qkv, L0_attn_W_out, L0_attn_s)
    x = x + _L0_xattn_ref(_layernorm(x, axis=-1), L0_xattn_k, fside_S2_0, ctx_2048, ctx_2048, 8)
    x = x + _L0_ffn_ref(_layernorm(x, axis=-1), L0_ffn_gate_w, L0_ffn_base_gate_up, L0_ffn_base_down, L0_ffn_expert_gate_up, L0_ffn_expert_down)
    x = x + _L1_attn_ref(_layernorm(x, axis=-1), L1_attn_w_qkv, L1_attn_w_proj)
    x = x + _L1_xattn_ref(8, 128, 256, L1_xattn_time_decay, L1_xattn_time_first, _layernorm(x, axis=-1), ctx_2048)
    x = x + _L1_ffn_ref(_layernorm(x, axis=-1), L1_ffn_w_gate_up, L1_ffn_w_down)
    return x

_drawn_inputs = setup_inputs


def setup_inputs(seed=0):
    import zlib

    import numpy as np

    out = dict(_drawn_inputs(seed))
    spreads = {'L0_attn_s': (0.0, 2.0)}
    factors = {'L0_ffn_gate_w': 8.0,
     'L0_ffn_base_gate_up': 8.0,
     'L0_ffn_base_down': 8.0,
     'L0_ffn_expert_gate_up': 8.0,
     'L0_ffn_expert_down': 8.0,
     'L1_ffn_w_gate_up': 8.0,
     'L1_ffn_w_down': 8.0,
     'L1_attn_w_qkv': 8.0,
     'L1_attn_w_proj': 8.0,
     'L1_xattn_time_decay': 4.826,
     'L1_xattn_time_first': 5.379}
    for name, (base, spread) in spreads.items():
        noise = np.random.default_rng([zlib.crc32(name.encode()), seed]).standard_normal(out[name].shape)
        drawn = base * np.exp(spread * noise) if base else spread * noise
        out[name] = jnp.asarray(drawn.astype(out[name].dtype))
    for name, factor in factors.items():
        out[name] = (out[name] * factor).astype(out[name].dtype)
    return out
```

```python
import numpy as np
from contextlib import ExitStack

import concourse.bass as bass
from concourse import mybir

F32 = mybir.dt.float32
BF16 = mybir.dt.bfloat16
ALU = mybir.AluOpType
ACT = mybir.ActivationFunctionType
AX = mybir.AxisListType

P = 128
B, S, D = 8, 128, 256
KD = D // P
LN_EPS = 1e-5
MASKED = -1e30

NQ, NKV, HD, WINDOW = 32, 8, 64, 64
QM = NQ // NKV
ROT = HD // 4
QKV = (NQ + 2 * NKV) * HD
CH = 512
QCH = NQ * HD // CH
PAIRS = NQ // 2
UNITS = 4
HU = NQ // UNITS

C_ID, C_SWA, C_CAUSAL, C_ROPE, C_LOWER, C_END = 0, 128, 256, 384, 416, 480


def constants():
    t = np.zeros((P, C_END), np.float32)
    q, k = np.arange(S)[:, None], np.arange(S)[None, :]
    t[:, C_ID:C_ID + P] = np.eye(P)
    t[:, C_SWA:C_SWA + S] = np.where((q >= k) & (q < k + WINDOW), MASKED, 0.0)
    t[:, C_CAUSAL:C_CAUSAL + S] = np.where(q >= k, 0.0, MASKED)
    freq = np.float32(1 / 1024) ** np.linspace(0, 1, ROT, dtype=np.float32)
    theta = np.arange(S, dtype=np.float32)[:, None] * freq[None, :]
    t[:, C_ROPE:C_ROPE + ROT] = np.cos(theta)
    t[:, C_ROPE + ROT:C_ROPE + 2 * ROT] = np.sin(theta)
    e = np.arange(8)
    t[:, C_LOWER:C_LOWER + 64] = (e[None, :] < e[:, None]).astype(np.float32).reshape(1, 64)
    return t


def whole(tensor, shape):
    return tensor[tuple(slice(None) for _ in shape)]


def layer0_attention(nc, g):
    with ExitStack() as ctx:
        def sb(name, shape, dt=F32):
            return whole(ctx.enter_context(nc.sbuf_tensor(name, shape, dt)), shape)

        def sem(name):
            return ctx.enter_context(nc.semaphore(name))

        wqkv = g.big_w[:, 0:KD * QKV].rearrange("p (k n) -> p k n", k=KD)
        wout = g.big_w[:, KD * QKV:KD * QKV + PAIRS * D].rearrange("p (t n) -> p t n", t=PAIRS)
        xn = sb("a_xn", [P, D])
        xT = sb("a_xT", [P, KD, S])
        qk_tok = sb("a_qk_tok", [P, (NQ + 2 * NKV) * HD])
        v_tok = sb("a_v_tok", [P, NKV * HD])
        qT = sb("a_qT", [P, PAIRS, S])
        kT = sb("a_kT", [P, NKV, S])
        rot_a = sb("a_rot_a", [P, 2, 8, 2, ROT])
        rot_b = sb("a_rot_b", [P, 2, 8, 2, ROT])
        prob = sb("a_prob", [P, 2, HU, S])
        probT = sb("a_probT", [P, 2, 2, 4 * S])
        oT = sb("a_oT", [P, PAIRS, S])
        sink8 = sb("a_sink8", [P, UNITS, HU])
        rmax = sb("a_rmax", [P, 2, HU])
        rowm = sb("a_rowm", [P, 2, HU])
        sinke = sb("a_sinke", [P, 2, HU])
        psum_p = sb("a_psum_p", [P, 2, HU])
        den = sb("a_den", [P, 2, HU])
        rden = sb("a_rden", [P, 2, HU])
        stats = sb("a_stats", [P, B, 6])
        mv = sb("a_mv", [P, B, 2])
        veps = sb("a_veps", [P, B])
        rstd = sb("a_rstd", [P, B, 1])
        sink_raw = sb("a_sink_raw", [P, NQ])
        ctx_tok = sb("a_ctx_tok", [P, B, D])

        const_in, x_in, ctx_in, sink_in = sem("const_in"), sem("x_in"), sem("ctx_in"), sem("sink_in")
        wq_in = [sem(f"wq_in{c}") for c in range(QCH + 2)]
        wout_in = sem("wout_in")
        masks_ready, sink_ready = sem("masks_ready"), sem("sink_ready")
        stats_done, mv_done, veps_done, rstd_done = sem("stats_done"), sem("mv_done"), sem("veps_done"), sem("rstd_done")
        ctxT_mm, ctxT_out = sem("ctxT_mm"), sem("ctxT_out")
        xn_ready, xT_mm, xT_ready = sem("a_xn_ready"), sem("a_xT_mm"), sem("a_xT_ready")
        proj_mm = sem("proj_mm")
        turned = sem("turned")
        straight = sem("straight")
        rope_done = sem("rope_done")
        v_ready = sem("v_ready")
        qkT_mm, qkT_ready = sem("qkT_mm"), sem("qkT_ready")
        score_mm, rmax_done, rowm_done, shifted, sinkd = (
            sem("score_mm"), sem("rmax_done"), sem("rowm_done"), sem("shifted"), sem("sinkd"))
        exp_done, sum_done, den_done, rden_done, prob_ready = (
            sem("exp_done"), sem("sum_done"), sem("den_done"), sem("rden_done"), sem("prob_ready"))
        probT_mm, probT_ready, av_mm, oT_ready, y_mm, x_added = (
            sem("probT_mm"), sem("probT_ready"), sem("av_mm"), sem("oT_ready"), sem("y_mm"), sem("x_added"))

        ps = g.ps
        S_BANK, PT_BANK, O_BANK, M_BANK = 0, 4, 6, 7
        NCH = QCH + 2
        NT = QCH + 2

        def chunk_copies(c):
            if c < QCH:
                return [qk_tok[:, c * CH:(c + 1) * CH].rearrange("p (h a r) -> p h a r", h=8, a=2)]
            k = qk_tok[:, QCH * CH:].rearrange("p (h d a r) -> p h d a r", h=NKV, d=2, a=2)
            return [k[:, :, 0], k[:, :, 1]]

        def chunk_bank(c):
            return O_BANK if c == 1 else M_BANK

        def scores(slot):
            return ps[:, S_BANK + 2 * slot:S_BANK + 2 * slot + 2, :]

        block = ctx.enter_context(nc.Block())

        @block.sync
        def _(sp):
            sp.dma_start(g.x_sb[:, :, :], g.x.rearrange("b s d -> s b d")).then_inc(x_in, 16)
            sp.dma_start(g.const[:, :], g.table[:, :]).then_inc(const_in, 16)
            src = g.w_qkv.rearrange("(k p) n -> p k n", k=KD)
            for c in range(NCH):
                sp.dma_start(wqkv[:, :, c * CH:(c + 1) * CH], src[:, :, c * CH:(c + 1) * CH]).then_inc(wq_in[c], 16)
            sp.dma_start(wout, g.w_out.rearrange("(t p) n -> p t n", t=PAIRS)).then_inc(wout_in, 16)

        @block.gpsimd
        def _(pool):
            def rope_add(c, n):
                pool.wait_ge(turned, n + 1)
                for dst in chunk_copies(c):
                    add = nc.gpsimd.tensor_tensor(dst[:, :, :, 0:ROT], rot_a[:, c % 2], rot_b[:, c % 2], ALU.add)
                add.then_inc(rope_done, 1)

            def body(b, has_next):
                for step in ("N0", "r0", "N1", "r1", "r2", "N2", "r3", "N3", "r4"):
                    k = int(step[1])
                    if step[0] == "N":
                        pool.wait_ge(rden_done, UNITS * b + k + 1)
                        nc.gpsimd.tensor_tensor(
                            prob[:, k % 2], prob[:, k % 2],
                            rden[:, k % 2, :].unsqueeze(2).to_broadcast([P, HU, S]), ALU.mult).then_inc(prob_ready, 1)
                    elif has_next:
                        rope_add(k, (QCH + 1) * (b + 1) + k)

            pool.wait_ge(mv_done, B)
            nc.gpsimd.tensor_scalar_add(veps[:, :], mv[:, :, 1], LN_EPS).then_inc(veps_done, 1)
            pool.wait_ge(veps_done, 1)
            pool.wait_ge(g.half_ready, 1)
            nc.gpsimd.tensor_tensor(rstd[:, :, 0], veps[:, :], g.neg_half[:, 0:B], ALU.pow).then_inc(rstd_done, 1)
            for c in range(QCH + 1):
                rope_add(c, c)
            with pool.Fori(0, B - 1) as b:
                body(b, True)
            body(B - 1, False)

        @block.scalar
        def _(act):
            act.dma_start(ctx_tok[:, :, :], g.ctx.rearrange("b s d -> s b d")).then_inc(ctx_in, 16)
            act.dma_start(sink_raw[:, :], g.sink.rearrange("a g m -> a (g m)").to_broadcast([P, NQ])).then_inc(sink_in, 16)

            def xT_out(b):
                act.wait_ge(xT_mm, b + 1)
                nc.scalar.copy(xT[:, :, :], ps[:, M_BANK, 0:KD * S].rearrange("p (k s) -> p k s", k=KD)).then_inc(xT_ready, 1)

            def straight_out(c, n):
                act.wait_ge(turned, (QCH + 1) * n + c + 1)
                bank = ps[:, chunk_bank(c), :].rearrange("p (h a r) -> p h a r", h=8, a=2)
                for dst in chunk_copies(c):
                    copy = nc.scalar.copy(dst[:, :, :, ROT:2 * ROT], bank[:, :, :, ROT:2 * ROT])
                copy.then_inc(straight, 1)

            def v_out(n):
                act.wait_ge(proj_mm, NCH * n + NCH)
                nc.scalar.copy(v_tok[:, :], ps[:, M_BANK, :]).then_inc(v_ready, 1)

            def qkT_out(t, n):
                act.wait_ge(qkT_mm, NT * n + t + 1)
                dst = qT[:, 4 * t:4 * t + 4, :] if t < QCH else kT[:, 4 * (t - QCH):4 * (t - QCH) + 4, :]
                nc.scalar.copy(dst, ps[:, S_BANK + t % 4, :].rearrange("p (t s) -> p t s", t=4)).then_inc(qkT_ready, 1)

            def exps(u, n):
                act.wait_ge(shifted, n + 1)
                nc.scalar.activation(prob[:, u % 2], prob[:, u % 2], ACT.Exp, scale=HD ** -0.5).then_inc(exp_done, 1)
                act.wait_ge(sinkd, n + 1)
                nc.scalar.activation(sinke[:, u % 2], sinke[:, u % 2], ACT.Exp, scale=HD ** -0.5).then_inc(exp_done, 1)

            def probT_out(u, n):
                for p in range(2):
                    act.wait_ge(probT_mm, 2 * n + p + 1)
                    nc.scalar.copy(probT[:, u % 2, p, :], ps[:, PT_BANK + p, :]).then_inc(probT_ready, 1)

            def oT_out(u, n):
                act.wait_ge(av_mm, n + 1)
                nc.scalar.copy(oT[:, 4 * u:4 * u + 4, :], ps[:, O_BANK, :].rearrange("p (t s) -> p t s", t=4)).then_inc(oT_ready, 1)

            def body(b, has_next):
                steps = "x e0 e1 n0 n1 P0 e2 o0 n2 P1 e3 o1 n3 P2 n4 o2 T0 T1 T2 P3 T3 o3 v T4 T5"
                for step in steps.split():
                    k = int(step[1]) if len(step) > 1 else 0
                    if step[0] == "e":
                        exps(k, UNITS * b + k)
                    elif step[0] == "P":
                        probT_out(k, UNITS * b + k)
                    elif step[0] == "o":
                        oT_out(k, UNITS * b + k)
                    elif has_next:
                        if step[0] == "x":
                            xT_out(b + 1)
                        elif step[0] == "n":
                            straight_out(k, b + 1)
                        elif step[0] == "T":
                            qkT_out(k, b + 1)
                        else:
                            v_out(b + 1)

            for h in range(4):
                act.wait_ge(ctxT_mm, h + 1)
                nc.scalar.copy(g.ctxT[:, :, 2 * h * S:2 * (h + 1) * S],
                               ps[:, h, :].rearrange("p (k s) -> p k s", k=KD)).then_inc(ctxT_out, 1)
            xT_out(0)
            for c in range(QCH + 1):
                straight_out(c, 0)
            v_out(0)
            for t in range(NT):
                qkT_out(t, 0)
            with act.Fori(0, B - 1) as b:
                body(b, True)
            body(B - 1, False)

        @block.tensor
        def _(pe):
            def turn_x(b):
                pe.wait_ge(xn_ready, b + 1)
                for k in range(KD):
                    mm = nc.tensor.transpose(ps[:, M_BANK, k * S:(k + 1) * S], xn[:, k * P:(k + 1) * P], g.ident)
                mm.then_inc(xT_mm, 1)

            def project(c, n, first=False):
                if first:
                    pe.wait_ge(wq_in[c], 16)
                if c == 0:
                    pe.wait_ge(xT_ready, n + 1)
                elif c >= 2:
                    prev = c - 1 if c > 2 else 0
                    pe.wait_ge(straight, (QCH + 1) * n + prev + 1)
                for k in range(KD):
                    mm = nc.tensor.matmul(ps[:, chunk_bank(c), :], xT[:, k, :], wqkv[:, k, c * CH:(c + 1) * CH],
                                          start=(k == 0), stop=(k == KD - 1))
                mm.then_inc(proj_mm, 1)

            def turn_qk(t, n):
                if t < QCH:
                    pe.wait_ge(rope_done, (QCH + 1) * n + t + 1)
                    pe.wait_ge(straight, (QCH + 1) * n + t + 1)
                else:
                    pe.wait_ge(rope_done, (QCH + 1) * (n + 1))
                    pe.wait_ge(straight, (QCH + 1) * (n + 1))
                    pe.wait_ge(qkT_ready, NT * n + t - 3)
                for i in range(4):
                    if t < QCH:
                        src = qk_tok[:, (4 * t + i) * P:(4 * t + i + 1) * P]
                    else:
                        kv = 4 * (t - QCH) + i
                        src = qk_tok[:, (PAIRS + kv) * P:(PAIRS + kv + 1) * P]
                    mm = nc.tensor.transpose(ps[:, S_BANK + t % 4, i * S:(i + 1) * S], src, g.ident)
                mm.then_inc(qkT_mm, 1)

            def score(u, b):
                if u == 0:
                    pe.wait_ge(qkT_ready, NT * (b + 1))
                elif u >= 2:
                    pe.wait_ge(shifted, UNITS * b + u - 1)
                for p in range(2):
                    nc.tensor.matmul(ps[:, S_BANK + 2 * (u % 2) + p, :], g.ident_bf,
                                     g.swa_bf.unsqueeze(1).to_broadcast([P, 4, S]), start=True, stop=False,
                                     skip_group_check=True)
                for i in range(4):
                    for p in range(2):
                        mm = nc.tensor.matmul(ps[:, S_BANK + 2 * (u % 2) + p, i * S:(i + 1) * S],
                                              qT[HD * p:HD * (p + 1), 4 * u + i, :],
                                              kT[HD * p:HD * (p + 1), 2 * u + i // 2, :],
                                              start=False, stop=True, skip_group_check=True)
                mm.then_inc(score_mm, 1)

            def turn_prob(u, n, first):
                pe.wait_ge(prob_ready, n + 1)
                if not first:
                    pe.wait_ge(probT_ready, 2 * n)
                for p in range(2):
                    for i in range(4):
                        mm = nc.tensor.transpose(ps[:, PT_BANK + p, i * S:(i + 1) * S], prob[:, u % 2, 4 * p + i, :], g.ident)
                    mm.then_inc(probT_mm, 1)

            def attend(u, n, b, first):
                pe.wait_ge(probT_ready, 2 * n + 2)
                if u == 0:
                    pe.wait_ge(v_ready, b + 1)
                if not first:
                    pe.wait_ge(oT_ready, n)
                for kv in range(2):
                    for p in range(2):
                        mm = nc.tensor.matmul(ps[HD * p:HD * (p + 1), O_BANK, kv * 2 * S:(kv + 1) * 2 * S],
                                              v_tok[:, (2 * u + kv) * HD:(2 * u + kv + 1) * HD],
                                              probT[:, u % 2, p, kv * 2 * S:(kv + 1) * 2 * S], start=True, stop=True,
                                              skip_group_check=True)
                mm.then_inc(av_mm, 1)

            def output(b):
                pe.wait_ge(oT_ready, UNITS * (b + 1))
                for t in range(PAIRS):
                    mm = nc.tensor.matmul(ps[:, M_BANK, 0:D], oT[:, t, :], wout[:, t, :],
                                          start=(t == 0), stop=(t == PAIRS - 1))
                mm.then_inc(y_mm, 1)

            def body(b, has_next, first):
                steps = "S0 S1 x c0 c1 P0 S2 A0 c2 P1 S3 A1 c3 P2 c4 A2 T0 T1 T2 P3 T3 A3 c5 Y T4 T5"
                for step in steps.split():
                    k = int(step[1]) if len(step) > 1 else 0
                    n = UNITS * b + k
                    if step[0] == "S":
                        score(k, b)
                    elif step[0] == "P":
                        turn_prob(k, n, first and k == 0)
                    elif step[0] == "A":
                        attend(k, n, b, first and k == 0)
                    elif step[0] == "Y":
                        if has_next:
                            pe.wait_ge(v_ready, b + 2)
                        output(b)
                    elif has_next:
                        if step[0] == "x":
                            if not first:
                                pe.wait_ge(x_added, b)
                            turn_x(b + 1)
                        elif step[0] == "c":
                            if k == 1 and not first:
                                pe.wait_ge(oT_ready, UNITS * b)
                            project(k, b + 1)
                        elif step[0] == "T":
                            if k == 0:
                                pe.wait_ge(shifted, UNITS * b + 3)
                            if k == 2:
                                pe.wait_ge(shifted, UNITS * b + 4)
                            turn_qk(k, b + 1)
                if not has_next:
                    return

            pe.wait_ge(const_in, 16)
            pe.wait_ge(ctx_in, 16)
            for h in range(4):
                for k in range(KD):
                    for j in range(2):
                        mm = nc.tensor.transpose(ps[:, h, (2 * k + j) * S:(2 * k + j + 1) * S],
                                                 ctx_tok[:, 2 * h + j, k * P:(k + 1) * P], g.ident)
                mm.then_inc(ctxT_mm, 1)
            turn_x(0)
            for c in range(NCH):
                project(c, 0, first=True)
            pe.wait_ge(ctxT_out, 4)
            for t in range(NT):
                turn_qk(t, 0)
            pe.wait_ge(masks_ready, 3)
            pe.wait_ge(wout_in, 16)
            body(0, True, True)
            with pe.Fori(1, B - 1) as b:
                body(b, True, False)
            body(B - 1, False, False)

        @block.vector
        def _(dve):
            def normalise(b):
                nc.vector.tensor_scalar(xn[:, :], g.x_sb[:, b, :], mv[:, b, 0:1], rstd[:, b, :],
                                        ALU.subtract, ALU.mult).then_inc(xn_ready, 1)

            cos = g.const[:, C_ROPE:C_ROPE + ROT]
            sin = g.const[:, C_ROPE + ROT:C_ROPE + 2 * ROT]

            def turn(c, n, first=False):
                dve.wait_ge(proj_mm, NCH * n + c + 1)
                if not (first and c < 2):
                    dve.wait_ge(rope_done, (QCH + 1) * n + c - 1)
                s = c % 2
                bank = ps[:, chunk_bank(c), :].rearrange("p (h a r) -> p h a r", h=8, a=2)[:, :, :, 0:ROT]
                nc.vector.tensor_tensor(rot_a[:, s], bank,
                                        cos.unsqueeze(1).unsqueeze(1).to_broadcast([P, 8, 2, ROT]), ALU.mult)
                wide = sin.unsqueeze(1).to_broadcast([P, 8, ROT])
                nc.vector.tensor_tensor(rot_b[:, s, :, 0, :], bank[:, :, 1, :], wide, ALU.mult)
                nc.vector.scalar_tensor_tensor(out=rot_b[:, s, :, 1, :], in0=bank[:, :, 0, :], scalar=-1.0, in1=wide,
                                               op0=ALU.mult, op1=ALU.mult).then_inc(turned, 1)

            def shift(u, n):
                s = u % 2
                dve.wait_ge(score_mm, n + 1)
                nc.vector.tensor_reduce(rmax[:, s, :], scores(s).rearrange("p c (i k) -> p (c i) k", i=4),
                                        AX.X, ALU.max).then_inc(rmax_done, 1)
                dve.wait_ge(rmax_done, n + 1)
                nc.vector.tensor_tensor(rowm[:, s, :], rmax[:, s, :], sink8[:, u, :], ALU.max).then_inc(rowm_done, 1)
                dve.wait_ge(rowm_done, n + 1)
                nc.vector.tensor_tensor(prob[:, s], scores(s).rearrange("p c (i k) -> p (c i) k", i=4),
                                        rowm[:, s, :].unsqueeze(2).to_broadcast([P, HU, S]), ALU.subtract).then_inc(shifted, 1)
                nc.vector.tensor_tensor(sinke[:, s, :], sink8[:, u, :], rowm[:, s, :], ALU.subtract).then_inc(sinkd, 1)

            def total(u, n):
                s = u % 2
                dve.wait_ge(exp_done, 2 * n + 2)
                nc.vector.tensor_reduce(psum_p[:, s, :], prob[:, s], AX.X, ALU.add).then_inc(sum_done, 1)
                dve.wait_ge(sum_done, n + 1)
                nc.vector.tensor_tensor(den[:, s, :], psum_p[:, s, :], sinke[:, s, :], ALU.add).then_inc(den_done, 1)
                dve.wait_ge(den_done, n + 1)
                nc.vector.reciprocal(rden[:, s, :], den[:, s, :]).then_inc(rden_done, 1)

            def body(b, has_next):
                steps = "x S0 S1 D0 R0 D1 R1 S2 R2 S3 D2 R3 D3 R4"
                for step in steps.split():
                    k = int(step[1]) if len(step) > 1 else 0
                    n = UNITS * b + k
                    if step[0] == "S":
                        shift(k, n)
                    elif step[0] == "D":
                        total(k, n)
                    elif has_next:
                        if step[0] == "x":
                            normalise(b + 1)
                        else:
                            turn(k, b + 1)
                dve.wait_ge(y_mm, b + 1)
                nc.vector.tensor_tensor(g.x_sb[:, b, :], g.x_sb[:, b, :], ps[:, M_BANK, 0:D], ALU.add).then_inc(x_added, 1)

            nc.vector.memset(g.neg_half[:, :], -0.5).then_inc(g.half_ready, 1)
            dve.wait_ge(x_in, 16)
            for b in range(B):
                nc.vector.bn_stats(stats[:, b, :], g.x_sb[:, b, :]).then_inc(stats_done, 1)
            for b in range(B):
                dve.wait_ge(stats_done, b + 1)
                nc.vector.bn_aggr(mv[:, b, :], stats[:, b, :]).then_inc(mv_done, 1)
            dve.wait_ge(const_in, 16)
            nc.vector.tensor_copy(g.ident_bf, g.const[:, C_ID:C_ID + P]).then_inc(masks_ready, 1)
            nc.vector.tensor_copy(g.swa_bf, g.const[:, C_SWA:C_SWA + P]).then_inc(masks_ready, 1)
            nc.vector.tensor_copy(g.causal_bf, g.const[:, C_CAUSAL:C_CAUSAL + P]).then_inc(masks_ready, 1)
            dve.wait_ge(sink_in, 16)
            nc.vector.tensor_scalar(sink8.rearrange("p u (a v j) -> p u a v j", a=2, v=2)[:, :, 0],
                                    sink_raw.rearrange("p (u v j a) -> p u v j a", u=UNITS, v=2, j=2)[:, :, :, :, 0],
                                    HD ** 0.5, None, ALU.mult)
            nc.vector.tensor_scalar(sink8.rearrange("p u (a v j) -> p u a v j", a=2, v=2)[:, :, 1],
                                    sink_raw.rearrange("p (u v j a) -> p u v j a", u=UNITS, v=2, j=2)[:, :, :, :, 1],
                                    HD ** 0.5, None, ALU.mult).then_inc(sink_ready, 1)
            dve.wait_ge(rstd_done, 1)
            normalise(0)
            for c in range(QCH + 1):
                turn(c, 0, first=True)
            dve.wait_ge(sink_ready, 1)
            with dve.Fori(0, B - 1) as b:
                body(b, True)
            body(B - 1, False)



class LayerNorm:

    def __init__(self, nc, g, ctx):
        self.nc, self.g = nc, g
        self.stats = ctx.enter_context(nc.sbuf_tensor("ln_stats", [P, B, 6], F32))
        self.mv = ctx.enter_context(nc.sbuf_tensor("ln_mv", [P, B, 2], F32))
        self.veps = ctx.enter_context(nc.sbuf_tensor("ln_veps", [P, B], F32))
        self.rstd = ctx.enter_context(nc.sbuf_tensor("ln_rstd", [P, B, 1], F32))
        self.stats_done = ctx.enter_context(nc.semaphore("ln_stats_done"))
        self.mv_done = ctx.enter_context(nc.semaphore("ln_mv_done"))
        self.veps_done = ctx.enter_context(nc.semaphore("ln_veps_done"))
        self.rstd_done = ctx.enter_context(nc.semaphore("ln_rstd_done"))
        self.xn_ready = ctx.enter_context(nc.semaphore("ln_xn_ready"))
        self.turned_mm = ctx.enter_context(nc.semaphore("ln_turned_mm"))
        self.turned_out = ctx.enter_context(nc.semaphore("ln_turned_out"))

    def vector(self, dve, r):
        nc, g = self.nc, self.g
        for b in range(B):
            nc.vector.bn_stats(self.stats[:, b, :], g.x_sb[:, b, :]).then_inc(self.stats_done, 1)
        for b in range(B):
            dve.wait_ge(self.stats_done, B * r + b + 1)
            nc.vector.bn_aggr(self.mv[:, b, :], self.stats[:, b, :]).then_inc(self.mv_done, 1)
        dve.wait_ge(self.rstd_done, r + 1)
        for b in range(B):
            nc.vector.tensor_scalar(g.xn[:, b, :], g.x_sb[:, b, :], self.mv[:, b, 0:1], self.rstd[:, b, :],
                                    ALU.subtract, ALU.mult).then_inc(self.xn_ready, 1)

    def gpsimd(self, pool, r):
        nc, g = self.nc, self.g
        pool.wait_ge(self.mv_done, B * (r + 1))
        nc.gpsimd.tensor_scalar_add(self.veps[:, :], self.mv[:, :, 1], LN_EPS).then_inc(self.veps_done, 1)
        pool.wait_ge(self.veps_done, r + 1)
        nc.gpsimd.tensor_tensor(self.rstd[:, :, 0], self.veps[:, :], g.neg_half[:, 0:B], ALU.pow).then_inc(self.rstd_done, 1)

    def tensor(self, pe, r):
        nc, g = self.nc, self.g
        for h in range(B // 2):
            pe.wait_ge(self.xn_ready, B * r + 2 * h + 2)
            for k in range(KD):
                for j in range(2):
                    mm = nc.tensor.transpose(g.ps[:, h, (2 * k + j) * S:(2 * k + j + 1) * S],
                                             g.xn[:, 2 * h + j, k * P:(k + 1) * P], g.ident)
            mm.then_inc(self.turned_mm, 1)

    def scalar(self, act, r, dst):
        nc, g = self.nc, self.g
        for h in range(B // 2):
            act.wait_ge(self.turned_mm, B // 2 * r + h + 1)
            nc.scalar.copy(dst(h), g.ps[:, h, :].rearrange("p (k j s) -> p k j s", k=KD, j=2)).then_inc(self.turned_out, 1)

    def out(self, r, h=B // 2):
        return B // 2 * r + h


def pair_of(t):
    return lambda h: t[:, :, 2 * h * S:2 * (h + 1) * S].rearrange("p k (j s) -> p k j s", j=2)


NH0 = 16
NI = 8


def layer0_convolution(nc, g):
    with ExitStack() as ctx:
        def sb(name, shape, dt=F32):
            return whole(ctx.enter_context(nc.sbuf_tensor(name, shape, dt)), shape)

        def sem(name):
            return ctx.enter_context(nc.semaphore(name))

        ln = g.ln
        N = B * NI * NI
        toep = sb("b_toep", [P, 2, 2 * P])
        kv = sb("b_kv", [P, 2, KD * N])
        z = sb("b_z", [P, 2, KD * N])
        oT = sb("b_oT", [P, KD * B, P])
        skip = sb("b_skip", [P, P])
        vx = sb("b_vx", [P, KD * B, P])
        skips = sb("b_skips", [P, KD * B, NH0])
        toep_in = [sem("toep_in0"), sem("toep_in1")]
        skip_in = sem("skip_in")
        kv_ready, conv_mm, z_ready, head_out = sem("kv_ready"), sem("conv_mm"), sem("z_ready"), sem("head_out")
        vx_done, skips_done, skip_term, oT_done = sem("vx_done"), sem("skips_done"), sem("skip_term"), sem("b_oT_done")
        back_mm, back_added = sem("back_mm"), sem("back_added")

        def channels(t, h):
            return t.rearrange("p c (h i) -> p c h i", h=NH0)[:, :, h, :]

        vT = g.xnT.rearrange("p k (b s) -> p (k b) s", b=B)
        xT = g.ctxT.rearrange("p k (b s) -> p (k b) s", b=B)
        wide = [P, KD * B, NI, NI]

        block = ctx.enter_context(nc.Block())

        @block.sync
        def _(sp):
            sp.dma_start(skip[:, :], g.skip.unsqueeze(0).to_broadcast([P, P])).then_inc(skip_in, 16)
            for s in range(2):
                sp.dma_start(toep[:, s, :], g.toeplitz[s]).then_inc(toep_in[s], 16)
            g.load_expert(sp, 0, 0)
            g.load_expert(sp, 1, 1)
            sp.dma_start(g.wqkv1_raw[:, :, :], g.w_qkv1.rearrange("(k p) n -> p k n", k=KD)).then_inc(g.wqkv1_in, 16)
            sp.dma_start(g.wproj1_raw[:, :, :], g.w_proj1.rearrange("(k p) n -> p k n", k=KD)).then_inc(g.wproj1_in, 16)
            sp.dma_start(g.ffn_gu[:, :, :], g.w_gu1.rearrange("(k p) n -> p k n", k=KD)).then_inc(g.ffn_gu_in, 16)
            sp.dma_start(g.ffn_dn[:, :, :], g.w_dn1.rearrange("(k p) n -> p k n", p=P)).then_inc(g.ffn_dn_in, 16)
            with sp.Fori(1, NH0 // 2) as i:
                for s in range(2):
                    sp.wait_ge(conv_mm, 2 * i + s - 1)
                    sp.dma_start(toep[:, s, :], g.toeplitz[2 * i + s]).then_inc(toep_in[s], 16)

        @block.gpsimd
        def _(pool):
            ln.gpsimd(pool, 0)
            pool.wait_ge(ln.turned_out, ln.out(0))

            def products(n, s, first):
                if not first:
                    pool.wait_ge(conv_mm, n - 1)
                nc.gpsimd.tensor_tensor(kv[:, s, :].rearrange("p (c i j) -> p c i j", i=NI, j=NI),
                                        channels(vT, n).unsqueeze(3).to_broadcast(wide),
                                        channels(xT, n).unsqueeze(2).to_broadcast(wide), ALU.mult).then_inc(kv_ready, 1)

            products(0, 0, True)
            products(1, 1, True)
            with pool.Fori(1, NH0 // 2) as i:
                for s in range(2):
                    products(2 * i + s, s, False)
            pool.wait_ge(skips_done, 1)
            nc.gpsimd.tensor_tensor(vx.rearrange("p c (h j) -> p c h j", h=NH0), xT.rearrange("p c (h j) -> p c h j", h=NH0),
                                    skips.unsqueeze(3).to_broadcast([P, KD * B, NH0, NI]), ALU.mult).then_inc(skip_term, 1)

        @block.tensor
        def _(pe):
            ln.tensor(pe, 0)
            pe.wait_ge(ln.turned_out, ln.out(0))

            def convolve(n, s, i, first):
                pe.wait_ge(toep_in[s], 16 * (i + 1))
                pe.wait_ge(kv_ready, n + 1)
                if not first:
                    pe.wait_ge(z_ready, n - 1)
                near, far = toep[:, s, 0:P], toep[:, s, P:2 * P]
                nc.tensor.matmul(g.ps[:, 2 * s, :], near, kv[:, s, 0:N], start=True, stop=True)
                nc.tensor.matmul(g.ps[:, 2 * s + 1, :], near, kv[:, s, N:2 * N], start=True, stop=False)
                nc.tensor.matmul(g.ps[:, 2 * s + 1, :], far, kv[:, s, 0:N], start=False, stop=True).then_inc(conv_mm, 1)

            convolve(0, 0, 0, True)
            convolve(1, 1, 0, True)
            with pe.Fori(1, NH0 // 2) as i:
                for s in range(2):
                    convolve(2 * i + s, s, i, False)
            pe.wait_ge(oT_done, 1)
            for h in range(B // 2):
                for j in range(2):
                    for k in range(KD):
                        mm = nc.tensor.transpose(g.ps[:, 4 + h, (2 * j + k) * P:(2 * j + k + 1) * P],
                                                 oT[:, k * B + 2 * h + j, :], g.ident)
                mm.then_inc(back_mm, 1)

        @block.scalar
        def _(act):
            ln.scalar(act, 0, pair_of(g.xnT))

        @block.vector
        def _(dve):
            ln.vector(dve, 0)
            dve.wait_ge(ln.turned_out, ln.out(0))
            dve.wait_ge(skip_in, 16)
            nc.vector.tensor_tensor(vx[:, :, :], vT, xT, ALU.mult).then_inc(vx_done, 1)
            dve.wait_ge(vx_done, 1)
            nc.vector.tensor_tensor(vx[:, :, :], vx[:, :, :], skip[:, :].unsqueeze(1).to_broadcast([P, KD * B, P]),
                                    ALU.mult).then_inc(vx_done, 1)
            dve.wait_ge(vx_done, 2)
            nc.vector.tensor_reduce(skips[:, :, :], vx.rearrange("p c (h i) -> p c h i", h=NH0), AX.X, ALU.add).then_inc(skips_done, 1)

            def gather(n, s):
                dve.wait_ge(conv_mm, n + 1)
                nc.vector.tensor_tensor(z[:, s, :].rearrange("p (c i j) -> p c i j", i=NI, j=NI),
                                        g.ps[:, 2 * s:2 * s + 2, :].rearrange("p k (b i j) -> p (k b) i j", i=NI, j=NI),
                                        channels(xT, n).unsqueeze(3).to_broadcast(wide), ALU.mult).then_inc(z_ready, 1)
                dve.wait_ge(z_ready, n + 1)
                nc.vector.tensor_reduce(channels(oT, n), z[:, s, :].rearrange("p (c i j) -> p c j i", i=NI, j=NI),
                                        AX.X, ALU.add).then_inc(head_out, 1)

            with dve.Fori(0, NH0 // 2) as i:
                for s in range(2):
                    gather(2 * i + s, s)
            dve.wait_ge(head_out, NH0)
            dve.wait_ge(skip_term, 1)
            nc.vector.tensor_tensor(oT[:, :, :], oT[:, :, :], vx[:, :, :], ALU.add).then_inc(oT_done, 1)
            for h in range(B // 2):
                dve.wait_ge(back_mm, h + 1)
                dst = g.x_sb[:, 2 * h:2 * h + 2, :]
                nc.vector.tensor_tensor(dst, dst, g.ps[:, 4 + h, :].rearrange("p (j l) -> p j l", j=2), ALU.add).then_inc(back_added, 1)
            dve.wait_ge(back_added, B // 2)


NE, TOP = 8, 2
ROUND = 1.5 * 2.0 ** 23


class GatedExpert:

    def __init__(self, nc, g, tag, ctx, nf):
        self.nc, self.g, self.nf = nc, g, nf
        self.sg = ctx.enter_context(nc.sbuf_tensor(tag + "_sg", [P, 2, 512], F32))
        self.h = ctx.enter_context(nc.sbuf_tensor(tag + "_h", [P, 2, nf, 512], F32))
        self.gu_mm = ctx.enter_context(nc.semaphore(tag + "_gu_mm"))
        self.silu_done = ctx.enter_context(nc.semaphore(tag + "_silu_done"))
        self.h_ready = ctx.enter_context(nc.semaphore(tag + "_h_ready"))
        self.y_mm = ctx.enter_context(nc.semaphore(tag + "_y_mm"))
        self.y_added = ctx.enter_context(nc.semaphore(tag + "_y_added"))

    def tensor(self, pe, e, gu, dn, first):
        nc, g, nf = self.nc, self.g, self.nf
        for half in range(2):
            for f in range(nf):
                n = 2 * nf * e + nf * half + f
                if not (first and half == 0 and f < 2):
                    pe.wait_ge(self.h_ready, n - 1)
                for a in range(2):
                    col = (a * nf + f) * P
                    for k in range(KD):
                        mm = nc.tensor.matmul(g.ps[:, 2 * (f % 2) + a, :], gu[:, k, col:col + P],
                                              g.xnT[:, k, half * 512:(half + 1) * 512], start=(k == 0), stop=(k == KD - 1))
                mm.then_inc(self.gu_mm, 1)
        for q in range(4):
            half = q // 2
            if q % 2 == 0:
                pe.wait_ge(self.h_ready, 2 * nf * e + nf * (half + 1))
            if not first:
                pe.wait_ge(self.y_added, 4 * e + q - 3)
            for j in range(2):
                t = 2 * (q % 2) + j
                for f in range(nf):
                    mm = nc.tensor.matmul(g.ps[:, 4 + q, j * D:(j + 1) * D], self.h[:, half, f, t * P:(t + 1) * P],
                                          dn[:, f, :], start=(f == 0), stop=(f == nf - 1))
            mm.then_inc(self.y_mm, 1)

    def scalar(self, act, e, first):
        nc, g, nf = self.nc, self.g, self.nf
        for n0 in range(2 * nf):
            n = 2 * nf * e + n0
            act.wait_ge(self.gu_mm, n + 1)
            if not (first and n0 < 2):
                act.wait_ge(self.h_ready, n - 1)
            nc.scalar.activation(self.sg[:, n0 % 2, :], g.ps[:, 2 * (n0 % 2), :], ACT.Silu).then_inc(self.silu_done, 1)

    def vector_h(self, dve, e):
        nc, g, nf = self.nc, self.g, self.nf
        for n0 in range(2 * nf):
            n = 2 * nf * e + n0
            dve.wait_ge(self.silu_done, n + 1)
            nc.vector.tensor_tensor(self.h[:, n0 // nf, n0 % nf, :], self.sg[:, n0 % 2, :], g.ps[:, 2 * (n0 % 2) + 1, :],
                                    ALU.mult).then_inc(self.h_ready, 1)


def layer0_experts(nc, g):
    with ExitStack() as ctx:
        def sb(name, shape, dt=F32):
            return whole(ctx.enter_context(nc.sbuf_tensor(name, shape, dt)), shape)

        def sem(name):
            return ctx.enter_context(nc.semaphore(name))

        ln = g.ln
        ex = GatedExpert(nc, g, "c", ctx, 4)
        gate_w = sb("c_gate_w", [P, KD, NE])
        lmax, lsum, lrec = sb("c_lmax", [P, B]), sb("c_lsum", [P, B]), sb("c_lrec", [P, B])
        prob = sb("c_prob", [P, B, NE])
        above = sb("c_above", [P, B, NE, NE])
        tied = sb("c_tied", [P, B, NE, NE])
        rank = sb("c_rank", [P, B, NE])
        comb = sb("c_comb", [P, B, NE + 1])
        now = sb("c_now", [P, 2, B])
        gate_in, logit_mm, expd, combined = sem("gate_in"), sem("logit_mm"), sem("c_expd"), sem("combined")
        step, now_ready = sem("router_step"), sem("now_ready")
        quant = Ternary(nc, g, ctx)

        block = ctx.enter_context(nc.Block())

        @block.sync
        def _(sp):
            sp.dma_start(gate_w[:, :, :], g.gate_w.rearrange("(k p) n -> p k n", k=KD)).then_inc(gate_in, 16)
            with sp.Fori(1, NE // 2) as i:
                for s in range(2):
                    sp.wait_ge(ex.y_mm, 4 * (2 * i + s) - 4)
                    g.load_expert(sp, 2 * i + s, s)
            sp.wait_ge(ex.y_mm, 4 * NE - 4)
            g.load_expert(sp, NE, 0)

        @block.gpsimd
        def _(pool):
            ln.gpsimd(pool, 1)
            quant.gpsimd(pool)

        @block.tensor
        def _(pe):
            ln.tensor(pe, 1)
            pe.wait_ge(gate_in, 16)
            for b in range(B):
                if b % 2 == 0:
                    pe.wait_ge(ln.turned_out, ln.out(1, b // 2 + 1))
                for k in range(KD):
                    mm = nc.tensor.matmul(g.ps[:, 7, b * NE:(b + 1) * NE], g.xnT[:, k, b * S:(b + 1) * S], gate_w[:, k, :],
                                          start=(k == 0), stop=(k == KD - 1))
            mm.then_inc(logit_mm, 1)

            def expert(e, s, i, first):
                pe.wait_ge(g.gu_in[s], 16 * (i + 1))
                pe.wait_ge(g.dn_in[s], 16 * (i + 1))
                ex.tensor(pe, e, g.ex_gu[s], g.ex_dn[s], first)

            expert(0, 0, 0, True)
            expert(1, 1, 0, False)
            with pe.Fori(1, NE // 2) as i:
                for s in range(2):
                    expert(2 * i + s, s, i, False)
            expert(NE, 0, NE // 2, False)

        @block.scalar
        def _(act):
            ln.scalar(act, 1, pair_of(g.xnT))
            act.wait_ge(step, 2)
            nc.scalar.activation(prob[:, :, :], prob[:, :, :], ACT.Exp).then_inc(expd, 1)
            ex.scalar(act, 0, True)
            ex.scalar(act, 1, False)
            with act.Fori(1, NE // 2) as i:
                for s in range(2):
                    ex.scalar(act, 2 * i + s, False)
            ex.scalar(act, NE, False)

        @block.vector
        def _(dve):
            ln.vector(dve, 1)
            wide = [P, B, NE, NE]
            mine, other = prob.unsqueeze(3).to_broadcast(wide), prob.unsqueeze(2).to_broadcast(wide)
            per_token = [P, B, NE]
            done = 0

            def stepped(ins):
                nonlocal done
                done += 1
                ins.then_inc(step, 1)
                dve.wait_ge(step, done)

            dve.wait_ge(logit_mm, 1)
            logits = g.ps[:, 7, 0:B * NE].rearrange("p (b e) -> p b e", b=B)
            stepped(nc.vector.tensor_reduce(lmax[:, :], logits, AX.X, ALU.max))
            stepped(nc.vector.tensor_tensor(prob[:, :, :], logits, lmax.unsqueeze(2).to_broadcast(per_token), ALU.subtract))
            dve.wait_ge(expd, 1)
            stepped(nc.vector.tensor_reduce(lsum[:, :], prob[:, :, :], AX.X, ALU.add))
            stepped(nc.vector.reciprocal(lrec[:, :], lsum[:, :]))
            stepped(nc.vector.tensor_tensor(prob[:, :, :], prob[:, :, :], lrec.unsqueeze(2).to_broadcast(per_token), ALU.mult))
            stepped(nc.vector.tensor_tensor(above[:, :, :, :], other, mine, ALU.is_gt))
            stepped(nc.vector.tensor_tensor(tied[:, :, :, :], other, mine, ALU.is_equal))
            lower = g.const[:, C_LOWER:C_LOWER + NE * NE].rearrange("p (e j) -> p e j", e=NE).unsqueeze(1).to_broadcast(wide)
            stepped(nc.vector.tensor_tensor(tied[:, :, :, :], tied[:, :, :, :], lower, ALU.mult))
            stepped(nc.vector.tensor_tensor(above[:, :, :, :], above[:, :, :, :], tied[:, :, :, :], ALU.add))
            stepped(nc.vector.tensor_reduce(rank[:, :, :], above[:, :, :, :], AX.X, ALU.add))
            stepped(nc.vector.scalar_tensor_tensor(out=prob[:, :, :], in0=rank[:, :, :], scalar=float(TOP), in1=prob[:, :, :],
                                                   op0=ALU.is_lt, op1=ALU.mult))
            stepped(nc.vector.tensor_reduce(lsum[:, :], prob[:, :, :], AX.X, ALU.add))
            stepped(nc.vector.reciprocal(lrec[:, :], lsum[:, :]))
            stepped(nc.vector.memset(comb[:, :, :], 1.0))
            stepped(nc.vector.tensor_tensor(comb[:, :, 0:NE], prob[:, :, :], lrec.unsqueeze(2).to_broadcast(per_token), ALU.mult))

            def expert(e, s):
                nc.vector.tensor_copy(now[:, s, :], comb[:, :, e]).then_inc(now_ready, 1)
                ex.vector_h(dve, e)
                dve.wait_ge(now_ready, e + 1)
                for q in range(4):
                    dve.wait_ge(ex.y_mm, 4 * e + q + 1)
                    for j in range(2):
                        b = 2 * q + j
                        add = nc.vector.scalar_tensor_tensor(out=g.x_sb[:, b, :], in0=g.ps[:, 4 + q, j * D:(j + 1) * D],
                                                             scalar=now[:, s, b:b + 1], in1=g.x_sb[:, b, :],
                                                             op0=ALU.mult, op1=ALU.add)
                    add.then_inc(ex.y_added, 1)

            expert(0, 0)
            quant.vector(dve)
            expert(1, 1)
            with dve.Fori(1, NE // 2) as i:
                for s in range(2):
                    expert(2 * i + s, s)
            expert(NE, 0)
            dve.wait_ge(ex.y_added, 4 * (NE + 1))


class Ternary:

    def __init__(self, nc, g, ctx):
        self.nc, self.g = nc, g
        self.asum = ctx.enter_context(nc.sbuf_tensor("t_asum", [P, 2], F32))
        self.total = ctx.enter_context(nc.sbuf_tensor("t_total", [P, 2], F32))
        self.inv = ctx.enter_context(nc.sbuf_tensor("t_inv", [P, 2], F32))
        self.asum_done = ctx.enter_context(nc.semaphore("ternary_asum_done"))
        self.total_done = ctx.enter_context(nc.semaphore("ternary_total_done"))
        self.step = ctx.enter_context(nc.semaphore("ternary_step"))

    def gpsimd(self, pool):
        pool.wait_ge(self.asum_done, 2)
        self.nc.gpsimd.partition_all_reduce(self.total[:, :], self.asum[:, :], P,
                                            bass.bass_isa.ReduceOp.add).then_inc(self.total_done, 1)

    def vector(self, dve):
        nc, g = self.nc, self.g
        raws, outs = (g.wqkv1_raw, g.wproj1_raw), (g.wqkv1, g.wproj1)
        dve.wait_ge(g.wqkv1_in, 16)
        dve.wait_ge(g.wproj1_in, 16)
        for i, raw in enumerate(raws):
            nc.vector.tensor_reduce(self.asum[:, i:i + 1], raw.rearrange("p k n -> p (k n)"), AX.X, ALU.add,
                                    apply_absolute_value=True).then_inc(self.asum_done, 1)
        dve.wait_ge(self.total_done, 1)
        done = 0
        for i, raw in enumerate(raws):
            n = P * raw.shape[1] * raw.shape[2]
            nc.vector.tensor_scalar(g.wmean[:, i:i + 1], self.total[:, i:i + 1], 1.0 / n, 1e-5, ALU.mult, ALU.max).then_inc(self.step, 1)
            done += 1
            dve.wait_ge(self.step, done)
            nc.vector.reciprocal(self.inv[:, i:i + 1], g.wmean[:, i:i + 1]).then_inc(self.step, 1)
            done += 1
            dve.wait_ge(self.step, done)
            nc.vector.tensor_scalar(raw[:, :, :], raw[:, :, :], self.inv[:, i:i + 1], ROUND, ALU.mult, ALU.add).then_inc(self.step, 1)
            done += 1
            dve.wait_ge(self.step, done)
            nc.vector.tensor_scalar(raw[:, :, :], raw[:, :, :], ROUND, 1.0, ALU.subtract, ALU.min).then_inc(self.step, 1)
            done += 1
            dve.wait_ge(self.step, done)
            nc.vector.tensor_scalar(outs[i][:, :, :], raw[:, :, :], -1.0, None, ALU.max).then_inc(self.step, 1)
            done += 1
        dve.wait_ge(self.step, done)


NH1, HD1 = 16, 16
SLOT = 64
DUOS = NH1 * SLOT // P


class QuantizedTokens:

    def __init__(self, nc, g, tag, ctx, which):
        self.nc, self.g, self.which = nc, g, which
        def sb(name, shape, dt=F32):
            return whole(ctx.enter_context(nc.sbuf_tensor(tag + name, shape, dt)), shape)
        self.amax = sb("_amax", [P, B])
        self.inv = sb("_inv", [P, B])
        self.scale = sb("_scale", [P, B, 1])
        self.ints = sb("_ints", [P, B, D], BF16)
        self.intsT = sb("_intsT", [P, KD, B * S], BF16)
        self.step = ctx.enter_context(nc.semaphore(tag + "_q_step"))
        self.ints_ready = ctx.enter_context(nc.semaphore(tag + "_q_ints_ready"))
        self.turned_mm = ctx.enter_context(nc.semaphore(tag + "_q_turned_mm"))
        self.turned_out = ctx.enter_context(nc.semaphore(tag + "_q_turned_out"))

    def vector(self, dve, src):
        nc, g = self.nc, self.g
        def step(ins, n):
            ins.then_inc(self.step, 1)
            dve.wait_ge(self.step, n)
        step(nc.vector.tensor_reduce(self.amax[:, :], src, AX.X, ALU.max, apply_absolute_value=True), 1)
        step(nc.vector.tensor_scalar(self.amax[:, :], self.amax[:, :], 1e-5, None, ALU.max), 2)
        step(nc.vector.reciprocal(self.inv[:, :], self.amax[:, :]), 3)
        step(nc.vector.tensor_scalar(self.inv[:, :], self.inv[:, :], 127.0, None, ALU.mult), 4)
        step(nc.vector.tensor_scalar(self.scale[:, :, 0], self.amax[:, :], 1.0 / 127.0, g.wmean[:, self.which:self.which + 1],
                                     ALU.mult, ALU.mult), 5)
        for h in range(B // 2):
            for b in (2 * h, 2 * h + 1):
                ins = nc.vector.tensor_scalar(src[:, b, :], src[:, b, :], self.inv[:, b:b + 1], ROUND, ALU.mult, ALU.add)
            step(ins, 6 + 2 * h)
            two = src[:, 2 * h:2 * h + 2, :]
            step(nc.vector.tensor_scalar(two, two, ROUND, 127.0, ALU.subtract, ALU.min), 7 + 2 * h)
            nc.vector.tensor_scalar(self.ints[:, 2 * h:2 * h + 2, :], two, -128.0, None, ALU.max).then_inc(self.ints_ready, 1)

    def tensor(self, pe):
        nc, g = self.nc, self.g
        for h in range(B // 2):
            pe.wait_ge(self.ints_ready, h + 1)
            for k in range(KD):
                for j in range(2):
                    mm = nc.tensor.matmul(g.ps[:, h, (2 * k + j) * S:(2 * k + j + 1) * S],
                                          self.ints[:, 2 * h + j, k * P:(k + 1) * P], g.ident_bf, start=True, stop=True)
            mm.then_inc(self.turned_mm, 1)

    def scalar(self, act):
        nc, g = self.nc, self.g
        for h in range(B // 2):
            act.wait_ge(self.turned_mm, h + 1)
            nc.scalar.copy(self.intsT[:, :, 2 * h * S:2 * (h + 1) * S],
                           g.ps[:, h, :].rearrange("p (k s) -> p k s", k=KD)).then_inc(self.turned_out, 1)


def layer1_attention(nc, g):
    with ExitStack() as ctx:
        def sb(name, shape, dt=F32):
            return whole(ctx.enter_context(nc.sbuf_tensor(name, shape, dt)), shape)

        def sem(name):
            return ctx.enter_context(nc.semaphore(name))

        ln = g.ln
        qin = QuantizedTokens(nc, g, "d_in", ctx, 0)
        qout = QuantizedTokens(nc, g, "d_out", ctx, 1)
        qk_pad = sb("d_qk_pad", [P, 2 * NH1, SLOT])
        qkT = sb("d_qkT", [P, 2 * DUOS, S])
        v1 = sb("d_v1", [P, NH1, HD1 + 1])
        prob = sb("d_prob", [P, 2, 8, S])
        probT = sb("d_probT", [P, 2, 2, 4 * S])
        rmax = sb("d_rmax", [P, 2, 8])
        rden = sb("d_rden", [P, NH1])
        att = sb("d_att", [P, B, D])
        cleared = sem("d_cleared")
        qk_mm, qk_out, v_mm, v_out = sem("d_qk_mm"), sem("d_qk_out"), sem("d_v_mm"), sem("d_v_out")
        qkT_mm, qkT_out = sem("d_qkT_mm"), sem("d_qkT_out")
        score_mm, rmax_done, shifted, expd = sem("d_score_mm"), sem("d_rmax_done"), sem("d_shifted"), sem("d_expd")
        probT_mm, probT_out, av_mm, rden_done, att_out = (
            sem("d_probT_mm"), sem("d_probT_out"), sem("d_av_mm"), sem("d_rden_done"), sem("d_att_out"))
        y_mm, y_added = sem("d_y_mm"), sem("d_y_added")
        ps = g.ps
        PT_BANK, QK_BANK, O_BANK = 4, 6, 7
        U = 2

        block = ctx.enter_context(nc.Block())

        @block.gpsimd
        def _(pool):
            nc.gpsimd.memset(qk_pad[:, :, :], 0.0).then_inc(cleared, 1)
            nc.gpsimd.memset(v1[:, :, :], 1.0).then_inc(cleared, 1)
            ln.gpsimd(pool, 2)

        @block.scalar
        def _(act):
            qin.scalar(act)

            def turned_out(b):
                for t in range(4):
                    act.wait_ge(qkT_mm, 4 * b + t + 1)
                    nc.scalar.copy(qkT[:, 4 * t:4 * t + 4, :], ps[:, t, :].rearrange("p (c s) -> p c s", c=4)).then_inc(qkT_out, 1)

            def unit(u, b):
                n = U * b + u
                act.wait_ge(shifted, n + 1)
                nc.scalar.activation(prob[:, u], prob[:, u], ACT.Exp, scale=HD1 ** -0.5).then_inc(expd, 1)

            def probs(u, b):
                n = U * b + u
                for p in range(2):
                    act.wait_ge(probT_mm, 2 * n + p + 1)
                    nc.scalar.copy(probT[:, u, p, :], ps[:, PT_BANK + p, :]).then_inc(probT_out, 1)

            turned_out(0)
            with act.Fori(0, B - 1) as b:
                unit(0, b)
                unit(1, b)
                probs(0, b)
                probs(1, b)
                turned_out(b + 1)
            unit(0, B - 1)
            unit(1, B - 1)
            probs(0, B - 1)
            probs(1, B - 1)
            qout.scalar(act)

        @block.tensor
        def _(pe):
            qin.tensor(pe)
            pe.wait_ge(qin.turned_out, B // 2)

            def project(b, which):
                cols = slice(0, 2 * D) if which == "qk" else slice(2 * D, 3 * D)
                for k in range(KD):
                    mm = nc.tensor.matmul(ps[:, QK_BANK, 0:cols.stop - cols.start], qin.intsT[:, k, bass.ds(b * S, S)],
                                          g.wqkv1[:, k, cols], start=(k == 0), stop=(k == KD - 1))
                mm.then_inc(qk_mm if which == "qk" else v_mm, 1)

            def turn_qk(b):
                pe.wait_ge(qk_out, b + 1)
                for t in range(4):
                    for c in range(4):
                        mm = nc.tensor.transpose(ps[:, t, c * S:(c + 1) * S],
                                                 qk_pad[:, 8 * t + 2 * c:8 * t + 2 * c + 2, :].rearrange("p h d -> p (h d)"), g.ident)
                    mm.then_inc(qkT_mm, 1)

            def score(u, b):
                for p in range(2):
                    nc.tensor.matmul(ps[:, 2 * u + p, :], g.ident_bf, g.causal_bf.unsqueeze(1).to_broadcast([P, 4, S]),
                                     start=True, stop=False, skip_group_check=True)
                for i in range(4):
                    for p in range(2):
                        rows = slice(SLOT * p, SLOT * p + HD1)
                        mm = nc.tensor.matmul(ps[:, 2 * u + p, i * S:(i + 1) * S], qkT[rows, 4 * u + i, :],
                                              qkT[rows, DUOS + 4 * u + i, :], start=False, stop=True, skip_group_check=True)
                mm.then_inc(score_mm, 1)

            def turn_prob(u, b, first):
                n = U * b + u
                pe.wait_ge(expd, n + 1)
                if not first:
                    pe.wait_ge(probT_out, 2 * n)
                for p in range(2):
                    for i in range(4):
                        mm = nc.tensor.transpose(ps[:, PT_BANK + p, i * S:(i + 1) * S], prob[:, u, 4 * p + i, :], g.ident)
                    mm.then_inc(probT_mm, 1)

            def attend(u, b):
                n = U * b + u
                pe.wait_ge(probT_out, 2 * n + 2)
                for i in range(4):
                    for p in range(2):
                        h = 8 * u + 2 * i + p
                        mm = nc.tensor.matmul(ps[:, O_BANK, h * (HD1 + 1):(h + 1) * (HD1 + 1)],
                                              probT[:, u, p, i * S:(i + 1) * S], v1[:, h, :], start=True, stop=True)
                if u == U - 1:
                    mm.then_inc(av_mm, 1)

            def body(b, has_next, first):
                pe.wait_ge(qkT_out, 4 * b + 4)
                score(0, b)
                score(1, b)
                if has_next:
                    pe.wait_ge(v_out, b + 1)
                    project(b + 1, "qk")
                turn_prob(0, b, first)
                if first:
                    pe.wait_ge(v_out, 1)
                else:
                    pe.wait_ge(att_out, b)
                    pe.wait_ge(v_out, b + 1)
                attend(0, b)
                turn_prob(1, b, False)
                attend(1, b)
                if has_next:
                    pe.wait_ge(qk_out, b + 2)
                    project(b + 1, "v")
                    pe.wait_ge(shifted, U * b + 2)
                    turn_qk(b + 1)

            project(0, "qk")
            pe.wait_ge(qk_out, 1)
            project(0, "v")
            turn_qk(0)
            body(0, True, True)
            with pe.Fori(1, B - 1) as b:
                body(b, True, False)
            body(B - 1, False, False)
            qout.tensor(pe)
            for h in range(B // 2):
                pe.wait_ge(qout.turned_out, h + 1)
                for j in range(2):
                    b = 2 * h + j
                    for k in range(KD):
                        mm = nc.tensor.matmul(ps[:, 4 + h, j * D:(j + 1) * D], qout.intsT[:, k, b * S:(b + 1) * S],
                                              g.wproj1[:, k, :], start=(k == 0), stop=(k == KD - 1))
                mm.then_inc(y_mm, 1)

        @block.vector
        def _(dve):
            ln.vector(dve, 2)
            dve.wait_ge(ln.xn_ready, B * 3)
            qin.vector(dve, g.xn)
            dve.wait_ge(cleared, 2)

            def out_qk(b):
                dve.wait_ge(qk_mm, b + 1)
                nc.vector.tensor_scalar(qk_pad[:, :, 0:HD1], ps[:, QK_BANK, :].rearrange("p (h d) -> p h d", d=HD1),
                                        qin.scale[:, b, :], None, ALU.mult).then_inc(qk_out, 1)

            def out_v(b):
                dve.wait_ge(v_mm, b + 1)
                nc.vector.tensor_scalar(v1[:, :, 0:HD1], ps[:, QK_BANK, 0:D].rearrange("p (h d) -> p h d", d=HD1),
                                        qin.scale[:, b, :], None, ALU.mult).then_inc(v_out, 1)

            def shift(u, b):
                n = U * b + u
                dve.wait_ge(score_mm, n + 1)
                s = ps[:, 2 * u:2 * u + 2, :].rearrange("p a (i k) -> p (a i) k", i=4)
                nc.vector.tensor_reduce(rmax[:, u, :], s, AX.X, ALU.max).then_inc(rmax_done, 1)
                dve.wait_ge(rmax_done, n + 1)
                nc.vector.tensor_tensor(prob[:, u], s, rmax[:, u, :].unsqueeze(2).to_broadcast([P, 8, S]),
                                        ALU.subtract).then_inc(shifted, 1)

            def body(b, has_next):
                shift(0, b)
                shift(1, b)
                if has_next:
                    out_qk(b + 1)
                dve.wait_ge(av_mm, b + 1)
                o = ps[:, O_BANK, 0:NH1 * (HD1 + 1)].rearrange("p (h d) -> p h d", h=NH1)
                nc.vector.reciprocal(rden[:, :], o[:, :, HD1]).then_inc(rden_done, 1)
                dve.wait_ge(rden_done, b + 1)
                nc.vector.tensor_tensor(att[:, b, :].rearrange("p (h d) -> p h d", h=NH1), o[:, :, 0:HD1],
                                        rden.unsqueeze(2).to_broadcast([P, NH1, HD1]), ALU.mult).then_inc(att_out, 1)
                if has_next:
                    out_v(b + 1)

            out_qk(0)
            out_v(0)
            with dve.Fori(0, B - 1) as b:
                body(b, True)
            body(B - 1, False)
            dve.wait_ge(att_out, B)
            qout.vector(dve, att)
            for h in range(B // 2):
                dve.wait_ge(y_mm, h + 1)
                for j in range(2):
                    b = 2 * h + j
                    nc.vector.scalar_tensor_tensor(out=g.x_sb[:, b, :], in0=ps[:, 4 + h, j * D:(j + 1) * D],
                                                   scalar=qout.scale[:, b, :], in1=g.x_sb[:, b, :],
                                                   op0=ALU.mult, op1=ALU.add).then_inc(y_added, 1)
            dve.wait_ge(y_added, B)


NEVER = -1e38


def layer1_wkv(nc, g):
    with ExitStack() as ctx:
        def sb(name, shape, dt=F32):
            return whole(ctx.enter_context(nc.sbuf_tensor(name, shape, dt)), shape)

        def sem(name):
            return ctx.enter_context(nc.semaphore(name))

        T = S + 1
        k_pad = sb("e_k", [P, KD, B, T])
        ln = g.ln
        decay, first = sb("e_decay", [P, KD]), sb("e_first", [P, KD])
        w = sb("e_w", [P, KD])
        steps = sb("e_steps", [P, KD, B, T])
        run = {n: sb("e_" + n, [P, KD, B, T]) for n in ("pp", "aa", "bb", "keep", "new", "new_v")}
        q, old, now, num = (sb("e_" + n, [P, KD, B, S]) for n in ("q", "old", "now", "num"))
        den = g.xnT.rearrange("p k (b s) -> p k b s", b=B)
        params_in, w_ready, padded, steps_ready = sem("e_params_in"), sem("e_w_ready"), sem("e_padded"), sem("e_steps_ready")
        pp_done, q_done, keep_arg, new_arg, old_arg, now_arg = (
            sem("e_pp_done"), sem("e_q_done"), sem("e_keep_arg"), sem("e_new_arg"), sem("e_old_arg"), sem("e_now_arg"))
        exp_done, new_v_done, aa_done, bb_done = sem("e_exp_done"), sem("e_new_v_done"), sem("e_aa_done"), sem("e_bb_done")
        num_step, den_step, num_done, y_done, back_mm, y_added = (
            sem("e_num_step"), sem("e_den_step"), sem("e_num_done"), sem("e_y_done"), sem("e_back_mm"), sem("e_y_added"))

        def flat(t, k):
            return t[:, k].rearrange("p b t -> p (b t)")

        def at(n, k):
            return run[n][:, k, :, 1:T]

        def before(n, k):
            return run[n][:, k, :, 0:S]

        v = g.ctxT.rearrange("p k (b s) -> p k b s", b=B)
        block = ctx.enter_context(nc.Block())

        @block.sync
        def _(sp):
            sp.dma_start(decay[:, :], g.decay.rearrange("(k p) -> p k", k=KD), allow_slow_non_contiguous=True).then_inc(params_in, 16)
            sp.dma_start(first[:, :], g.first.rearrange("(k p) -> p k", k=KD), allow_slow_non_contiguous=True).then_inc(params_in, 16)

        @block.gpsimd
        def _(pool):
            nc.gpsimd.memset(k_pad[:, :, :, 0:1], NEVER).then_inc(padded, 1)
            nc.gpsimd.memset(run["keep"][:, :, :, 0:1], 0.0).then_inc(padded, 1)
            nc.gpsimd.memset(run["new"][:, :, :, 0:1], 0.0).then_inc(padded, 1)
            nc.gpsimd.memset(run["new_v"][:, :, :, 0:1], 0.0).then_inc(padded, 1)
            ln.gpsimd(pool, 3)
            for k in range(KD):
                pool.wait_ge(pp_done, k + 1)
                nc.gpsimd.tensor_tensor(at("new", k), k_pad[:, k, :, 1:T], at("pp", k), ALU.subtract).then_inc(new_arg, 1)
                pool.wait_ge(q_done, k + 1)
                nc.gpsimd.tensor_tensor(old[:, k], before("pp", k), q[:, k], ALU.subtract).then_inc(old_arg, 1)
                pool.wait_ge(exp_done, 4 * k + 2)
                nc.gpsimd.tensor_tensor(at("new_v", k), at("new", k), v[:, k], ALU.mult).then_inc(new_v_done, 1)
            for k in range(KD):
                pool.wait_ge(exp_done, 4 * k + 4)
                pool.wait_ge(aa_done, k + 1)
                nc.gpsimd.tensor_tensor(num[:, k], old[:, k], before("aa", k), ALU.mult).then_inc(num_step, 1)
                nc.gpsimd.tensor_tensor(q[:, k], now[:, k], v[:, k], ALU.mult).then_inc(num_step, 1)
                pool.wait_ge(num_step, 2 * k + 2)
                nc.gpsimd.tensor_tensor(num[:, k], num[:, k], q[:, k], ALU.add).then_inc(num_done, 1)

        @block.scalar
        def _(act):
            ln.scalar(act, 2, lambda h: k_pad[:, :, 2 * h:2 * h + 2, 1:T])
            act.wait_ge(params_in, 32)
            nc.scalar.activation(w[:, :], decay[:, :], ACT.Exp).then_inc(w_ready, 1)
            for k in range(KD):
                for ready, t in ((keep_arg, at("keep", k)), (new_arg, at("new", k)), (now_arg, now[:, k]), (old_arg, old[:, k])):
                    act.wait_ge(ready, k + 1)
                    nc.scalar.activation(t, t, ACT.Exp).then_inc(exp_done, 1)

        @block.tensor
        def _(pe):
            ln.tensor(pe, 3)
            for k in range(KD):
                pe.wait_ge(y_done, k + 1)
                for h in range(2):
                    for j in range(4):
                        mm = nc.tensor.transpose(g.ps[:, 4 + 2 * k + h, j * P:(j + 1) * P], num[:, k, 4 * h + j, :], g.ident)
                    mm.then_inc(back_mm, 1)

        @block.vector
        def _(dve):
            ln.vector(dve, 3)
            dve.wait_ge(w_ready, 1)
            nc.vector.tensor_scalar(w[:, :], w[:, :], -1.0, None, ALU.mult).then_inc(w_ready, 1)
            nc.vector.memset(steps[:, :, :, :], 0.0).then_inc(steps_ready, 1)
            dve.wait_ge(w_ready, 2)
            dve.wait_ge(steps_ready, 1)
            for k in range(KD):
                nc.vector.tensor_scalar(steps[:, k], steps[:, k], w[:, k:k + 1], None, ALU.add).then_inc(steps_ready, 1)
            dve.wait_ge(steps_ready, 3)
            nc.vector.memset(steps[:, :, :, 0:1], NEVER).then_inc(steps_ready, 1)
            dve.wait_ge(steps_ready, 4)
            dve.wait_ge(padded, 4)
            dve.wait_ge(ln.turned_out, ln.out(2))
            for k in range(KD):
                nc.vector.tensor_tensor_scan(flat(run["pp"], k), flat(steps, k), flat(k_pad, k), NEVER, ALU.add, ALU.max).then_inc(pp_done, 1)
                dve.wait_ge(pp_done, k + 1)
                k_now = k_pad[:, k, :, 1:T]
                nc.vector.scalar_tensor_tensor(out=at("keep", k), in0=before("pp", k), scalar=w[:, k:k + 1], in1=at("pp", k),
                                               op0=ALU.add, op1=ALU.subtract).then_inc(keep_arg, 1)
                nc.vector.scalar_tensor_tensor(out=q[:, k], in0=k_now, scalar=first[:, k:k + 1], in1=before("pp", k),
                                               op0=ALU.add, op1=ALU.max).then_inc(q_done, 1)
                dve.wait_ge(q_done, k + 1)
                nc.vector.scalar_tensor_tensor(out=now[:, k], in0=k_now, scalar=first[:, k:k + 1], in1=q[:, k],
                                               op0=ALU.add, op1=ALU.subtract).then_inc(now_arg, 1)
            for k in range(KD):
                dve.wait_ge(exp_done, 4 * k + 2)
                nc.vector.tensor_tensor_scan(flat(run["bb"], k), flat(run["keep"], k), flat(run["new"], k), 0.0,
                                             ALU.mult, ALU.add).then_inc(bb_done, 1)
                dve.wait_ge(new_v_done, k + 1)
                nc.vector.tensor_tensor_scan(flat(run["aa"], k), flat(run["keep"], k), flat(run["new_v"], k), 0.0,
                                             ALU.mult, ALU.add).then_inc(aa_done, 1)
                dve.wait_ge(bb_done, k + 1)
                dve.wait_ge(exp_done, 4 * k + 4)
                nc.vector.tensor_tensor(den[:, k], old[:, k], before("bb", k), ALU.mult).then_inc(den_step, 1)
                dve.wait_ge(den_step, 3 * k + 1)
                nc.vector.tensor_tensor(den[:, k], den[:, k], now[:, k], ALU.add).then_inc(den_step, 1)
                dve.wait_ge(den_step, 3 * k + 2)
                nc.vector.reciprocal(den[:, k], den[:, k]).then_inc(den_step, 1)
                dve.wait_ge(den_step, 3 * k + 3)
                dve.wait_ge(num_done, k + 1)
                nc.vector.tensor_tensor(num[:, k], num[:, k], den[:, k], ALU.mult).then_inc(y_done, 1)
            for k in range(KD):
                for h in range(2):
                    dve.wait_ge(back_mm, 2 * k + h + 1)
                    dst = g.x_sb[:, 4 * h:4 * h + 4, k * P:(k + 1) * P]
                    nc.vector.tensor_tensor(dst, dst, g.ps[:, 4 + 2 * k + h, :].rearrange("p (j c) -> p j c", j=4),
                                            ALU.add).then_inc(y_added, 1)
            dve.wait_ge(y_added, 2 * KD)


def layer1_ffn(nc, g):
    with ExitStack() as ctx:
        ln = g.ln
        ex = GatedExpert(nc, g, "f", ctx, 8)
        stored = ctx.enter_context(nc.semaphore("stored"))
        block = ctx.enter_context(nc.Block())

        @block.gpsimd
        def _(pool):
            ln.gpsimd(pool, 4)

        @block.scalar
        def _(act):
            ln.scalar(act, 3, pair_of(g.xnT))
            ex.scalar(act, 0, True)

        @block.tensor
        def _(pe):
            ln.tensor(pe, 4)
            pe.wait_ge(g.ffn_gu_in, 16)
            pe.wait_ge(g.ffn_dn_in, 16)
            pe.wait_ge(ln.turned_out, ln.out(3))
            ex.tensor(pe, 0, g.ffn_gu, g.ffn_dn, True)

        @block.vector
        def _(dve):
            ln.vector(dve, 4)
            ex.vector_h(dve, 0)
            for q in range(4):
                dve.wait_ge(ex.y_mm, q + 1)
                dst = g.x_sb[:, 2 * q:2 * q + 2, :]
                nc.vector.tensor_tensor(dst, dst, g.ps[:, 4 + q, :].rearrange("p (j n) -> p j n", j=2), ALU.add).then_inc(ex.y_added, 1)

        @block.sync
        def _(sp):
            for q in range(4):
                sp.wait_ge(ex.y_added, q + 1)
                sp.dma_start(g.out.rearrange("b s d -> s b d")[:, 2 * q:2 * q + 2, :], g.x_sb[:, 2 * q:2 * q + 2, :]).then_inc(stored, 16)
            sp.wait_ge(stored, 4 * 16)


STAGES = (layer0_attention, layer0_convolution, layer0_experts, layer1_attention, layer1_wkv, layer1_ffn)


class Shared:
    pass


def build(nc, args, out):
    g = Shared()
    g.out = out
    (g.x, g.ctx, g.sink, g.w_qkv, g.w_out, g.table, g.skip, g.toeplitz, g.gate_w, g.w_gu, g.w_dn, g.w_qkv1, g.w_proj1,
     g.decay, g.first, g.w_gu1, g.w_dn1) = args
    with ExitStack() as ctx:
        def sb(name, shape, dt=F32):
            return whole(ctx.enter_context(nc.sbuf_tensor(name, shape, dt)), shape)

        def sem(name):
            return ctx.enter_context(nc.semaphore(name))

        g.ps = ctx.enter_context(nc.psum_tensor("ps", [P, 8, 512], F32))
        g.x_sb = sb("x_sb", [P, B, D])
        g.xn = sb("xn", [P, B, D])
        g.xnT = sb("xnT", [P, KD, B * S])
        g.ctxT = sb("ctxT", [P, KD, B * S])
        g.big_w = sb("big_w", [P, KD * QKV + PAIRS * D])
        g.const = sb("const", [P, C_END])
        g.ident = g.const[:, C_ID:C_ID + P]
        masks = sb("masks", [P, 3, P], BF16)
        g.ident_bf, g.swa_bf, g.causal_bf = (masks[:, i, :] for i in range(3))
        g.neg_half = sb("neg_half", [P, 8])
        g.half_ready = sem("half_ready")
        g.ln = LayerNorm(nc, g, ctx)

        GU, DN = KD * 1024, 4 * D
        g.ex_gu = [g.big_w[:, s * GU:(s + 1) * GU].rearrange("p (k n) -> p k n", k=KD) for s in range(2)]
        g.ex_dn = [g.big_w[:, 2 * GU + s * DN:2 * GU + (s + 1) * DN].rearrange("p (f n) -> p f n", f=4) for s in range(2)]
        g.gu_in, g.dn_in = [sem("gu_in0"), sem("gu_in1")], [sem("dn_in0"), sem("dn_in1")]

        def load_expert(sp, e, s):
            sp.dma_start(g.ex_gu[s], g.w_gu[e].rearrange("(k p) n -> p k n", k=KD)).then_inc(g.gu_in[s], 16)
            sp.dma_start(g.ex_dn[s], g.w_dn[e].rearrange("(f p) n -> p f n", f=4)).then_inc(g.dn_in[s], 16)

        g.load_expert = load_expert
        g.wqkv1_raw, g.wproj1_raw = sb("wqkv1_raw", [P, KD, 3 * D]), sb("wproj1_raw", [P, KD, D])
        g.wqkv1, g.wproj1 = sb("wqkv1", [P, KD, 3 * D], BF16), sb("wproj1", [P, KD, D], BF16)
        g.wmean = sb("wmean", [P, 2])
        g.wqkv1_in, g.wproj1_in = sem("wqkv1_in"), sem("wproj1_in")
        g.ffn_gu, g.ffn_dn = sb("ffn_gu", [P, KD, 2048]), sb("ffn_dn", [P, 8, D])
        g.ffn_gu_in, g.ffn_dn_in = sem("ffn_gu_in"), sem("ffn_dn_in")
        for stage in STAGES:
            stage(nc, g)


def kernel(**inputs):
    import concourse.bacc as _bacc
    from concourse import mybir as _mybir
    from concourse.bass_utils import run_bass_kernel_spmd as _run

    f = {k: np.ascontiguousarray(v) for k, v in inputs.items()}
    k = np.concatenate([np.zeros((16, P), np.float32), f["L0_xattn_k"]], axis=1)
    toeplitz = np.ascontiguousarray(k[:, P + np.arange(2 * P)[None, :] - np.arange(P)[:, None]])
    arrays = {
        "x": f["x"], "ctx": f["ctx_2048"], "sink": f["L0_attn_s"],
        "w_qkv": f["L0_attn_W_qkv"], "w_out": f["L0_attn_W_out"], "table": constants(),
        "skip": f["fside_S2_0"], "toeplitz": toeplitz, "gate_w": f["L0_ffn_gate_w"],
        "w_gu": np.concatenate([f["L0_ffn_expert_gate_up"], f["L0_ffn_base_gate_up"][None]]),
        "w_dn": np.concatenate([f["L0_ffn_expert_down"], f["L0_ffn_base_down"][None]]),
        "w_qkv1": np.ascontiguousarray(f["L1_attn_w_qkv"].T), "w_proj1": np.ascontiguousarray(f["L1_attn_w_proj"].T),
        "decay": f["L1_xattn_time_decay"], "first": f["L1_xattn_time_first"],
        "w_gu1": np.ascontiguousarray(f["L1_ffn_w_gate_up"].T), "w_dn1": np.ascontiguousarray(f["L1_ffn_w_down"].T),
    }
    nc = _bacc.Bacc("TRN2", target_bir_lowering=False, num_devices=1)
    args = [nc.dram_tensor(f"in_{n}_dram", a.shape, _mybir.dt.from_np(a.dtype), kind="ExternalInput").ap()
            for n, a in arrays.items()]
    out = nc.dram_tensor("out_0_dram", (B, S, D), F32, kind="ExternalOutput").ap()
    build(nc, args, out)
    r = _run(nc, [{f"in_{n}_dram": a for n, a in arrays.items()}], core_ids=[0])
    return r.results[0]["out_0_dram"]
```

```python
import numpy as np
from contextlib import ExitStack

import concourse.bass as bass
from concourse import mybir

F32 = mybir.dt.float32
BF16 = mybir.dt.bfloat16
ALU = mybir.AluOpType
ACT = mybir.ActivationFunctionType
AX = mybir.AxisListType

P = 128
B, S, D = 8, 128, 256
KD = D // P
LN_EPS = 1e-5
MASKED = -1e30

NE, TOP = 8, 2
TILES = B * S * TOP // P + NE - 1

NQ, NKV, HD, WINDOW = 32, 8, 64, 64
QM = NQ // NKV
ROT = HD // 4
QKV = (NQ + 2 * NKV) * HD
CH = 512
QCH = NQ * HD // CH
PAIRS = NQ // 2
UNITS = 4
HU = NQ // UNITS

C_ID, C_SWA, C_CAUSAL, C_ROPE, C_LOWER, C_EARLIER, C_ONES, C_COUNT, C_END = 0, 128, 256, 384, 416, 480, 608, 736, 768


def constants():
    t = np.zeros((P, C_END), np.float32)
    q, k = np.arange(S)[:, None], np.arange(S)[None, :]
    t[:, C_ID:C_ID + P] = np.eye(P)
    t[:, C_SWA:C_SWA + S] = np.where((q >= k) & (q < k + WINDOW), MASKED, 0.0)
    t[:, C_CAUSAL:C_CAUSAL + S] = np.where(q >= k, 0.0, MASKED)
    freq = np.float32(1 / 1024) ** np.linspace(0, 1, ROT, dtype=np.float32)
    theta = np.arange(S, dtype=np.float32)[:, None] * freq[None, :]
    t[:, C_ROPE:C_ROPE + ROT] = np.cos(theta)
    t[:, C_ROPE + ROT:C_ROPE + 2 * ROT] = np.sin(theta)
    e = np.arange(8)
    t[:, C_LOWER:C_LOWER + 64] = (e[None, :] < e[:, None]).astype(np.float32).reshape(1, 64)
    t[:, C_EARLIER:C_EARLIER + S] = q < k
    t[:, C_ONES:C_ONES + S] = 1.0
    t[:, C_COUNT:C_COUNT + 32] = np.arange(32)
    return t


def whole(tensor, shape):
    return tensor[tuple(slice(None) for _ in shape)]


def layer0_attention(nc, g):
    with ExitStack() as ctx:
        def sb(name, shape, dt=F32):
            return whole(ctx.enter_context(nc.sbuf_tensor(name, shape, dt)), shape)

        def sem(name):
            g.stage_sems.append(ctx.enter_context(nc.semaphore(name)))
            return g.stage_sems[-1]

        wqkv = g.big_w[:, 0:KD * QKV].rearrange("p (k n) -> p k n", k=KD)
        wout = g.big_w[:, KD * QKV:KD * QKV + PAIRS * D].rearrange("p (t n) -> p t n", t=PAIRS)
        xn = sb("a_xn", [P, D])
        xT = sb("a_xT", [P, KD, S])
        qk_tok = sb("a_qk_tok", [P, (NQ + 2 * NKV) * HD])
        v_tok = sb("a_v_tok", [P, NKV * HD])
        qT = g.xnT.rearrange("p k (t s) -> p (k t) s", t=PAIRS // KD)
        kT = g.ex_dn[:, NE - 1].rearrange("p f (t s) -> p (f t) s", s=S)
        prob = g.ex_gu[:, NE - 1].rearrange("p k (i s) -> p k i s", s=S)
        rot_a = sb("a_rot_a", [P, 2, 8, 2, ROT])
        rot_b = sb("a_rot_b", [P, 2, 8, 2, ROT])
        probT = sb("a_probT", [P, 2, 2, 4 * S])
        oT = g.xn.rearrange("p b (k s) -> p (b k) s", s=S)
        sink8 = sb("a_sink8", [P, UNITS, HU])
        rmax = sb("a_rmax", [P, 2, HU])
        rowm = sb("a_rowm", [P, 2, HU])
        sinke = sb("a_sinke", [P, 2, HU])
        psum_p = sb("a_psum_p", [P, 2, HU])
        den = sb("a_den", [P, 2, HU])
        rden = sb("a_rden", [P, 2, HU])
        stats = sb("a_stats", [P, B, 6])
        mv = sb("a_mv", [P, B, 2])
        veps = sb("a_veps", [P, B])
        rstd = sb("a_rstd", [P, B, 1])
        sink_raw = sb("a_sink_raw", [P, NQ])
        ctx_tok = g.xn

        const_in, x_in, ctx_in, sink_in = sem("const_in"), sem("x_in"), sem("ctx_in"), sem("sink_in")
        wq_in = [sem(f"wq_in{c}") for c in range(QCH + 2)]
        wout_in = sem("wout_in")
        masks_ready, sink_ready = sem("masks_ready"), sem("sink_ready")
        stats_done, mv_done, veps_done, rstd_done = sem("stats_done"), sem("mv_done"), sem("veps_done"), sem("rstd_done")
        ctxT_mm, ctxT_out = sem("ctxT_mm"), sem("ctxT_out")
        xn_ready, xT_mm, xT_ready = sem("a_xn_ready"), sem("a_xT_mm"), sem("a_xT_ready")
        proj_mm = sem("proj_mm")
        turned = sem("turned")
        straight = sem("straight")
        rope_done = sem("rope_done")
        v_ready = sem("v_ready")
        qkT_mm, qkT_ready = sem("qkT_mm"), sem("qkT_ready")
        score_mm, rmax_done, rowm_done, shifted, sinkd = (
            sem("score_mm"), sem("rmax_done"), sem("rowm_done"), sem("shifted"), sem("sinkd"))
        exp_done, sum_done, den_done, rden_done, prob_ready = (
            sem("exp_done"), sem("sum_done"), sem("den_done"), sem("rden_done"), sem("prob_ready"))
        probT_mm, probT_ready, av_mm, oT_ready, y_mm, x_added = (
            sem("probT_mm"), sem("probT_ready"), sem("av_mm"), sem("oT_ready"), sem("y_mm"), sem("x_added"))

        ps = g.ps
        S_BANK, PT_BANK, O_BANK, M_BANK = 0, 4, 6, 7
        NCH = QCH + 2
        TURNED = ("k0", "q0", "q1", "q2", "k1", "q3")
        NT = len(TURNED)

        def column(c):
            return QCH * CH if c == 0 else (c - 1) * CH if c <= QCH else c * CH

        def chunk_copies(c):
            if c > 0:
                return [qk_tok[:, (c - 1) * CH:c * CH].rearrange("p (h a r) -> p h a r", h=8, a=2)]
            k = qk_tok[:, QCH * CH:].rearrange("p (h d a r) -> p h d a r", h=NKV, d=2, a=2)
            return [k[:, :, 0], k[:, :, 1]]

        def chunk_bank(c):
            return PT_BANK + 1 if c in (0, 3) else M_BANK

        def turned_bank(t):
            return S_BANK + (t if t < 4 else t - 2)

        def scores(slot):
            return ps[:, S_BANK + 2 * slot:S_BANK + 2 * slot + 2, :]

        block = ctx.enter_context(nc.Block())

        @block.sync
        def _(sp):
            sp.dma_start(g.x_sb[:, :, :], g.x.rearrange("b s d -> s b d")).then_inc(x_in, 16)
            sp.dma_start(g.const[:, :], g.table[:, :]).then_inc(const_in, 16)
            src = g.w_qkv.rearrange("(k p) n -> p k n", k=KD)
            for c in range(NCH):
                at = column(c)
                sp.dma_start(wqkv[:, :, at:at + CH], src[:, :, at:at + CH]).then_inc(wq_in[c], 16)
            sp.dma_start(wout, g.w_out.rearrange("(t p) n -> p t n", t=PAIRS)).then_inc(wout_in, 16)
            for e in range(NE - 1):
                sp.dma_start(g.ex_gu[:, e], g.w_gu[e].rearrange("(k p) n -> p k n", k=KD)).then_inc(g.ex_in, 16)
                sp.dma_start(g.ex_dn[:, e], g.w_dn[e].rearrange("(f p) n -> p f n", f=4)).then_inc(g.ex_in, 16)

        @block.gpsimd
        def _(pool):
            def rope_add(c, n):
                pool.wait_ge(turned, n + 1)
                for dst in chunk_copies(c):
                    add = nc.gpsimd.tensor_tensor(dst[:, :, :, 0:ROT], rot_a[:, c % 2], rot_b[:, c % 2], ALU.add)
                add.then_inc(rope_done, 1)

            def normalise(u, n):
                pool.wait_ge(rden_done, n + 1)
                nc.gpsimd.tensor_tensor(prob[:, u % 2], prob[:, u % 2],
                                        rden[:, u % 2, :].unsqueeze(2).to_broadcast([P, HU, S]),
                                        ALU.mult).then_inc(prob_ready, 1)

            def body(b, has_next):
                for step in "R0 R1 D2 R2 R3 D3 R4 N0 N1".split():
                    k = int(step[1])
                    if step[0] == "D":
                        normalise(k, UNITS * b + k)
                    elif has_next and step[0] == "R":
                        rope_add(k, (QCH + 1) * (b + 1) + k)
                    elif has_next:
                        normalise(k, UNITS * (b + 1) + k)

            pool.wait_ge(mv_done, B)
            nc.gpsimd.tensor_scalar_add(veps[:, :], mv[:, :, 1], LN_EPS).then_inc(veps_done, 1)
            pool.wait_ge(veps_done, 1)
            pool.wait_ge(g.half_ready, 1)
            nc.gpsimd.tensor_tensor(rstd[:, :, 0], veps[:, :], g.neg_half[:, 0:B], ALU.pow).then_inc(rstd_done, 1)
            for c in range(QCH + 1):
                rope_add(c, c)
            for u in range(2):
                normalise(u, u)
            with pool.Fori(0, B - 1) as b:
                body(b, True)
            body(B - 1, False)

        @block.scalar
        def _(act):
            act.dma_start(ctx_tok[:, :, :], g.ctx.rearrange("b s d -> s b d")).then_inc(ctx_in, 16)
            act.dma_start(sink_raw[:, :], g.sink.rearrange("a g m -> a (g m)").to_broadcast([P, NQ])).then_inc(sink_in, 16)

            def xT_out(b):
                act.wait_ge(xT_mm, b + 1)
                nc.scalar.copy(xT[:, :, :], ps[:, O_BANK, 0:KD * S].rearrange("p (k s) -> p k s", k=KD)).then_inc(xT_ready, 1)

            def straight_out(c, n):
                act.wait_ge(turned, (QCH + 1) * n + c + 1)
                bank = ps[:, chunk_bank(c), :].rearrange("p (h a r) -> p h a r", h=8, a=2)
                for dst in chunk_copies(c):
                    copy = nc.scalar.copy(dst[:, :, :, ROT:2 * ROT], bank[:, :, :, ROT:2 * ROT])
                copy.then_inc(straight, 1)

            def v_out(n):
                act.wait_ge(proj_mm, NCH * n + NCH)
                nc.scalar.copy(v_tok[:, :], ps[:, M_BANK, :]).then_inc(v_ready, 1)

            def qkT_out(t, n):
                act.wait_ge(qkT_mm, NT * n + t + 1)
                at = 4 * int(TURNED[t][1])
                dst = (qT if TURNED[t][0] == "q" else kT)[:, at:at + 4, :]
                nc.scalar.copy(dst, ps[:, turned_bank(t), :].rearrange("p (t s) -> p t s", t=4)).then_inc(qkT_ready, 1)

            def exps(u, n):
                act.wait_ge(shifted, n + 1)
                nc.scalar.activation(prob[:, u % 2], prob[:, u % 2], ACT.Exp, scale=HD ** -0.5).then_inc(exp_done, 1)
                act.wait_ge(sinkd, n + 1)
                nc.scalar.activation(sinke[:, u % 2], sinke[:, u % 2], ACT.Exp, scale=HD ** -0.5).then_inc(exp_done, 1)

            def probT_out(u, n):
                for p in range(2):
                    act.wait_ge(probT_mm, 2 * n + p + 1)
                    nc.scalar.copy(probT[:, u % 2, p, :], ps[:, PT_BANK + p, :]).then_inc(probT_ready, 1)

            def oT_out(u, n):
                act.wait_ge(av_mm, n + 1)
                nc.scalar.copy(oT[:, 4 * u:4 * u + 4, :], ps[:, O_BANK, :].rearrange("p (t s) -> p t s", t=4)).then_inc(oT_ready, 1)

            def body(b, has_next):
                steps = "x P0 e2 n0 n1 o0 P1 e3 n2 n3 o1 P2 n4 T0 T1 T2 T3 o2 T4 T5 P3 o3 v E0 E1"
                for step in steps.split():
                    k = int(step[1]) if len(step) > 1 else 0
                    if step[0] == "e":
                        exps(k, UNITS * b + k)
                    elif step[0] == "P":
                        probT_out(k, UNITS * b + k)
                    elif step[0] == "o":
                        oT_out(k, UNITS * b + k)
                    elif has_next:
                        if step[0] == "x":
                            xT_out(b + 1)
                        elif step[0] == "n":
                            straight_out(k, b + 1)
                        elif step[0] == "T":
                            qkT_out(k, b + 1)
                        elif step[0] == "E":
                            exps(k, UNITS * (b + 1) + k)
                        else:
                            v_out(b + 1)

            for h in range(4):
                act.wait_ge(ctxT_mm, h + 1)
                nc.scalar.copy(g.ctxT[:, :, 2 * h * S:2 * (h + 1) * S],
                               ps[:, h, :].rearrange("p (k s) -> p k s", k=KD)).then_inc(ctxT_out, 1)
            xT_out(0)
            for c in range(QCH + 1):
                straight_out(c, 0)
            v_out(0)
            for t in range(NT):
                qkT_out(t, 0)
            for u in range(2):
                exps(u, u)
            with act.Fori(0, B - 1) as b:
                body(b, True)
            body(B - 1, False)

        @block.tensor
        def _(pe):
            def turn_x(b):
                pe.wait_ge(xn_ready, b + 1)
                for k in range(KD):
                    mm = nc.tensor.transpose(ps[:, O_BANK, k * S:(k + 1) * S], xn[:, k * P:(k + 1) * P], g.ident)
                mm.then_inc(xT_mm, 1)

            def project(c, n, first=False):
                if first:
                    pe.wait_ge(wq_in[c], 16)
                if c == 0:
                    pe.wait_ge(xT_ready, n + 1)
                elif c == 1 and not first:
                    pe.wait_ge(x_added, n - 1)
                elif c in (2, 4):
                    pe.wait_ge(straight, (QCH + 1) * n + c)
                elif c == 5:
                    pe.wait_ge(straight, (QCH + 1) * n + c)
                if not first and c in (0, 3):
                    pe.wait_ge(probT_ready, 2 * (UNITS * (n - 1) + c // 3) + 2)
                at = column(c)
                for k in range(KD):
                    mm = nc.tensor.matmul(ps[:, chunk_bank(c), :], xT[:, k, :], wqkv[:, k, at:at + CH],
                                          start=(k == 0), stop=(k == KD - 1))
                mm.then_inc(proj_mm, 1)

            def turn_qk(t, n):
                kind, i0 = TURNED[t][0], int(TURNED[t][1])
                chunk = i0 + 1 if kind == "q" else 0
                pe.wait_ge(rope_done, (QCH + 1) * n + chunk + 1)
                pe.wait_ge(straight, (QCH + 1) * n + chunk + 1)
                if t >= 4:
                    pe.wait_ge(qkT_ready, NT * n + t - 1)
                for i in range(4):
                    tile = 4 * i0 + i if kind == "q" else PAIRS + 4 * i0 + i
                    mm = nc.tensor.transpose(ps[:, turned_bank(t), i * S:(i + 1) * S],
                                             qk_tok[:, tile * P:(tile + 1) * P], g.ident)
                mm.then_inc(qkT_mm, 1)

            def score(u, b):
                if u < 2:
                    pe.wait_ge(qkT_ready, NT * b + (2 if u == 0 else NT))
                else:
                    pe.wait_ge(shifted, UNITS * b + u - 1)
                for p in range(2):
                    nc.tensor.matmul(ps[:, S_BANK + 2 * (u % 2) + p, :], g.ident_bf,
                                     g.swa_bf.unsqueeze(1).to_broadcast([P, 4, S]), start=True, stop=False,
                                     skip_group_check=True)
                for i in range(4):
                    for p in range(2):
                        mm = nc.tensor.matmul(ps[:, S_BANK + 2 * (u % 2) + p, i * S:(i + 1) * S],
                                              qT[HD * p:HD * (p + 1), 4 * u + i, :],
                                              kT[HD * p:HD * (p + 1), 2 * u + i // 2, :],
                                              start=False, stop=True, skip_group_check=True)
                mm.then_inc(score_mm, 1)

            def turn_prob(u, n, first, b, has_next):
                pe.wait_ge(prob_ready, n + 1)
                if not first:
                    pe.wait_ge(probT_ready, 2 * n)
                for p in range(2):
                    if p == 1 and has_next and u in (1, 2):
                        pe.wait_ge(straight, (QCH + 1) * (b + 1) + (1 if u == 1 else 4))
                    for i in range(4):
                        mm = nc.tensor.transpose(ps[:, PT_BANK + p, i * S:(i + 1) * S], prob[:, u % 2, 4 * p + i, :], g.ident)
                    mm.then_inc(probT_mm, 1)

            def attend(u, n, b, first):
                pe.wait_ge(probT_ready, 2 * n + 2)
                if u == 0:
                    pe.wait_ge(v_ready, b + 1)
                if not first:
                    pe.wait_ge(oT_ready, n)
                for kv in range(2):
                    for p in range(2):
                        mm = nc.tensor.matmul(ps[HD * p:HD * (p + 1), O_BANK, kv * 2 * S:(kv + 1) * 2 * S],
                                              v_tok[:, (2 * u + kv) * HD:(2 * u + kv + 1) * HD],
                                              probT[:, u % 2, p, kv * 2 * S:(kv + 1) * 2 * S], start=True, stop=True,
                                              skip_group_check=True)
                mm.then_inc(av_mm, 1)

            def output(b):
                pe.wait_ge(oT_ready, UNITS * (b + 1))
                for t in range(PAIRS):
                    mm = nc.tensor.matmul(ps[:, M_BANK, 0:D], oT[:, t, :], wout[:, t, :],
                                          start=(t == 0), stop=(t == PAIRS - 1))
                mm.then_inc(y_mm, 1)

            def body(b, has_next, first):
                steps = "x P0 S2 c0 c1 A0 P1 S3 c2 c3 A1 c4 P2 T0 T1 T2 T3 A2 T4 T5 P3 N0 A3 c5 N1 Y"
                for step in steps.split():
                    k = int(step[1]) if len(step) > 1 else 0
                    n = UNITS * b + k
                    if step[0] == "S":
                        score(k, b)
                    elif step[0] == "P":
                        turn_prob(k, n, first and k == 0, b, has_next)
                    elif step[0] == "A":
                        attend(k, n, b, first and k == 0)
                    elif step[0] == "Y":
                        if has_next:
                            pe.wait_ge(v_ready, b + 2)
                        else:
                            pe.wait_ge(x_added, b)
                        output(b)
                    elif has_next:
                        if step[0] == "x":
                            turn_x(b + 1)
                        elif step[0] == "c":
                            project(k, b + 1)
                        elif step[0] == "N":
                            score(k, b + 1)
                        elif step[0] == "T":
                            if k == 0:
                                pe.wait_ge(shifted, UNITS * b + 3)
                            if k == 2:
                                pe.wait_ge(shifted, UNITS * b + 4)
                            turn_qk(k, b + 1)

            pe.wait_ge(const_in, 16)
            pe.wait_ge(ctx_in, 16)
            for h in range(4):
                for k in range(KD):
                    for j in range(2):
                        mm = nc.tensor.transpose(ps[:, h, (2 * k + j) * S:(2 * k + j + 1) * S],
                                                 ctx_tok[:, 2 * h + j, k * P:(k + 1) * P], g.ident)
                mm.then_inc(ctxT_mm, 1)
            turn_x(0)
            for c in range(NCH):
                project(c, 0, first=True)
            pe.wait_ge(ctxT_out, 4)
            for t in range(NT):
                turn_qk(t, 0)
            pe.wait_ge(masks_ready, 3)
            for u in range(2):
                score(u, 0)
            pe.wait_ge(wout_in, 16)
            body(0, True, True)
            with pe.Fori(1, B - 1) as b:
                body(b, True, False)
            body(B - 1, False, False)

        @block.vector
        def _(dve):
            def normalise(b):
                nc.vector.tensor_scalar(xn[:, :], g.x_sb[:, b, :], mv[:, b, 0:1], rstd[:, b, :],
                                        ALU.subtract, ALU.mult).then_inc(xn_ready, 1)

            cos = g.const[:, C_ROPE:C_ROPE + ROT]
            sin = g.const[:, C_ROPE + ROT:C_ROPE + 2 * ROT]

            def turn(c, n, first=False):
                dve.wait_ge(proj_mm, NCH * n + c + 1)
                if not (first and c < 2):
                    dve.wait_ge(rope_done, (QCH + 1) * n + c - 1)
                s = c % 2
                bank = ps[:, chunk_bank(c), :].rearrange("p (h a r) -> p h a r", h=8, a=2)[:, :, :, 0:ROT]
                nc.vector.tensor_tensor(rot_a[:, s], bank,
                                        cos.unsqueeze(1).unsqueeze(1).to_broadcast([P, 8, 2, ROT]), ALU.mult)
                wide = sin.unsqueeze(1).to_broadcast([P, 8, ROT])
                nc.vector.tensor_tensor(rot_b[:, s, :, 0, :], bank[:, :, 1, :], wide, ALU.mult)
                nc.vector.scalar_tensor_tensor(out=rot_b[:, s, :, 1, :], in0=bank[:, :, 0, :], scalar=-1.0, in1=wide,
                                               op0=ALU.mult, op1=ALU.mult).then_inc(turned, 1)

            def shift(u, n):
                s = u % 2
                dve.wait_ge(score_mm, n + 1)
                nc.vector.tensor_reduce(rmax[:, s, :], scores(s).rearrange("p c (i k) -> p (c i) k", i=4),
                                        AX.X, ALU.max).then_inc(rmax_done, 1)
                dve.wait_ge(rmax_done, n + 1)
                nc.vector.tensor_tensor(rowm[:, s, :], rmax[:, s, :], sink8[:, u, :], ALU.max).then_inc(rowm_done, 1)
                dve.wait_ge(rowm_done, n + 1)
                nc.vector.tensor_tensor(prob[:, s], scores(s).rearrange("p c (i k) -> p (c i) k", i=4),
                                        rowm[:, s, :].unsqueeze(2).to_broadcast([P, HU, S]), ALU.subtract).then_inc(shifted, 1)
                nc.vector.tensor_tensor(sinke[:, s, :], sink8[:, u, :], rowm[:, s, :], ALU.subtract).then_inc(sinkd, 1)

            def total(u, n):
                s = u % 2
                dve.wait_ge(exp_done, 2 * n + 2)
                nc.vector.tensor_reduce(psum_p[:, s, :], prob[:, s], AX.X, ALU.add).then_inc(sum_done, 1)
                dve.wait_ge(sum_done, n + 1)
                nc.vector.tensor_tensor(den[:, s, :], psum_p[:, s, :], sinke[:, s, :], ALU.add).then_inc(den_done, 1)
                dve.wait_ge(den_done, n + 1)
                nc.vector.reciprocal(rden[:, s, :], den[:, s, :]).then_inc(rden_done, 1)

            def add(b):
                dve.wait_ge(y_mm, b + 1)
                nc.vector.tensor_tensor(g.x_sb[:, b, :], g.x_sb[:, b, :], ps[:, M_BANK, 0:D], ALU.add).then_inc(x_added, 1)

            def body(b, has_next, first):
                steps = "x Y S2 R0 R1 D2 S3 R2 R3 D3 R4 N0 M0 N1 M1"
                for step in steps.split():
                    k = int(step[1]) if len(step) > 1 else 0
                    n = UNITS * b + k
                    if step[0] == "S":
                        shift(k, n)
                    elif step[0] == "D":
                        total(k, n)
                    elif step[0] == "Y":
                        if not first:
                            add(b - 1)
                    elif has_next:
                        if step[0] == "x":
                            normalise(b + 1)
                        elif step[0] == "N":
                            shift(k, UNITS * (b + 1) + k)
                        elif step[0] == "M":
                            total(k, UNITS * (b + 1) + k)
                        else:
                            turn(k, b + 1)

            nc.vector.memset(g.neg_half[:, :], -0.5).then_inc(g.half_ready, 1)
            dve.wait_ge(x_in, 16)
            for b in range(B):
                nc.vector.bn_stats(stats[:, b, :], g.x_sb[:, b, :]).then_inc(stats_done, 1)
            for b in range(B):
                dve.wait_ge(stats_done, b + 1)
                nc.vector.bn_aggr(mv[:, b, :], stats[:, b, :]).then_inc(mv_done, 1)
            dve.wait_ge(const_in, 16)
            nc.vector.tensor_copy(g.ident_bf, g.const[:, C_ID:C_ID + P]).then_inc(masks_ready, 1)
            nc.vector.tensor_copy(g.swa_bf, g.const[:, C_SWA:C_SWA + P]).then_inc(masks_ready, 1)
            nc.vector.tensor_copy(g.causal_bf, g.const[:, C_CAUSAL:C_CAUSAL + P]).then_inc(masks_ready, 1)
            dve.wait_ge(sink_in, 16)
            nc.vector.tensor_scalar(sink8.rearrange("p u (a v j) -> p u a v j", a=2, v=2)[:, :, 0],
                                    sink_raw.rearrange("p (u v j a) -> p u v j a", u=UNITS, v=2, j=2)[:, :, :, :, 0],
                                    HD ** 0.5, None, ALU.mult)
            nc.vector.tensor_scalar(sink8.rearrange("p u (a v j) -> p u a v j", a=2, v=2)[:, :, 1],
                                    sink_raw.rearrange("p (u v j a) -> p u v j a", u=UNITS, v=2, j=2)[:, :, :, :, 1],
                                    HD ** 0.5, None, ALU.mult).then_inc(sink_ready, 1)
            dve.wait_ge(rstd_done, 1)
            normalise(0)
            for c in range(QCH + 1):
                turn(c, 0, first=True)
            dve.wait_ge(sink_ready, 1)
            for u in range(2):
                shift(u, u)
                total(u, u)
            body(0, True, True)
            with dve.Fori(1, B - 1) as b:
                body(b, True, False)
            body(B - 1, False, False)
            add(B - 1)



class LayerNorm:

    def __init__(self, nc, g, ctx):
        self.nc, self.g = nc, g
        self.stats = ctx.enter_context(nc.sbuf_tensor("ln_stats", [P, B, 6], F32))
        self.mv = ctx.enter_context(nc.sbuf_tensor("ln_mv", [P, B, 2], F32))
        self.veps = ctx.enter_context(nc.sbuf_tensor("ln_veps", [P, B], F32))
        self.rstd = ctx.enter_context(nc.sbuf_tensor("ln_rstd", [P, B, 1], F32))
        self.stats_done = ctx.enter_context(nc.semaphore("ln_stats_done"))
        self.mv_done = ctx.enter_context(nc.semaphore("ln_mv_done"))
        self.veps_done = ctx.enter_context(nc.semaphore("ln_veps_done"))
        self.rstd_done = ctx.enter_context(nc.semaphore("ln_rstd_done"))
        self.xn_ready = ctx.enter_context(nc.semaphore("ln_xn_ready"))
        self.turned_mm = ctx.enter_context(nc.semaphore("ln_turned_mm"))
        self.turned_out = ctx.enter_context(nc.semaphore("ln_turned_out"))

    def vector(self, dve, r):
        nc, g = self.nc, self.g
        for b in range(B):
            nc.vector.bn_stats(self.stats[:, b, :], g.x_sb[:, b, :]).then_inc(self.stats_done, 1)
        for b in range(B):
            dve.wait_ge(self.stats_done, B * r + b + 1)
            nc.vector.bn_aggr(self.mv[:, b, :], self.stats[:, b, :]).then_inc(self.mv_done, 1)
        dve.wait_ge(self.rstd_done, r + 1)
        for b in range(B):
            nc.vector.tensor_scalar(g.xn[:, b, :], g.x_sb[:, b, :], self.mv[:, b, 0:1], self.rstd[:, b, :],
                                    ALU.subtract, ALU.mult).then_inc(self.xn_ready, 1)

    def gpsimd(self, pool, r):
        nc, g = self.nc, self.g
        pool.wait_ge(self.mv_done, B * (r + 1))
        nc.gpsimd.tensor_scalar_add(self.veps[:, :], self.mv[:, :, 1], LN_EPS).then_inc(self.veps_done, 1)
        pool.wait_ge(self.veps_done, r + 1)
        nc.gpsimd.tensor_tensor(self.rstd[:, :, 0], self.veps[:, :], g.neg_half[:, 0:B], ALU.pow).then_inc(self.rstd_done, 1)

    def tensor(self, pe, r):
        nc, g = self.nc, self.g
        for h in range(B // 2):
            pe.wait_ge(self.xn_ready, B * r + 2 * h + 2)
            for k in range(KD):
                for j in range(2):
                    mm = nc.tensor.transpose(g.ps[:, h, (2 * k + j) * S:(2 * k + j + 1) * S],
                                             g.xn[:, 2 * h + j, k * P:(k + 1) * P], g.ident)
            mm.then_inc(self.turned_mm, 1)

    def scalar(self, act, r, dst):
        nc, g = self.nc, self.g
        for h in range(B // 2):
            act.wait_ge(self.turned_mm, B // 2 * r + h + 1)
            nc.scalar.copy(dst(h), g.ps[:, h, :].rearrange("p (k j s) -> p k j s", k=KD, j=2)).then_inc(self.turned_out, 1)

    def out(self, r, h=B // 2):
        return B // 2 * r + h


def pair_of(t):
    return lambda h: t[:, :, 2 * h * S:2 * (h + 1) * S].rearrange("p k (j s) -> p k j s", j=2)


NH0 = 16
NI = 8


def layer0_convolution(nc, g):
    with ExitStack() as ctx:
        def sb(name, shape, dt=F32):
            return whole(ctx.enter_context(nc.sbuf_tensor(name, shape, dt)), shape)

        def sem(name):
            return ctx.enter_context(nc.semaphore(name))

        ln = g.ln
        N = B * NI * NI
        toep = sb("b_toep", [P, 2, 2 * P])
        kv = sb("b_kv", [P, 2, KD * N])
        z = sb("b_z", [P, 2, KD * N])
        oT = sb("b_oT", [P, KD * B, P])
        skip = sb("b_skip", [P, P])
        vx = g.xn.rearrange("p b (k s) -> p (b k) s", k=KD)
        skips = sb("b_skips", [P, KD * B, NH0])
        zero = sb("b_zero", [P, D])
        zero_ready = sem("zero_ready")
        toep_in = [sem("toep_in0"), sem("toep_in1")]
        skip_in = sem("skip_in")
        kv_ready, conv_mm, z_ready, head_out = sem("kv_ready"), sem("conv_mm"), sem("z_ready"), sem("head_out")
        vx_done, skips_done, skip_term, oT_done = sem("vx_done"), sem("skips_done"), sem("skip_term"), sem("b_oT_done")
        back_mm, back_added = sem("back_mm"), sem("back_added")

        def channels(t, h):
            return t.rearrange("p c (h i) -> p c h i", h=NH0)[:, :, h, :]

        vT = g.xnT.rearrange("p k (b s) -> p (k b) s", b=B)
        xT = g.ctxT.rearrange("p k (b s) -> p (k b) s", b=B)
        wide = [P, KD * B, NI, NI]

        block = ctx.enter_context(nc.Block())

        @block.sync
        def _(sp):
            sp.dma_start(skip[:, :], g.skip.unsqueeze(0).to_broadcast([P, P])).then_inc(skip_in, 16)
            for s in range(2):
                sp.dma_start(toep[:, s, :], g.toeplitz[s]).then_inc(toep_in[s], 16)
            e = NE - 1
            sp.dma_start(g.ex_gu[:, e], g.w_gu[e].rearrange("(k p) n -> p k n", k=KD)).then_inc(g.ex_in, 16)
            sp.dma_start(g.ex_dn[:, e], g.w_dn[e].rearrange("(f p) n -> p f n", f=4)).then_inc(g.ex_in, 16)
            sp.dma_start(g.base_gu, g.w_gu[NE].rearrange("(k p) n -> p k n", k=KD)).then_inc(g.base_in, 16)
            sp.dma_start(g.base_dn, g.w_dn[NE].rearrange("(f p) n -> p f n", f=4)).then_inc(g.base_in, 16)
            sp.dma_start(g.wqkv1_raw, g.w_qkv1.rearrange("(k p) n -> p k n", k=KD)).then_inc(g.wqkv1_in, 16)
            sp.dma_start(g.wproj1_raw, g.w_proj1.rearrange("(k p) n -> p k n", k=KD)).then_inc(g.wproj1_in, 16)
            sp.wait_ge(zero_ready, 1)
            sp.dma_start(g.slots_x.rearrange("(t p) d -> p t d", p=P), zero.unsqueeze(1).to_broadcast([P, TILES, D])).then_inc(g.slots_clear, 16)
            with sp.Fori(1, NH0 // 2) as i:
                for s in range(2):
                    sp.wait_ge(conv_mm, 2 * i + s - 1)
                    sp.dma_start(toep[:, s, :], g.toeplitz[2 * i + s]).then_inc(toep_in[s], 16)

        @block.gpsimd
        def _(pool):
            nc.gpsimd.memset(zero[:, :], 0.0).then_inc(zero_ready, 1)
            ln.gpsimd(pool, 0)
            pool.wait_ge(ln.turned_out, ln.out(0))

            def products(n, s, first):
                if not first:
                    pool.wait_ge(conv_mm, n - 1)
                nc.gpsimd.tensor_tensor(kv[:, s, :].rearrange("p (c i j) -> p c i j", i=NI, j=NI),
                                        channels(vT, n).unsqueeze(3).to_broadcast(wide),
                                        channels(xT, n).unsqueeze(2).to_broadcast(wide), ALU.mult).then_inc(kv_ready, 1)

            products(0, 0, True)
            products(1, 1, True)
            with pool.Fori(1, NH0 // 2) as i:
                for s in range(2):
                    products(2 * i + s, s, False)
            pool.wait_ge(skips_done, 1)
            nc.gpsimd.tensor_tensor(vx.rearrange("p c (h j) -> p c h j", h=NH0), xT.rearrange("p c (h j) -> p c h j", h=NH0),
                                    skips.unsqueeze(3).to_broadcast([P, KD * B, NH0, NI]), ALU.mult).then_inc(skip_term, 1)

        @block.tensor
        def _(pe):
            ln.tensor(pe, 0)
            pe.wait_ge(ln.turned_out, ln.out(0))

            def convolve(n, s, i, first):
                pe.wait_ge(toep_in[s], 16 * (i + 1))
                pe.wait_ge(kv_ready, n + 1)
                if not first:
                    pe.wait_ge(z_ready, n - 1)
                near, far = toep[:, s, 0:P], toep[:, s, P:2 * P]
                nc.tensor.matmul(g.ps[:, 2 * s, :], near, kv[:, s, 0:N], start=True, stop=True)
                nc.tensor.matmul(g.ps[:, 2 * s + 1, :], near, kv[:, s, N:2 * N], start=True, stop=False)
                nc.tensor.matmul(g.ps[:, 2 * s + 1, :], far, kv[:, s, 0:N], start=False, stop=True).then_inc(conv_mm, 1)

            convolve(0, 0, 0, True)
            convolve(1, 1, 0, True)
            with pe.Fori(1, NH0 // 2) as i:
                for s in range(2):
                    convolve(2 * i + s, s, i, False)
            pe.wait_ge(oT_done, 1)
            for h in range(B // 2):
                for j in range(2):
                    for k in range(KD):
                        mm = nc.tensor.transpose(g.ps[:, 4 + h, (2 * j + k) * P:(2 * j + k + 1) * P],
                                                 oT[:, k * B + 2 * h + j, :], g.ident)
                mm.then_inc(back_mm, 1)

        @block.scalar
        def _(act):
            ln.scalar(act, 0, pair_of(g.xnT))

        @block.vector
        def _(dve):
            ln.vector(dve, 0)
            dve.wait_ge(ln.turned_out, ln.out(0))
            dve.wait_ge(skip_in, 16)
            nc.vector.tensor_tensor(vx[:, :, :], vT, xT, ALU.mult).then_inc(vx_done, 1)
            dve.wait_ge(vx_done, 1)
            nc.vector.tensor_tensor(vx[:, :, :], vx[:, :, :], skip[:, :].unsqueeze(1).to_broadcast([P, KD * B, P]),
                                    ALU.mult).then_inc(vx_done, 1)
            dve.wait_ge(vx_done, 2)
            nc.vector.tensor_reduce(skips[:, :, :], vx.rearrange("p c (h i) -> p c h i", h=NH0), AX.X, ALU.add).then_inc(skips_done, 1)

            def gather(n, s):
                dve.wait_ge(conv_mm, n + 1)
                nc.vector.tensor_tensor(z[:, s, :].rearrange("p (c i j) -> p c i j", i=NI, j=NI),
                                        g.ps[:, 2 * s:2 * s + 2, :].rearrange("p k (b i j) -> p (k b) i j", i=NI, j=NI),
                                        channels(xT, n).unsqueeze(3).to_broadcast(wide), ALU.mult).then_inc(z_ready, 1)
                dve.wait_ge(z_ready, n + 1)
                nc.vector.tensor_reduce(channels(oT, n), z[:, s, :].rearrange("p (c i j) -> p c j i", i=NI, j=NI),
                                        AX.X, ALU.add).then_inc(head_out, 1)

            with dve.Fori(0, NH0 // 2) as i:
                for s in range(2):
                    gather(2 * i + s, s)
            dve.wait_ge(head_out, NH0)
            dve.wait_ge(skip_term, 1)
            nc.vector.tensor_tensor(oT[:, :, :], oT[:, :, :], vx[:, :, :], ALU.add).then_inc(oT_done, 1)
            for h in range(B // 2):
                dve.wait_ge(back_mm, h + 1)
                dst = g.x_sb[:, 2 * h:2 * h + 2, :]
                nc.vector.tensor_tensor(dst, dst, g.ps[:, 4 + h, :].rearrange("p (j l) -> p j l", j=2), ALU.add).then_inc(back_added, 1)
            dve.wait_ge(back_added, B // 2)


ROUND = 1.5 * 2.0 ** 23


class GatedExpert:

    def __init__(self, nc, g, tag, ctx, nf, kept):
        self.nc, self.g, self.nf, self.kept = nc, g, nf, kept
        self.sg = ctx.enter_context(nc.sbuf_tensor(tag + "_sg", [P, 2, 512], F32))
        self.h = ctx.enter_context(nc.sbuf_tensor(tag + "_h", [P, kept, nf, 512], F32))
        self.gu_mm = ctx.enter_context(nc.semaphore(tag + "_gu_mm"))
        self.silu_done = ctx.enter_context(nc.semaphore(tag + "_silu_done"))
        self.h_ready = ctx.enter_context(nc.semaphore(tag + "_h_ready"))
        self.y_mm = ctx.enter_context(nc.semaphore(tag + "_y_mm"))
        self.y_added = ctx.enter_context(nc.semaphore(tag + "_y_added"))

    def tensor_block(self, half, f, gu):
        nc, g, nf = self.nc, self.g, self.nf
        n = nf * half + f
        if n >= 2:
            nc.tensor.wait_ge(self.h_ready, n - 1)
        for a in range(2):
            col = (a * nf + f) * P
            for k in range(KD):
                mm = nc.tensor.matmul(g.ps[:, 2 * (f % 2) + a, :], gu[:, k, col:col + P],
                                      g.xnT[:, k, half * 512:(half + 1) * 512], start=(k == 0), stop=(k == KD - 1))
        mm.then_inc(self.gu_mm, 1)

    def tensor_down(self, half, dn):
        nc, g, nf = self.nc, self.g, self.nf
        nc.tensor.wait_ge(self.h_ready, nf * (half + 1))
        for q in (2 * half, 2 * half + 1):
            for j in range(2):
                t = 2 * (q % 2) + j
                for f in range(nf):
                    mm = nc.tensor.matmul(g.ps[:, 4 + q, j * D:(j + 1) * D], self.h[:, half % self.kept, f, t * P:(t + 1) * P],
                                          dn[:, f, :], start=(f == 0), stop=(f == nf - 1))
            mm.then_inc(self.y_mm, 1)

    def scalar_block(self, act, half, f):
        nc, g, nf = self.nc, self.g, self.nf
        n = nf * half + f
        act.wait_ge(self.gu_mm, n + 1)
        if n >= 2:
            act.wait_ge(self.h_ready, n - 1)
        nc.scalar.activation(self.sg[:, n % 2, :], g.ps[:, 2 * (n % 2), :], ACT.Silu).then_inc(self.silu_done, 1)

    def vector_block(self, dve, half, f):
        nc, g, nf = self.nc, self.g, self.nf
        n = nf * half + f
        dve.wait_ge(self.silu_done, n + 1)
        nc.vector.tensor_tensor(self.h[:, half % self.kept, f, :], self.sg[:, n % 2, :], g.ps[:, 2 * (n % 2) + 1, :],
                                ALU.mult).then_inc(self.h_ready, 1)

    def vector_add(self, dve, q):
        nc, g = self.nc, self.g
        dve.wait_ge(self.y_mm, q + 1)
        dst = g.x_sb[:, 2 * q:2 * q + 2, :]
        nc.vector.tensor_tensor(dst, dst, g.ps[:, 4 + q, :].rearrange("p (j n) -> p j n", j=2), ALU.add).then_inc(self.y_added, 1)


def layer0_experts(nc, g):
    with ExitStack() as ctx:
        def sb(name, shape, dt=F32):
            return whole(ctx.enter_context(nc.sbuf_tensor(name, shape, dt)), shape)

        def sem(name):
            return ctx.enter_context(nc.semaphore(name))

        ln = g.ln
        ex = GatedExpert(nc, g, "c", ctx, 4, 1)
        gate_w = sb("c_gate_w", [P, KD, NE])
        lmax, lsum, lrec = sb("c_lmax", [P, B]), sb("c_lsum", [P, B]), sb("c_lrec", [P, B])
        prob = sb("c_prob", [P, B, NE])
        above = sb("c_above", [P, B, NE, NE])
        tied = sb("c_tied", [P, B, NE, NE])
        rank = sb("c_rank", [P, B, NE])
        chosen = sb("c_chosen", [P, B, NE])
        weight = sb("c_weight", [P, TOP, B])
        tiles_of = sb("c_tiles_of", [P, NE])
        tiles_to = sb("c_tiles_to", [P, NE])
        tiles_from = sb("c_tiles_from", [P, NE])
        place = sb("c_place", [P, B, NE])
        mine_at = sb("c_mine_at", [P, B, NE])
        slot = sb("c_slot", [P, TOP, B], mybir.dt.uint32)
        past = sb("c_past", [P, TILES, NE])
        expert_f = sb("c_expert_f", [P, TILES])
        expert_of = sb("c_expert_of", [P, TILES], mybir.dt.int32)
        HID = 4 * P
        rows = sb("c_rows", [P, 2, D])
        rowsT = sb("c_rowsT", [P, 2, KD, P])
        sg = g.xn[:, 0:B // 2, :].rearrange("p (s b) d -> p s (b d)", s=2)
        hid = g.xn[:, B // 2:B, :].rearrange("p (s b) d -> p s (b d)", s=2)
        hidT = sb("c_tile_hT", [P, 2, 4, P])
        y = sb("c_tile_y", [P, 2, D])
        back = g.expert_back
        gate_in, logit_mm, expd = sem("gate_in"), sem("logit_mm"), sem("c_expd")
        step = sem("router_step")
        chosen_ready, place_mm, slots_ready, tiles_ready = sem("chosen_ready"), sem("place_mm"), sem("slots_ready"), sem("tiles_ready")
        scattered = sem("scattered")
        rows_in = [sem("rows_in0"), sem("rows_in1")]
        rows_mm, rowsT_out, tile_mm, tile_silu, tile_h = sem("rows_mm"), sem("rowsT_out"), sem("tile_mm"), sem("tile_silu"), sem("tile_h")
        hT_mm, hT_out, tile_y_mm, tile_y_out = sem("hT_mm"), sem("hT_out"), sem("tile_y_mm"), sem("tile_y_out")
        y_stored = [sem("y_stored0"), sem("y_stored1")]
        gathered, back_added = sem("gathered"), sem("c_back_added")
        quant = Ternary(nc, g, ctx)
        X_BANK, H_BANK, Y_BANK = 4, 5, 6
        LOOP = (TILES - 3) // 2
        assert 2 + 2 * LOOP == TILES - 1

        block = ctx.enter_context(nc.Block())

        @block.sync
        def _(sp):
            sp.dma_start(gate_w[:, :, :], g.gate_w.rearrange("(k p) n -> p k n", k=KD)).then_inc(gate_in, 16)

            def load(n, s):
                sp.dma_start(rows[:, s, :], g.slots_x[bass.ds(n * P, P), :]).then_inc(rows_in[s], 16)

            def store(n, s):
                sp.wait_ge(tile_y_out, n + 1)
                sp.dma_start(g.slots_y[bass.ds(n * P, P), :], y[:, s, :]).then_inc(y_stored[s], 16)

            sp.wait_ge(scattered, 16 * TOP * B)
            load(0, 0)
            load(1, 1)
            sp.wait_ge(rows_mm, 1)
            load(2, 0)
            sp.wait_ge(rows_mm, 2)
            load(3, 1)
            with sp.Fori(0, LOOP - 1) as i:
                for s in range(2):
                    store(2 * i + s, s)
                    sp.wait_ge(rows_mm, 2 * i + s + 3)
                    load(2 * i + s + 4, s)
            last = 2 * LOOP - 2
            store(last, 0)
            sp.wait_ge(rows_mm, last + 3)
            load(last + 4, 0)
            for n in range(last + 1, TILES):
                store(n, n % 2)

        @block.gpsimd
        def _(pool):
            ln.gpsimd(pool, 1)
            pool.wait_ge(g.slots_clear, 16)
            pool.wait_ge(slots_ready, 1)
            for r in range(TOP):
                for b in range(B):
                    nc.gpsimd.indirect_dma_start(g.slots_x[:, :], bass.IndirectOffsetOnAxis(ap=slot[:, r, b:b + 1], axis=0),
                                                 g.xn[:, b, :], None).then_inc(scattered, 16)
            quant.gpsimd(pool)
            for s in range(2):
                pool.wait_ge(y_stored[s], 16 * ((TILES + 1 - s) // 2))
            for b in range(B):
                for r in range(TOP):
                    nc.gpsimd.indirect_dma_start(back[:, r, b, :], None, g.slots_y[:, :],
                                                 bass.IndirectOffsetOnAxis(ap=slot[:, r, b:b + 1], axis=0)).then_inc(gathered, 16)

        @block.tensor
        def _(pe):
            ln.tensor(pe, 1)
            pe.wait_ge(gate_in, 16)
            for b in range(B):
                if b % 2 == 0:
                    pe.wait_ge(ln.turned_out, ln.out(1, b // 2 + 1))
                for k in range(KD):
                    mm = nc.tensor.matmul(g.ps[:, 7, b * NE:(b + 1) * NE], g.xnT[:, k, b * S:(b + 1) * S], gate_w[:, k, :],
                                          start=(k == 0), stop=(k == KD - 1))
            mm.then_inc(logit_mm, 1)
            pe.wait_ge(g.base_in, 32)
            ex.tensor_block(0, 0, g.base_gu)
            ex.tensor_block(0, 1, g.base_gu)
            pe.wait_ge(chosen_ready, 1)
            earlier, ones = g.const[:, C_EARLIER:C_EARLIER + P], g.const[:, C_ONES:C_ONES + P]
            flat = chosen.rearrange("p b e -> p (b e)")
            nc.tensor.matmul(g.ps[:, 7, 64:128], earlier, flat, start=True, stop=False, skip_group_check=True)
            for b in range(B - 1):
                nc.tensor.matmul(g.ps[:, 7, 64 + NE * (b + 1):128], ones, chosen[:, b, :].unsqueeze(1).to_broadcast([P, B - 1 - b, NE]),
                                 start=False, stop=False, skip_group_check=True)
            for b in range(B):
                mm = nc.tensor.matmul(g.ps[:, 7, 128:128 + NE], ones, chosen[:, b, :], start=False, stop=True, skip_group_check=True)
            mm.then_inc(place_mm, 1)
            ex.tensor_block(0, 2, g.base_gu)
            ex.tensor_block(0, 3, g.base_gu)
            ex.tensor_down(0, g.base_dn)

            def turn_rows(n, s, i, first=False):
                pe.wait_ge(rows_in[s], 16 * (i + 1))
                if not first:
                    pe.wait_ge(rowsT_out, n)
                for k in range(KD):
                    mm = nc.tensor.transpose(g.ps[:, X_BANK, k * P:(k + 1) * P], rows[:, s, k * P:(k + 1) * P], g.ident)
                mm.then_inc(rows_mm, 1)

            def up(n, s, first=False):
                pe.wait_ge(rowsT_out, n + 1)
                if not first:
                    pe.wait_ge(tile_h, n - 1)
                e = pe.value_load(expert_of[0:1, bass.ds(n, 1)], min_val=0, max_val=NE - 1)
                for a in range(2):
                    for k in range(KD):
                        mm = nc.tensor.matmul(g.ps[:, 2 * s + a, :], rowsT[:, s, k, :], g.ex_gu[:, e, k, a * HID:(a + 1) * HID],
                                              start=(k == 0), stop=(k == KD - 1))
                mm.then_inc(tile_mm, 1)

            def turn_h(n, s, first=False):
                pe.wait_ge(tile_h, n + 1)
                if not first:
                    pe.wait_ge(hT_out, n)
                for f in range(4):
                    mm = nc.tensor.transpose(g.ps[:, H_BANK, f * P:(f + 1) * P], hid[:, s, f * P:(f + 1) * P], g.ident)
                mm.then_inc(hT_mm, 1)

            def down(n, s, first=False):
                pe.wait_ge(hT_out, n + 1)
                if not first:
                    pe.wait_ge(tile_y_out, n - 1)
                e = pe.value_load(expert_of[0:1, bass.ds(n, 1)], min_val=0, max_val=NE - 1)
                for f in range(4):
                    mm = nc.tensor.matmul(g.ps[:, Y_BANK + s, 0:D], hidT[:, s, f, :], g.ex_dn[:, e, f, :],
                                          start=(f == 0), stop=(f == 3))
                mm.then_inc(tile_y_mm, 1)

            pe.wait_ge(g.ex_in, 32 * NE)
            pe.wait_ge(tiles_ready, 1)
            pe.wait_ge(ex.y_added, 2)
            turn_rows(0, 0, 0, True)
            turn_rows(1, 1, 0)
            up(0, 0, True)
            up(1, 1, True)
            turn_h(0, 0, True)
            turn_rows(2, 0, 1)

            def pair(i, first):
                for s in range(2):
                    n = 2 * i + s
                    up(n, s)
                    turn_h(n - 1, 1 - s)
                    turn_rows(n + 1, 1 - s, i + s)
                    down(n - 2, s, first)

            pair(1, True)
            with pe.Fori(2, LOOP + 1) as i:
                pair(i, False)
            last = TILES - 1
            up(last, 0)
            turn_h(last - 1, 1)
            down(last - 2, 0)
            turn_h(last, 0)
            down(last - 1, 1)
            down(last, 0)
            for f in range(4):
                ex.tensor_block(1, f, g.base_gu)
            pe.wait_ge(tile_y_out, TILES)
            ex.tensor_down(1, g.base_dn)

        @block.scalar
        def _(act):
            ln.scalar(act, 1, pair_of(g.xnT))
            act.wait_ge(step, 2)
            nc.scalar.activation(prob[:, :, :], prob[:, :, :], ACT.Exp).then_inc(expd, 1)
            for f in range(4):
                ex.scalar_block(act, 0, f)

            def rows_out(n, s):
                act.wait_ge(rows_mm, n + 1)
                nc.scalar.copy(rowsT[:, s], g.ps[:, X_BANK, 0:D].rearrange("p (k t) -> p k t", k=KD)).then_inc(rowsT_out, 1)

            def silu(n, s):
                act.wait_ge(tile_mm, n + 1)
                nc.scalar.activation(sg[:, s, :], g.ps[:, 2 * s, :], ACT.Silu).then_inc(tile_silu, 1)

            def h_out(n, s):
                act.wait_ge(hT_mm, n + 1)
                nc.scalar.copy(hidT[:, s], g.ps[:, H_BANK, :].rearrange("p (f t) -> p f t", f=4)).then_inc(hT_out, 1)

            rows_out(0, 0)
            rows_out(1, 1)
            silu(0, 0)
            silu(1, 1)
            h_out(0, 0)
            rows_out(2, 0)
            with act.Fori(1, LOOP + 1) as i:
                for s in range(2):
                    n = 2 * i + s
                    silu(n, s)
                    h_out(n - 1, 1 - s)
                    rows_out(n + 1, 1 - s)
            last = TILES - 1
            silu(last, 0)
            h_out(last - 1, 1)
            h_out(last, 0)
            for f in range(4):
                ex.scalar_block(act, 1, f)

        @block.vector
        def _(dve):
            ln.vector(dve, 1)
            wide = [P, B, NE, NE]
            mine, other = prob.unsqueeze(3).to_broadcast(wide), prob.unsqueeze(2).to_broadcast(wide)
            per_token = [P, B, NE]
            done = 0

            def stepped(ins):
                nonlocal done
                done += 1
                ins.then_inc(step, 1)
                dve.wait_ge(step, done)

            dve.wait_ge(logit_mm, 1)
            logits = g.ps[:, 7, 0:B * NE].rearrange("p (b e) -> p b e", b=B)
            stepped(nc.vector.tensor_reduce(lmax[:, :], logits, AX.X, ALU.max))
            stepped(nc.vector.tensor_tensor(prob[:, :, :], logits, lmax.unsqueeze(2).to_broadcast(per_token), ALU.subtract))
            dve.wait_ge(expd, 1)
            stepped(nc.vector.tensor_reduce(lsum[:, :], prob[:, :, :], AX.X, ALU.add))
            stepped(nc.vector.reciprocal(lrec[:, :], lsum[:, :]))
            stepped(nc.vector.tensor_tensor(prob[:, :, :], prob[:, :, :], lrec.unsqueeze(2).to_broadcast(per_token), ALU.mult))
            stepped(nc.vector.tensor_tensor(above[:, :, :, :], other, mine, ALU.is_gt))
            stepped(nc.vector.tensor_tensor(tied[:, :, :, :], other, mine, ALU.is_equal))
            lower = g.const[:, C_LOWER:C_LOWER + NE * NE].rearrange("p (e j) -> p e j", e=NE).unsqueeze(1).to_broadcast(wide)
            stepped(nc.vector.tensor_tensor(tied[:, :, :, :], tied[:, :, :, :], lower, ALU.mult))
            stepped(nc.vector.tensor_tensor(above[:, :, :, :], above[:, :, :, :], tied[:, :, :, :], ALU.add))
            stepped(nc.vector.tensor_reduce(rank[:, :, :], above[:, :, :, :], AX.X, ALU.add))
            nc.vector.tensor_scalar(chosen[:, :, :], rank[:, :, :], float(TOP), None, ALU.is_lt).then_inc(chosen_ready, 1)
            ex.vector_block(dve, 0, 0)
            ex.vector_block(dve, 0, 1)
            dve.wait_ge(place_mm, 1)
            places = g.ps[:, 7, 64:128].rearrange("p (b e) -> p b e", b=B)
            stepped(nc.vector.tensor_scalar(tiles_of[:, :], g.ps[:, 7, 128:128 + NE], 1.0 / P, (P - 1) / P - 0.5 + 0.5 / P, ALU.mult, ALU.add))
            stepped(nc.vector.tensor_scalar(tiles_of[:, :], tiles_of[:, :], ROUND, None, ALU.add))
            stepped(nc.vector.tensor_scalar(tiles_of[:, :], tiles_of[:, :], ROUND, None, ALU.subtract))
            stepped(nc.vector.tensor_tensor_scan(tiles_to[:, :], g.const[:, C_ONES:C_ONES + NE], tiles_of[:, :], 0.0, ALU.mult, ALU.add))
            stepped(nc.vector.tensor_tensor(tiles_from[:, :], tiles_to[:, :], tiles_of[:, :], ALU.subtract))
            stepped(nc.vector.scalar_tensor_tensor(out=place[:, :, :], in0=tiles_from.unsqueeze(1).to_broadcast(per_token), scalar=float(P),
                                                   in1=places, op0=ALU.mult, op1=ALU.add))
            for r in range(TOP):
                stepped(nc.vector.scalar_tensor_tensor(out=mine_at[:, :, :], in0=rank[:, :, :], scalar=float(r), in1=place[:, :, :],
                                                       op0=ALU.is_equal, op1=ALU.mult))
                stepped(nc.vector.tensor_reduce(lmax[:, :], mine_at[:, :, :], AX.X, ALU.add))
                stepped(nc.vector.tensor_copy(slot[:, r, :], lmax[:, :]))
            dve.sem_inc(slots_ready, 1)
            stepped(nc.vector.tensor_tensor(past[:, :, :], tiles_to.unsqueeze(1).to_broadcast([P, TILES, NE]),
                                            g.const[:, C_COUNT:C_COUNT + TILES].unsqueeze(2).to_broadcast([P, TILES, NE]), ALU.is_le))
            stepped(nc.vector.tensor_reduce(expert_f[:, :], past[:, :, :], AX.X, ALU.add))
            stepped(nc.vector.tensor_scalar(expert_f[:, :], expert_f[:, :], float(NE - 1), None, ALU.min))
            nc.vector.tensor_copy(expert_of[:, :], expert_f[:, :]).then_inc(tiles_ready, 1)
            ex.vector_block(dve, 0, 2)
            ex.vector_block(dve, 0, 3)
            for r in range(TOP):
                stepped(nc.vector.scalar_tensor_tensor(out=mine_at[:, :, :], in0=rank[:, :, :], scalar=float(r), in1=prob[:, :, :],
                                                       op0=ALU.is_equal, op1=ALU.mult))
                stepped(nc.vector.tensor_reduce(weight[:, r, :], mine_at[:, :, :], AX.X, ALU.add))
            stepped(nc.vector.tensor_tensor(lsum[:, :], weight[:, 0, :], weight[:, 1, :], ALU.add))
            stepped(nc.vector.reciprocal(lrec[:, :], lsum[:, :]))
            stepped(nc.vector.tensor_tensor(weight[:, :, :], weight[:, :, :], lrec.unsqueeze(1).to_broadcast([P, TOP, B]), ALU.mult))
            ex.vector_add(dve, 0)
            ex.vector_add(dve, 1)
            quant.vector(dve)

            def hidden(n, s, first=False):
                dve.wait_ge(tile_silu, n + 1)
                if not first:
                    dve.wait_ge(hT_mm, n - 1)
                nc.vector.tensor_tensor(hid[:, s, :], sg[:, s, :], g.ps[:, 2 * s + 1, :], ALU.mult).then_inc(tile_h, 1)

            def y_out(n, s, i, first=False):
                dve.wait_ge(tile_y_mm, n + 1)
                if not first:
                    dve.wait_ge(y_stored[s], 16 * i)
                nc.vector.tensor_copy(y[:, s, :], g.ps[:, Y_BANK + s, 0:D]).then_inc(tile_y_out, 1)

            hidden(0, 0, True)
            hidden(1, 1, True)
            for s in range(2):
                hidden(2 + s, s)
                y_out(s, s, 0, True)
            with dve.Fori(2, LOOP + 1) as i:
                for s in range(2):
                    hidden(2 * i + s, s)
                    y_out(2 * i + s - 2, s, i - 1)
            last = TILES - 1
            hidden(last, 0)
            for n in range(last - 2, TILES):
                y_out(n, n % 2, n // 2)
            for f in range(4):
                ex.vector_block(dve, 1, f)
            for b in range(B):
                dve.wait_ge(gathered, 16 * TOP * B)
                for r in range(TOP):
                    if r > 0:
                        dve.wait_ge(back_added, TOP * b + r)
                    nc.vector.scalar_tensor_tensor(out=g.x_sb[:, b, :], in0=back[:, r, b, :], scalar=weight[:, r, b:b + 1],
                                                   in1=g.x_sb[:, b, :], op0=ALU.mult, op1=ALU.add).then_inc(back_added, 1)
            dve.wait_ge(back_added, TOP * B)
            ex.vector_add(dve, 2)
            ex.vector_add(dve, 3)
            dve.wait_ge(ex.y_added, 4)


class Ternary:

    def __init__(self, nc, g, ctx):
        self.nc, self.g = nc, g
        self.asum = ctx.enter_context(nc.sbuf_tensor("t_asum", [P, 2], F32))
        self.total = ctx.enter_context(nc.sbuf_tensor("t_total", [P, 2], F32))
        self.inv = ctx.enter_context(nc.sbuf_tensor("t_inv", [P, 2], F32))
        self.asum_done = ctx.enter_context(nc.semaphore("ternary_asum_done"))
        self.total_done = ctx.enter_context(nc.semaphore("ternary_total_done"))
        self.step = ctx.enter_context(nc.semaphore("ternary_step"))

    def gpsimd(self, pool):
        pool.wait_ge(self.asum_done, 2)
        self.nc.gpsimd.partition_all_reduce(self.total[:, :], self.asum[:, :], P,
                                            bass.bass_isa.ReduceOp.add).then_inc(self.total_done, 1)

    def vector(self, dve):
        nc, g = self.nc, self.g
        raws, outs = (g.wqkv1_raw, g.wproj1_raw), (g.wqkv1, g.wproj1)
        dve.wait_ge(g.wqkv1_in, 16)
        dve.wait_ge(g.wproj1_in, 16)
        for i, raw in enumerate(raws):
            nc.vector.tensor_reduce(self.asum[:, i:i + 1], raw.rearrange("p k n -> p (k n)"), AX.X, ALU.add,
                                    apply_absolute_value=True).then_inc(self.asum_done, 1)
        dve.wait_ge(self.total_done, 1)
        done = 0
        for i, raw in enumerate(raws):
            n = P * raw.shape[1] * raw.shape[2]
            nc.vector.tensor_scalar(g.wmean[:, i:i + 1], self.total[:, i:i + 1], 1.0 / n, 1e-5, ALU.mult, ALU.max).then_inc(self.step, 1)
            done += 1
            dve.wait_ge(self.step, done)
            nc.vector.reciprocal(self.inv[:, i:i + 1], g.wmean[:, i:i + 1]).then_inc(self.step, 1)
            done += 1
            dve.wait_ge(self.step, done)
            nc.vector.tensor_scalar(raw[:, :, :], raw[:, :, :], self.inv[:, i:i + 1], ROUND, ALU.mult, ALU.add).then_inc(self.step, 1)
            done += 1
            dve.wait_ge(self.step, done)
            nc.vector.tensor_scalar(raw[:, :, :], raw[:, :, :], ROUND, 1.0, ALU.subtract, ALU.min).then_inc(self.step, 1)
            done += 1
            dve.wait_ge(self.step, done)
            nc.vector.tensor_scalar(outs[i][:, :, :], raw[:, :, :], -1.0, None, ALU.max).then_inc(self.step, 1)
            done += 1
        dve.wait_ge(self.step, done)


NH1, HD1 = 16, 16
SLOT = 32
QUADS = NH1 * SLOT // P


class QuantizedTokens:

    def __init__(self, nc, g, tag, ctx, which):
        self.nc, self.g, self.which = nc, g, which
        def sb(name, shape, dt=F32):
            return whole(ctx.enter_context(nc.sbuf_tensor(tag + name, shape, dt)), shape)
        self.amax = sb("_amax", [P, B])
        self.inv = sb("_inv", [P, B])
        self.scale = sb("_scale", [P, B, 1])
        self.ints = sb("_ints", [P, B, D], BF16)
        self.intsT = sb("_intsT", [P, KD, B * S], BF16)
        self.step = ctx.enter_context(nc.semaphore(tag + "_q_step"))
        self.ints_ready = ctx.enter_context(nc.semaphore(tag + "_q_ints_ready"))
        self.turned_mm = ctx.enter_context(nc.semaphore(tag + "_q_turned_mm"))
        self.turned_out = ctx.enter_context(nc.semaphore(tag + "_q_turned_out"))

    def vector(self, dve, src):
        nc, g = self.nc, self.g
        def step(ins, n):
            ins.then_inc(self.step, 1)
            dve.wait_ge(self.step, n)
        step(nc.vector.tensor_reduce(self.amax[:, :], src, AX.X, ALU.max, apply_absolute_value=True), 1)
        step(nc.vector.tensor_scalar(self.amax[:, :], self.amax[:, :], 1e-5, None, ALU.max), 2)
        step(nc.vector.reciprocal(self.inv[:, :], self.amax[:, :]), 3)
        step(nc.vector.tensor_scalar(self.inv[:, :], self.inv[:, :], 127.0, None, ALU.mult), 4)
        step(nc.vector.tensor_scalar(self.scale[:, :, 0], self.amax[:, :], 1.0 / 127.0, g.wmean[:, self.which:self.which + 1],
                                     ALU.mult, ALU.mult), 5)
        for h in range(B // 2):
            for b in (2 * h, 2 * h + 1):
                ins = nc.vector.tensor_scalar(src[:, b, :], src[:, b, :], self.inv[:, b:b + 1], ROUND, ALU.mult, ALU.add)
            step(ins, 6 + 2 * h)
            two = src[:, 2 * h:2 * h + 2, :]
            step(nc.vector.tensor_scalar(two, two, ROUND, 127.0, ALU.subtract, ALU.min), 7 + 2 * h)
            nc.vector.tensor_scalar(self.ints[:, 2 * h:2 * h + 2, :], two, -128.0, None, ALU.max).then_inc(self.ints_ready, 1)

    def tensor(self, pe):
        nc, g = self.nc, self.g
        for h in range(B // 2):
            pe.wait_ge(self.ints_ready, h + 1)
            for k in range(KD):
                for j in range(2):
                    mm = nc.tensor.matmul(g.ps[:, h, (2 * k + j) * S:(2 * k + j + 1) * S],
                                          self.ints[:, 2 * h + j, k * P:(k + 1) * P], g.ident_bf, start=True, stop=True)
            mm.then_inc(self.turned_mm, 1)

    def scalar(self, act):
        nc, g = self.nc, self.g
        for h in range(B // 2):
            act.wait_ge(self.turned_mm, h + 1)
            nc.scalar.copy(self.intsT[:, :, 2 * h * S:2 * (h + 1) * S],
                           g.ps[:, h, :].rearrange("p (k s) -> p k s", k=KD)).then_inc(self.turned_out, 1)


def layer1_attention(nc, g):
    with ExitStack() as ctx:
        def sb(name, shape, dt=F32):
            return whole(ctx.enter_context(nc.sbuf_tensor(name, shape, dt)), shape)

        def sem(name):
            return ctx.enter_context(nc.semaphore(name))

        ln = g.ln
        qin = QuantizedTokens(nc, g, "d_in", ctx, 0)
        qout = QuantizedTokens(nc, g, "d_out", ctx, 1)
        qk_pad = sb("d_qk_pad", [P, 2 * NH1, SLOT])
        qkT = sb("d_qkT", [P, 2 * QUADS, S])
        v1 = sb("d_v1", [P, 2, NH1, SLOT])
        prob = sb("d_prob", [P, 2, 8, S])
        probT = sb("d_probT", [P, 2, 2, 4 * S])
        headT = sb("d_headT", [P, QUADS, S])
        rmax = sb("d_rmax", [P, 2, 8])
        rden = sb("d_rden", [P, NH1])
        att = sb("d_att", [P, B, D])
        cleared = sem("d_cleared")
        qk_mm, qk_out, v_mm, v_out = sem("d_qk_mm"), sem("d_qk_out"), sem("d_v_mm"), sem("d_v_out")
        qkT_mm, qkT_out = sem("d_qkT_mm"), sem("d_qkT_out")
        score_mm, rmax_done, shifted, expd = sem("d_score_mm"), sem("d_rmax_done"), sem("d_shifted"), sem("d_expd")
        probT_mm, probT_out, av_mm, rden_done, att_out = (
            sem("d_probT_mm"), sem("d_probT_out"), sem("d_av_mm"), sem("d_rden_done"), sem("d_att_out"))
        headT_out, back_mm = sem("d_headT_out"), sem("d_back_mm")
        y_mm, y_added = sem("d_y_mm"), sem("d_y_added")
        ps = g.ps
        T_BANK, PT_BANK, V_BANK, BACK_BANK, QK_BANK, AV_BANK = 0, 4, 4, 5, 6, 7
        U = 2
        LOOP = (B - 2) // 2

        block = ctx.enter_context(nc.Block())

        @block.sync
        def _(sp):
            sp.dma_start(g.ffn_gu[:, :, :], g.w_gu1.rearrange("(k p) n -> p k n", k=KD)).then_inc(g.ffn_gu_in, 16)
            sp.dma_start(g.ffn_dn[:, :, :], g.w_dn1.rearrange("(k p) n -> p k n", p=P)).then_inc(g.ffn_dn_in, 16)

        @block.gpsimd
        def _(pool):
            nc.gpsimd.memset(qk_pad[:, :, :], 0.0).then_inc(cleared, 1)
            nc.gpsimd.memset(v1[:, :, :, :], 0.0).then_inc(cleared, 1)
            pool.wait_ge(cleared, 2)
            nc.gpsimd.memset(v1[:, :, :, HD1:HD1 + 1], 1.0).then_inc(cleared, 1)
            ln.gpsimd(pool, 2)

        @block.scalar
        def _(act):
            qin.scalar(act)

            def qkT_copy(b):
                for t in range(2):
                    act.wait_ge(qkT_mm, 2 * b + t + 1)
                    nc.scalar.copy(qkT[:, 4 * t:4 * t + 4, :], ps[:, T_BANK + t, :].rearrange("p (c s) -> p c s", c=4)).then_inc(qkT_out, 1)

            def exp(u, b):
                act.wait_ge(shifted, U * b + u + 1)
                nc.scalar.activation(prob[:, u], prob[:, u], ACT.Exp, scale=HD1 ** -0.5).then_inc(expd, 1)

            def probT_copy(u, b):
                for p in range(2):
                    act.wait_ge(probT_mm, 2 * (U * b + u) + p + 1)
                    nc.scalar.copy(probT[:, u, p, :], ps[:, PT_BANK + p, :]).then_inc(probT_out, 1)

            def headT_copy(b):
                act.wait_ge(av_mm, b + 1)
                nc.scalar.copy(headT[:, :, :], ps[:, AV_BANK, :].rearrange("p (c s) -> p c s", c=QUADS)).then_inc(headT_out, 1)

            def body(b, first, last):
                exp(0, b)
                if not first:
                    headT_copy(b - 1)
                exp(1, b)
                if not last:
                    qkT_copy(b + 1)
                probT_copy(0, b)
                probT_copy(1, b)

            qkT_copy(0)
            body(0, True, False)
            with act.Fori(1, B - 1) as b:
                body(b, False, False)
            body(B - 1, False, True)
            headT_copy(B - 1)
            qout.scalar(act)

        @block.tensor
        def _(pe):
            qin.tensor(pe)
            pe.wait_ge(qin.turned_out, B // 2)

            def project(b, bank, cols, done):
                for k in range(KD):
                    mm = nc.tensor.matmul(ps[:, bank, 0:cols.stop - cols.start], qin.intsT[:, k, bass.ds(b * S, S)],
                                          g.wqkv1[:, k, cols], start=(k == 0), stop=(k == KD - 1))
                mm.then_inc(done, 1)

            def project_qk(b):
                project(b, QK_BANK, slice(0, 2 * D), qk_mm)

            def project_v(b):
                project(b, V_BANK, slice(2 * D, 3 * D), v_mm)

            def turn_qk(b):
                pe.wait_ge(qk_out, b + 1)
                for t in range(2):
                    for c in range(4):
                        mm = nc.tensor.transpose(ps[:, T_BANK + t, c * S:(c + 1) * S],
                                                 qk_pad[:, 16 * t + 4 * c:16 * t + 4 * c + 4, :].rearrange("p h d -> p (h d)"), g.ident)
                    mm.then_inc(qkT_mm, 1)

            def score(u, b):
                for p in range(2):
                    nc.tensor.matmul(ps[:, 2 * u + p, :], g.ident_bf, g.causal_bf.unsqueeze(1).to_broadcast([P, 4, S]),
                                     start=True, stop=False, skip_group_check=True)
                for c in range(QUADS):
                    for p in range(2):
                        rows = slice(SLOT * (2 * u + p), SLOT * (2 * u + p) + HD1)
                        mm = nc.tensor.matmul(ps[:, 2 * u + p, c * S:(c + 1) * S], qkT[rows, c, :], qkT[rows, QUADS + c, :],
                                              start=False, stop=True, skip_group_check=True,
                                              tile_position=(SLOT * (2 * u + p), 0))
                mm.then_inc(score_mm, 1)

            def turn_prob(u, b):
                pe.wait_ge(expd, U * b + u + 1)
                if u == 1:
                    pe.wait_ge(probT_out, 2 * U * b + 2)
                for p in range(2):
                    for i in range(4):
                        mm = nc.tensor.transpose(ps[:, PT_BANK + p, i * S:(i + 1) * S], prob[:, u, 4 * p + i, :], g.ident)
                    mm.then_inc(probT_mm, 1)

            def attend(b, s):
                pe.wait_ge(probT_out, 2 * U * (b + 1))
                for c in range(QUADS):
                    for r in range(4):
                        mm = nc.tensor.matmul(ps[SLOT * r:SLOT * (r + 1), AV_BANK, c * S:(c + 1) * S], v1[:, s, 4 * c + r, :],
                                              probT[:, r // 2, r % 2, c * S:(c + 1) * S], start=True, stop=True,
                                              skip_group_check=True)
                mm.then_inc(av_mm, 1)

            def turn_back(b):
                pe.wait_ge(headT_out, b + 1)
                for c in range(QUADS):
                    mm = nc.tensor.transpose(ps[:, BACK_BANK, c * P:(c + 1) * P], headT[:, c, :], g.ident)
                mm.then_inc(back_mm, 1)

            def body(b, s, first, last):
                pe.wait_ge(qkT_out, 2 * b + 2)
                score(0, b)
                if not first:
                    pe.wait_ge(shifted, U * b)
                score(1, b)
                if not first:
                    pe.wait_ge(v_out, b)
                    attend(b - 1, 1 - s)
                if not last:
                    project_qk(b + 1)
                    if not first:
                        pe.wait_ge(probT_out, 2 * U * b)
                    project_v(b + 1)
                if not first:
                    turn_back(b - 1)
                if not last:
                    pe.wait_ge(shifted, U * b + 1)
                    turn_qk(b + 1)
                    pe.wait_ge(v_out, b + 2)
                if not first:
                    pe.wait_ge(att_out, b)
                turn_prob(0, b)
                turn_prob(1, b)

            project_qk(0)
            project_v(0)
            turn_qk(0)
            pe.wait_ge(v_out, 1)
            body(0, 0, True, False)
            with pe.Fori(0, LOOP) as i:
                for s in (1, 0):
                    body(2 * i + 2 - s, s, False, False)
            body(B - 1, 1, False, True)
            attend(B - 1, 1)
            turn_back(B - 1)
            qout.tensor(pe)
            for h in range(B // 2):
                pe.wait_ge(qout.turned_out, h + 1)
                for j in range(2):
                    b = 2 * h + j
                    for k in range(KD):
                        mm = nc.tensor.matmul(ps[:, 4 + h, j * D:(j + 1) * D], qout.intsT[:, k, b * S:(b + 1) * S],
                                              g.wproj1[:, k, :], start=(k == 0), stop=(k == KD - 1))
                mm.then_inc(y_mm, 1)

        @block.vector
        def _(dve):
            ln.vector(dve, 2)
            dve.wait_ge(ln.xn_ready, B * 3)
            qin.vector(dve, g.xn)
            dve.wait_ge(cleared, 3)

            def out_qk(b):
                dve.wait_ge(qk_mm, b + 1)
                if not isinstance(b, int) or b > 0:
                    dve.wait_ge(qkT_mm, 2 * b)
                nc.vector.tensor_scalar(qk_pad[:, :, 0:HD1], ps[:, QK_BANK, :].rearrange("p (h d) -> p h d", d=HD1),
                                        qin.scale[:, b, :], None, ALU.mult).then_inc(qk_out, 1)

            def out_v(b, s):
                dve.wait_ge(v_mm, b + 1)
                nc.vector.tensor_scalar(v1[:, s, :, 0:HD1], ps[:, V_BANK, 0:D].rearrange("p (h d) -> p h d", d=HD1),
                                        qin.scale[:, b, :], None, ALU.mult).then_inc(v_out, 1)

            def shift(u, b):
                n = U * b + u
                dve.wait_ge(score_mm, n + 1)
                s = ps[:, 2 * u:2 * u + 2, :].rearrange("p a (i k) -> p (a i) k", i=4)
                nc.vector.tensor_reduce(rmax[:, u, :], s, AX.X, ALU.max).then_inc(rmax_done, 1)
                dve.wait_ge(rmax_done, n + 1)
                nc.vector.tensor_tensor(prob[:, u], s, rmax[:, u, :].unsqueeze(2).to_broadcast([P, 8, S]),
                                        ALU.subtract).then_inc(shifted, 1)

            def normalise(b):
                dve.wait_ge(back_mm, b + 1)
                o = ps[:, BACK_BANK, :].rearrange("p (h d) -> p h d", h=NH1)
                nc.vector.reciprocal(rden[:, :], o[:, :, HD1]).then_inc(rden_done, 1)
                dve.wait_ge(rden_done, b + 1)
                nc.vector.tensor_tensor(att[:, b, :].rearrange("p (h d) -> p h d", h=NH1), o[:, :, 0:HD1],
                                        rden.unsqueeze(2).to_broadcast([P, NH1, HD1]), ALU.mult).then_inc(att_out, 1)

            def body(b, s, first, last):
                shift(0, b)
                shift(1, b)
                if not last:
                    out_qk(b + 1)
                    out_v(b + 1, 1 - s)
                if not first:
                    normalise(b - 1)

            out_qk(0)
            out_v(0, 0)
            body(0, 0, True, False)
            with dve.Fori(0, LOOP) as i:
                for s in (1, 0):
                    body(2 * i + 2 - s, s, False, False)
            body(B - 1, 1, False, True)
            normalise(B - 1)
            dve.wait_ge(att_out, B)
            qout.vector(dve, att)
            for h in range(B // 2):
                dve.wait_ge(y_mm, h + 1)
                for j in range(2):
                    b = 2 * h + j
                    nc.vector.scalar_tensor_tensor(out=g.x_sb[:, b, :], in0=ps[:, 4 + h, j * D:(j + 1) * D],
                                                   scalar=qout.scale[:, b, :], in1=g.x_sb[:, b, :],
                                                   op0=ALU.mult, op1=ALU.add).then_inc(y_added, 1)
            dve.wait_ge(y_added, B)


NEVER = -1e38


def layer1_wkv(nc, g):
    with ExitStack() as ctx:
        def sb(name, shape, dt=F32):
            return whole(ctx.enter_context(nc.sbuf_tensor(name, shape, dt)), shape)

        def sem(name):
            return ctx.enter_context(nc.semaphore(name))

        T = S + 1
        k_pad = sb("e_k", [P, KD, B, T])
        ln = g.ln
        decay, first = sb("e_decay", [P, KD]), sb("e_first", [P, KD])
        w = sb("e_w", [P, KD])
        steps = sb("e_steps", [P, KD, B, T])
        run = {n: sb("e_" + n, [P, KD, B, T]) for n in ("pp", "aa", "bb", "keep", "new", "new_v")}
        q, old, now, num = (sb("e_" + n, [P, KD, B, S]) for n in ("q", "old", "now", "num"))
        den = g.xnT.rearrange("p k (b s) -> p k b s", b=B)
        params_in, w_ready, padded, steps_ready = sem("e_params_in"), sem("e_w_ready"), sem("e_padded"), sem("e_steps_ready")
        pp_done, q_done, keep_arg, new_arg, old_arg, now_arg = (
            sem("e_pp_done"), sem("e_q_done"), sem("e_keep_arg"), sem("e_new_arg"), sem("e_old_arg"), sem("e_now_arg"))
        exp_done, new_v_done, aa_done, bb_done = sem("e_exp_done"), sem("e_new_v_done"), sem("e_aa_done"), sem("e_bb_done")
        num_step, den_step, num_done, y_done, back_mm, y_added = (
            sem("e_num_step"), sem("e_den_step"), sem("e_num_done"), sem("e_y_done"), sem("e_back_mm"), sem("e_y_added"))

        def flat(t, k):
            return t[:, k].rearrange("p b t -> p (b t)")

        def at(n, k):
            return run[n][:, k, :, 1:T]

        def before(n, k):
            return run[n][:, k, :, 0:S]

        v = g.ctxT.rearrange("p k (b s) -> p k b s", b=B)
        block = ctx.enter_context(nc.Block())

        @block.sync
        def _(sp):
            sp.dma_start(decay[:, :], g.decay.rearrange("(k p) -> p k", k=KD), allow_slow_non_contiguous=True).then_inc(params_in, 16)
            sp.dma_start(first[:, :], g.first.rearrange("(k p) -> p k", k=KD), allow_slow_non_contiguous=True).then_inc(params_in, 16)

        @block.gpsimd
        def _(pool):
            nc.gpsimd.memset(k_pad[:, :, :, 0:1], NEVER).then_inc(padded, 1)
            nc.gpsimd.memset(run["keep"][:, :, :, 0:1], 0.0).then_inc(padded, 1)
            nc.gpsimd.memset(run["new"][:, :, :, 0:1], 0.0).then_inc(padded, 1)
            nc.gpsimd.memset(run["new_v"][:, :, :, 0:1], 0.0).then_inc(padded, 1)
            ln.gpsimd(pool, 3)
            for k in range(KD):
                pool.wait_ge(pp_done, k + 1)
                nc.gpsimd.tensor_tensor(at("new", k), k_pad[:, k, :, 1:T], at("pp", k), ALU.subtract).then_inc(new_arg, 1)
                pool.wait_ge(q_done, k + 1)
                nc.gpsimd.tensor_tensor(old[:, k], before("pp", k), q[:, k], ALU.subtract).then_inc(old_arg, 1)
                pool.wait_ge(exp_done, 4 * k + 2)
                nc.gpsimd.tensor_tensor(at("new_v", k), at("new", k), v[:, k], ALU.mult).then_inc(new_v_done, 1)
            for k in range(KD):
                pool.wait_ge(exp_done, 4 * k + 4)
                pool.wait_ge(aa_done, k + 1)
                nc.gpsimd.tensor_tensor(num[:, k], old[:, k], before("aa", k), ALU.mult).then_inc(num_step, 1)
                nc.gpsimd.tensor_tensor(q[:, k], now[:, k], v[:, k], ALU.mult).then_inc(num_step, 1)
                pool.wait_ge(num_step, 2 * k + 2)
                nc.gpsimd.tensor_tensor(num[:, k], num[:, k], q[:, k], ALU.add).then_inc(num_done, 1)

        @block.scalar
        def _(act):
            ln.scalar(act, 2, lambda h: k_pad[:, :, 2 * h:2 * h + 2, 1:T])
            act.wait_ge(params_in, 32)
            nc.scalar.activation(w[:, :], decay[:, :], ACT.Exp).then_inc(w_ready, 1)
            for k in range(KD):
                for ready, t in ((keep_arg, at("keep", k)), (new_arg, at("new", k)), (now_arg, now[:, k]), (old_arg, old[:, k])):
                    act.wait_ge(ready, k + 1)
                    nc.scalar.activation(t, t, ACT.Exp).then_inc(exp_done, 1)

        @block.tensor
        def _(pe):
            ln.tensor(pe, 3)
            for k in range(KD):
                pe.wait_ge(y_done, k + 1)
                for h in range(2):
                    for j in range(4):
                        mm = nc.tensor.transpose(g.ps[:, 4 + 2 * k + h, j * P:(j + 1) * P], num[:, k, 4 * h + j, :], g.ident)
                    mm.then_inc(back_mm, 1)

        @block.vector
        def _(dve):
            ln.vector(dve, 3)
            dve.wait_ge(w_ready, 1)
            nc.vector.tensor_scalar(w[:, :], w[:, :], -1.0, None, ALU.mult).then_inc(w_ready, 1)
            nc.vector.memset(steps[:, :, :, :], 0.0).then_inc(steps_ready, 1)
            dve.wait_ge(w_ready, 2)
            dve.wait_ge(steps_ready, 1)
            for k in range(KD):
                nc.vector.tensor_scalar(steps[:, k], steps[:, k], w[:, k:k + 1], None, ALU.add).then_inc(steps_ready, 1)
            dve.wait_ge(steps_ready, 3)
            nc.vector.memset(steps[:, :, :, 0:1], NEVER).then_inc(steps_ready, 1)
            dve.wait_ge(steps_ready, 4)
            dve.wait_ge(padded, 4)
            dve.wait_ge(ln.turned_out, ln.out(2))
            for k in range(KD):
                nc.vector.tensor_tensor_scan(flat(run["pp"], k), flat(steps, k), flat(k_pad, k), NEVER, ALU.add, ALU.max).then_inc(pp_done, 1)
                dve.wait_ge(pp_done, k + 1)
                k_now = k_pad[:, k, :, 1:T]
                nc.vector.scalar_tensor_tensor(out=at("keep", k), in0=before("pp", k), scalar=w[:, k:k + 1], in1=at("pp", k),
                                               op0=ALU.add, op1=ALU.subtract).then_inc(keep_arg, 1)
                nc.vector.scalar_tensor_tensor(out=q[:, k], in0=k_now, scalar=first[:, k:k + 1], in1=before("pp", k),
                                               op0=ALU.add, op1=ALU.max).then_inc(q_done, 1)
                dve.wait_ge(q_done, k + 1)
                nc.vector.scalar_tensor_tensor(out=now[:, k], in0=k_now, scalar=first[:, k:k + 1], in1=q[:, k],
                                               op0=ALU.add, op1=ALU.subtract).then_inc(now_arg, 1)
            for k in range(KD):
                dve.wait_ge(exp_done, 4 * k + 2)
                nc.vector.tensor_tensor_scan(flat(run["bb"], k), flat(run["keep"], k), flat(run["new"], k), 0.0,
                                             ALU.mult, ALU.add).then_inc(bb_done, 1)
                dve.wait_ge(new_v_done, k + 1)
                nc.vector.tensor_tensor_scan(flat(run["aa"], k), flat(run["keep"], k), flat(run["new_v"], k), 0.0,
                                             ALU.mult, ALU.add).then_inc(aa_done, 1)
                dve.wait_ge(bb_done, k + 1)
                dve.wait_ge(exp_done, 4 * k + 4)
                nc.vector.tensor_tensor(den[:, k], old[:, k], before("bb", k), ALU.mult).then_inc(den_step, 1)
                dve.wait_ge(den_step, 3 * k + 1)
                nc.vector.tensor_tensor(den[:, k], den[:, k], now[:, k], ALU.add).then_inc(den_step, 1)
                dve.wait_ge(den_step, 3 * k + 2)
                nc.vector.reciprocal(den[:, k], den[:, k]).then_inc(den_step, 1)
                dve.wait_ge(den_step, 3 * k + 3)
                dve.wait_ge(num_done, k + 1)
                nc.vector.tensor_tensor(num[:, k], num[:, k], den[:, k], ALU.mult).then_inc(y_done, 1)
            for k in range(KD):
                for h in range(2):
                    dve.wait_ge(back_mm, 2 * k + h + 1)
                    dst = g.x_sb[:, 4 * h:4 * h + 4, k * P:(k + 1) * P]
                    nc.vector.tensor_tensor(dst, dst, g.ps[:, 4 + 2 * k + h, :].rearrange("p (j c) -> p j c", j=4),
                                            ALU.add).then_inc(y_added, 1)
            dve.wait_ge(y_added, 2 * KD)


def layer1_ffn(nc, g):
    with ExitStack() as ctx:
        ln = g.ln
        ex = GatedExpert(nc, g, "f", ctx, 8, 2)
        stored = ctx.enter_context(nc.semaphore("stored"))
        block = ctx.enter_context(nc.Block())

        @block.gpsimd
        def _(pool):
            ln.gpsimd(pool, 4)

        @block.scalar
        def _(act):
            ln.scalar(act, 3, pair_of(g.xnT))
            for half in range(2):
                for f in range(ex.nf):
                    ex.scalar_block(act, half, f)

        @block.tensor
        def _(pe):
            ln.tensor(pe, 4)
            pe.wait_ge(g.ffn_gu_in, 16)
            pe.wait_ge(g.ffn_dn_in, 16)
            pe.wait_ge(ln.turned_out, ln.out(3))
            for half in range(2):
                for f in range(ex.nf):
                    ex.tensor_block(half, f, g.ffn_gu)
            for half in range(2):
                ex.tensor_down(half, g.ffn_dn)

        @block.vector
        def _(dve):
            ln.vector(dve, 4)
            for half in range(2):
                for f in range(ex.nf):
                    ex.vector_block(dve, half, f)
            for q in range(4):
                ex.vector_add(dve, q)

        @block.sync
        def _(sp):
            for q in range(4):
                sp.wait_ge(ex.y_added, q + 1)
                sp.dma_start(g.out.rearrange("b s d -> s b d")[:, 2 * q:2 * q + 2, :], g.x_sb[:, 2 * q:2 * q + 2, :]).then_inc(stored, 16)
            sp.wait_ge(stored, 4 * 16)


LAYER0 = (layer0_attention, layer0_convolution, layer0_experts)
LAYER1 = (layer1_attention, layer1_wkv, layer1_ffn)


def clear(nc, g):
    with nc.Block() as block:
        @block.sync
        def _(sp):
            if g.stage_sems:
                numbers = [s.num for s in g.stage_sems]
                assert numbers == list(range(numbers[0], numbers[0] + len(numbers)))
                sp.sem_clear(range(numbers[0], numbers[0] + len(numbers)))
    g.stage_sems = []


class Shared:
    pass


def build(nc, args, out):
    g = Shared()
    g.out = out
    g.stage_sems = []
    (g.x, g.ctx, g.sink, g.w_qkv, g.w_out, g.table, g.skip, g.toeplitz, g.gate_w, g.w_gu, g.w_dn, g.w_qkv1, g.w_proj1,
     g.decay, g.first, g.w_gu1, g.w_dn1) = args
    with ExitStack() as ctx:
        def sb(name, shape, dt=F32):
            return whole(ctx.enter_context(nc.sbuf_tensor(name, shape, dt)), shape)

        def sem(name):
            return ctx.enter_context(nc.semaphore(name))

        g.ps = ctx.enter_context(nc.psum_tensor("ps", [P, 8, 512], F32))
        g.x_sb = sb("x_sb", [P, B, D])
        g.xn = sb("xn", [P, B, D])
        g.xnT = sb("xnT", [P, KD, B * S])
        g.ctxT = sb("ctxT", [P, KD, B * S])
        g.big_w = sb("big_w", [P, KD * QKV + PAIRS * D])
        g.const = sb("const", [P, C_END])
        g.ident = g.const[:, C_ID:C_ID + P]
        masks = sb("masks", [P, 3, P], BF16)
        g.ident_bf, g.swa_bf, g.causal_bf = (masks[:, i, :] for i in range(3))
        g.neg_half = sb("neg_half", [P, 8])
        g.half_ready = sem("half_ready")
        g.ln = LayerNorm(nc, g, ctx)

        GU, DN = KD * 1024, 4 * D
        at = 0
        g.base_gu = g.big_w[:, at:at + GU].rearrange("p (k n) -> p k n", k=KD)
        at += GU
        g.base_dn = g.big_w[:, at:at + DN].rearrange("p (f n) -> p f n", f=4)
        at += DN
        g.wqkv1_raw = g.big_w[:, at:at + KD * 3 * D].rearrange("p (k n) -> p k n", k=KD)
        at += KD * 3 * D
        g.wproj1_raw = g.big_w[:, at:at + KD * D].rearrange("p (k n) -> p k n", k=KD)
        at += KD * D
        g.expert_back = g.big_w[:, at:at + TOP * B * D].rearrange("p (r b n) -> p r b n", r=TOP, b=B)
        g.base_in, g.ex_in, g.slots_clear = sem("base_in"), sem("ex_in"), sem("slots_clear")
        g.wqkv1, g.wproj1 = sb("wqkv1", [P, KD, 3 * D], BF16), sb("wproj1", [P, KD, D], BF16)
        g.wmean = sb("wmean", [P, 2])
        g.wqkv1_in, g.wproj1_in = sem("wqkv1_in"), sem("wproj1_in")
        g.ffn_gu_in, g.ffn_dn_in = sem("ffn_gu_in"), sem("ffn_dn_in")
        g.slots_x = nc.dram_tensor("slots_x", (TILES * P, D), F32, kind="Internal").ap()
        g.slots_y = nc.dram_tensor("slots_y", (TILES * P, D), F32, kind="Internal").ap()
        with ExitStack() as experts:
            g.ex_gu = whole(experts.enter_context(nc.sbuf_tensor("ex_gu", [P, NE, KD, 1024], F32)), [P, NE, KD, 1024])
            g.ex_dn = whole(experts.enter_context(nc.sbuf_tensor("ex_dn", [P, NE, 4, D], F32)), [P, NE, 4, D])
            for stage in LAYER0:
                stage(nc, g)
                if stage is layer0_attention:
                    clear(nc, g)
        g.ffn_gu, g.ffn_dn = sb("ffn_gu", [P, KD, 2048]), sb("ffn_dn", [P, 8, D])
        for stage in LAYER1:
            stage(nc, g)


def kernel(**inputs):
    import concourse.bacc as _bacc
    from concourse import mybir as _mybir
    from concourse.bass_utils import run_bass_kernel_spmd as _run

    f = {k: np.ascontiguousarray(v) for k, v in inputs.items()}
    k = np.concatenate([np.zeros((16, P), np.float32), f["L0_xattn_k"]], axis=1)
    toeplitz = np.ascontiguousarray(k[:, P + np.arange(2 * P)[None, :] - np.arange(P)[:, None]])
    arrays = {
        "x": f["x"], "ctx": f["ctx_2048"], "sink": f["L0_attn_s"],
        "w_qkv": f["L0_attn_W_qkv"], "w_out": f["L0_attn_W_out"], "table": constants(),
        "skip": f["fside_S2_0"], "toeplitz": toeplitz, "gate_w": f["L0_ffn_gate_w"],
        "w_gu": np.concatenate([f["L0_ffn_expert_gate_up"], f["L0_ffn_base_gate_up"][None]]),
        "w_dn": np.concatenate([f["L0_ffn_expert_down"], f["L0_ffn_base_down"][None]]),
        "w_qkv1": np.ascontiguousarray(f["L1_attn_w_qkv"].T), "w_proj1": np.ascontiguousarray(f["L1_attn_w_proj"].T),
        "decay": f["L1_xattn_time_decay"], "first": f["L1_xattn_time_first"],
        "w_gu1": np.ascontiguousarray(f["L1_ffn_w_gate_up"].T), "w_dn1": np.ascontiguousarray(f["L1_ffn_w_down"].T),
    }
    nc = _bacc.Bacc("TRN2", target_bir_lowering=False, num_devices=1)
    args = [nc.dram_tensor(f"in_{n}_dram", a.shape, _mybir.dt.from_np(a.dtype), kind="ExternalInput").ap()
            for n, a in arrays.items()]
    out = nc.dram_tensor("out_0_dram", (B, S, D), F32, kind="ExternalOutput").ap()
    build(nc, args, out)
    r = _run(nc, [{f"in_{n}_dram": a for n, a in arrays.items()}], core_ids=[0])
    return r.results[0]["out_0_dram"]
```

```python
import numpy as np
from contextlib import ExitStack

import concourse.bass as bass
from concourse import mybir

F32 = mybir.dt.float32
BF16 = mybir.dt.bfloat16
F32R = mybir.dt.float32r
ALU = mybir.AluOpType
ACT = mybir.ActivationFunctionType
AX = mybir.AxisListType

P = 128
B, S, D = 8, 128, 256
KD = D // P
LN_EPS = 1e-5
MASKED = -1e30

NE, TOP = 8, 2
TILES = B * S * TOP // P + NE - 1

NQ, NKV, HD, WINDOW = 32, 8, 64, 64
QM = NQ // NKV
ROT = HD // 4
QKV = (NQ + 2 * NKV) * HD
CH = 512
QCH = NQ * HD // CH
PAIRS = NQ // 2
UNITS = 4
HU = NQ // UNITS

C_ID, C_SWA, C_CAUSAL, C_ROPE, C_LOWER, C_EARLIER, C_ONES, C_COUNT, C_END = 0, 128, 256, 384, 416, 480, 608, 736, 768


def constants():
    t = np.zeros((P, C_END), np.float32)
    q, k = np.arange(S)[:, None], np.arange(S)[None, :]
    t[:, C_ID:C_ID + P] = np.eye(P)
    t[:, C_SWA:C_SWA + S] = np.where((q >= k) & (q < k + WINDOW), MASKED, 0.0)
    t[:, C_CAUSAL:C_CAUSAL + S] = np.where(q >= k, 0.0, MASKED)
    freq = np.float32(1 / 1024) ** np.linspace(0, 1, ROT, dtype=np.float32)
    theta = np.arange(S, dtype=np.float32)[:, None] * freq[None, :]
    t[:, C_ROPE:C_ROPE + ROT] = np.cos(theta)
    t[:, C_ROPE + ROT:C_ROPE + 2 * ROT] = np.sin(theta)
    e = np.arange(8)
    t[:, C_LOWER:C_LOWER + 64] = (e[None, :] < e[:, None]).astype(np.float32).reshape(1, 64)
    t[:, C_EARLIER:C_EARLIER + S] = q < k
    t[:, C_ONES:C_ONES + S] = 1.0
    t[:, C_COUNT:C_COUNT + 32] = np.arange(32)
    return t


def whole(tensor, shape):
    return tensor[tuple(slice(None) for _ in shape)]


def layer0_attention(nc, g):
    with ExitStack() as ctx:
        def sb(name, shape, dt=F32):
            return whole(ctx.enter_context(nc.sbuf_tensor(name, shape, dt)), shape)

        def sem(name):
            g.stage_sems.append(ctx.enter_context(nc.semaphore(name)))
            return g.stage_sems[-1]

        PIECES, SLOTS, WIDE = QCH + 2 + 4, 4, KD * CH
        raw = g.toep.rearrange("p (s h) n -> p s (h n)", s=SLOTS)
        wqkv_hi, wqkv_lo = sb("a_wqkv_hi", [P, QCH + 2, KD, CH], F32R), sb("a_wqkv_lo", [P, QCH + 2, KD, CH], F32R)
        wout_hi, wout_lo = sb("a_wout_hi", [P, PAIRS, D], F32R), sb("a_wout_lo", [P, PAIRS, D], F32R)
        xn = sb("a_xn", [P, D])
        xT_hi, xT_lo = sb("a_xT_hi", [P, KD, S], F32R), sb("a_xT_lo", [P, KD, S], F32R)
        qk_tok = sb("a_qk_tok", [P, (NQ + 2 * NKV) * HD])
        v_tok = sb("a_v_tok", [P, NKV * HD])
        qT = g.xnT.rearrange("p k (t s) -> p (k t) s", t=PAIRS // KD)
        kT = sb("a_kT", [P, NKV, S])
        prob = sb("a_prob", [P, 2, HU, S])
        rot_a = sb("a_rot_a", [P, 2, 8, 2, ROT])
        rot_b = sb("a_rot_b", [P, 2, 8, 2, ROT])
        probT = sb("a_probT", [P, 2, 2, 4 * S])
        oT_hi, oT_lo = sb("a_oT_hi", [P, PAIRS, S], F32R), sb("a_oT_lo", [P, PAIRS, S], F32R)
        sink8 = sb("a_sink8", [P, UNITS, HU])
        rmax = sb("a_rmax", [P, 2, HU])
        rowm = sb("a_rowm", [P, 2, HU])
        sinke = sb("a_sinke", [P, 2, HU])
        psum_p = sb("a_psum_p", [P, 2, HU])
        den = sb("a_den", [P, 2, HU])
        rden = sb("a_rden", [P, 2, HU])
        stats = sb("a_stats", [P, B, 6])
        mv = sb("a_mv", [P, B, 2])
        veps = sb("a_veps", [P, B])
        rstd = sb("a_rstd", [P, B, 1])
        sink_raw = sb("a_sink_raw", [P, NQ])
        ctx_tok = g.xn

        const_in, x_in, ctx_in, sink_in = sem("const_in"), sem("x_in"), sem("ctx_in"), sem("sink_in")
        raw_in = [sem(f"raw_in{i}") for i in range(SLOTS)]
        w_hi_done, w_split = sem("w_hi_done"), sem("w_split")
        xT_hi_done, oT_hi_done = sem("xT_hi_done"), sem("oT_hi_done")
        masks_ready, sink_ready = sem("masks_ready"), sem("sink_ready")
        stats_done, mv_done, veps_done, rstd_done = sem("stats_done"), sem("mv_done"), sem("veps_done"), sem("rstd_done")
        ctxT_mm, ctxT_out = sem("ctxT_mm"), sem("ctxT_out")
        xn_ready, xT_mm, xT_split = sem("a_xn_ready"), sem("a_xT_mm"), sem("a_xT_split")
        proj_mm = sem("proj_mm")
        turned = sem("turned")
        straight = sem("straight")
        rope_done = sem("rope_done")
        v_ready = sem("v_ready")
        qkT_mm, qkT_ready = sem("qkT_mm"), sem("qkT_ready")
        score_mm, rmax_done, rowm_done, shifted, sinkd = (
            sem("score_mm"), sem("rmax_done"), sem("rowm_done"), sem("shifted"), sem("sinkd"))
        exp_done, sum_done, den_done, rden_done, prob_ready = (
            sem("exp_done"), sem("sum_done"), sem("den_done"), sem("rden_done"), sem("prob_ready"))
        probT_mm, probT_ready, av_mm, oT_split, y_mm, x_added = (
            sem("probT_mm"), sem("probT_ready"), sem("av_mm"), sem("oT_split"), sem("y_mm"), sem("x_added"))

        ps = g.ps
        S_BANK, PT_BANK, O_BANK, M_BANK = 0, 4, 6, 7
        NCH = QCH + 2
        TURNED = ("k0", "q0", "q1", "q2", "k1", "q3")
        NT = len(TURNED)

        def column(c):
            return QCH * CH if c == 0 else (c - 1) * CH if c <= QCH else c * CH

        def chunk_copies(c):
            if c > 0:
                return [qk_tok[:, (c - 1) * CH:c * CH].rearrange("p (h a r) -> p h a r", h=8, a=2)]
            k = qk_tok[:, QCH * CH:].rearrange("p (h d a r) -> p h d a r", h=NKV, d=2, a=2)
            return [k[:, :, 0], k[:, :, 1]]

        def chunk_bank(c):
            return PT_BANK + 1 if c in (0, 3) else M_BANK

        def turned_bank(t):
            return S_BANK + (t if t < 4 else t - 2)

        def scores(slot):
            return ps[:, S_BANK + 2 * slot:S_BANK + 2 * slot + 2, :]

        block = ctx.enter_context(nc.Block())

        @block.sync
        def _(sp):
            sp.dma_start(g.x_sb[:, :, :], g.x.rearrange("b s d -> s b d")).then_inc(x_in, 16)
            sp.dma_start(g.const[:, :], g.table[:, :]).then_inc(const_in, 16)
            src = g.w_qkv.rearrange("(k p) n -> p k n", k=KD)
            for i in range(PIECES):
                slot = raw[:, i % SLOTS, :]
                if i >= SLOTS:
                    sp.wait_ge(w_split, i - SLOTS + 1)
                if i < NCH:
                    sp.dma_start(slot.rearrange("p (k n) -> p k n", k=KD), src[:, :, column(i):column(i) + CH]).then_inc(raw_in[i % SLOTS], 16)
                else:
                    t = 4 * (i - NCH)
                    sp.dma_start(slot.rearrange("p (t n) -> p t n", t=4),
                                 g.w_out.rearrange("(t p) n -> p t n", t=PAIRS)[:, t:t + 4, :]).then_inc(raw_in[i % SLOTS], 16)

            sp.wait_ge(w_split, PIECES)
            sp.dma_start(g.toep, g.toeplitz.rearrange("h m l -> m h l")).then_inc(g.toep_in, 16)

        def piece(i):
            if i < NCH:
                hi, lo = (t[:, i].rearrange("p k n -> p (k n)") for t in (wqkv_hi, wqkv_lo))
            else:
                hi, lo = (t[:, 4 * (i - NCH):4 * (i - NCH) + 4].rearrange("p t n -> p (t n)") for t in (wout_hi, wout_lo))
            return hi, lo, raw[:, i % SLOTS, :]

        @block.gpsimd
        def _(pool):
            def rope_add(c, n):
                pool.wait_ge(turned, n + 1)
                for dst in chunk_copies(c):
                    add = nc.gpsimd.tensor_tensor(dst[:, :, :, 0:ROT], rot_a[:, c % 2], rot_b[:, c % 2], ALU.add)
                add.then_inc(rope_done, 1)

            def normalise(u, n):
                pool.wait_ge(rden_done, n + 1)
                nc.gpsimd.tensor_tensor(prob[:, u % 2], prob[:, u % 2],
                                        rden[:, u % 2, :].unsqueeze(2).to_broadcast([P, HU, S]),
                                        ALU.mult).then_inc(prob_ready, 1)

            def body(b, has_next):
                for step in "R0 R1 D2 R2 R3 D3 R4 N0 N1".split():
                    k = int(step[1])
                    if step[0] == "D":
                        normalise(k, UNITS * b + k)
                    elif has_next and step[0] == "R":
                        rope_add(k, (QCH + 1) * (b + 1) + k)
                    elif has_next:
                        normalise(k, UNITS * (b + 1) + k)

            pool.wait_ge(mv_done, B)
            nc.gpsimd.tensor_scalar_add(veps[:, :], mv[:, :, 1], LN_EPS).then_inc(veps_done, 1)
            pool.wait_ge(veps_done, 1)
            pool.wait_ge(g.half_ready, 1)
            nc.gpsimd.tensor_tensor(rstd[:, :, 0], veps[:, :], g.neg_half[:, 0:B], ALU.pow).then_inc(rstd_done, 1)
            for c in range(QCH + 1):
                rope_add(c, c)
            for u in range(2):
                normalise(u, u)
            with pool.Fori(0, B - 1) as b:
                body(b, True)
            body(B - 1, False)

        @block.scalar
        def _(act):
            act.dma_start(ctx_tok[:, :, :], g.ctx.rearrange("b s d -> s b d")).then_inc(ctx_in, 16)
            act.dma_start(sink_raw[:, :], g.sink.rearrange("a g m -> a (g m)").to_broadcast([P, NQ])).then_inc(sink_in, 16)

            def weights_high(i):
                hi, _, whole_piece = piece(i)
                act.wait_ge(raw_in[i % SLOTS], 16 * (i // SLOTS + 1))
                nc.scalar.copy(hi, whole_piece).then_inc(w_hi_done, 1)

            def xT_out(b):
                act.wait_ge(xT_mm, b + 1)
                nc.scalar.copy(xT_hi[:, :, :], ps[:, O_BANK, 0:KD * S].rearrange("p (k s) -> p k s", k=KD)).then_inc(xT_hi_done, 1)

            def straight_out(c, n):
                act.wait_ge(turned, (QCH + 1) * n + c + 1)
                bank = ps[:, chunk_bank(c), :].rearrange("p (h a r) -> p h a r", h=8, a=2)
                for dst in chunk_copies(c):
                    copy = nc.scalar.copy(dst[:, :, :, ROT:2 * ROT], bank[:, :, :, ROT:2 * ROT])
                copy.then_inc(straight, 1)

            def v_out(n):
                act.wait_ge(proj_mm, NCH * n + NCH)
                nc.scalar.copy(v_tok[:, :], ps[:, M_BANK, :]).then_inc(v_ready, 1)

            def qkT_out(t, n):
                act.wait_ge(qkT_mm, NT * n + t + 1)
                at = 4 * int(TURNED[t][1])
                dst = (qT if TURNED[t][0] == "q" else kT)[:, at:at + 4, :]
                nc.scalar.copy(dst, ps[:, turned_bank(t), :].rearrange("p (t s) -> p t s", t=4)).then_inc(qkT_ready, 1)

            def exps(u, n):
                act.wait_ge(shifted, n + 1)
                nc.scalar.activation(prob[:, u % 2], prob[:, u % 2], ACT.Exp, scale=HD ** -0.5).then_inc(exp_done, 1)
                act.wait_ge(sinkd, n + 1)
                nc.scalar.activation(sinke[:, u % 2], sinke[:, u % 2], ACT.Exp, scale=HD ** -0.5).then_inc(exp_done, 1)

            def probT_out(u, n):
                for p in range(2):
                    act.wait_ge(probT_mm, 2 * n + p + 1)
                    nc.scalar.copy(probT[:, u % 2, p, :], ps[:, PT_BANK + p, :]).then_inc(probT_ready, 1)

            def oT_out(u, n):
                act.wait_ge(av_mm, n + 1)
                nc.scalar.copy(oT_hi[:, 4 * u:4 * u + 4, :], ps[:, O_BANK, :].rearrange("p (t s) -> p t s", t=4)).then_inc(oT_hi_done, 1)

            def body(b, has_next):
                steps = "P0 x e2 n0 n1 o0 P1 e3 n2 n3 o1 P2 n4 T0 T1 T2 T3 o2 T4 T5 P3 o3 v E0 E1"
                for step in steps.split():
                    k = int(step[1]) if len(step) > 1 else 0
                    if step[0] == "e":
                        exps(k, UNITS * b + k)
                    elif step[0] == "P":
                        probT_out(k, UNITS * b + k)
                    elif step[0] == "o":
                        oT_out(k, UNITS * b + k)
                    elif has_next:
                        if step[0] == "x":
                            xT_out(b + 1)
                        elif step[0] == "n":
                            straight_out(k, b + 1)
                        elif step[0] == "T":
                            qkT_out(k, b + 1)
                        elif step[0] == "E":
                            exps(k, UNITS * (b + 1) + k)
                        else:
                            v_out(b + 1)

            weights_high(0)
            weights_high(1)
            xT_out(0)
            weights_high(2)
            weights_high(3)
            for h in range(4):
                act.wait_ge(ctxT_mm, h + 1)
                nc.scalar.copy(g.ctxT[:, :, 2 * h * S:2 * (h + 1) * S],
                               ps[:, h, :].rearrange("p (k s) -> p k s", k=KD)).then_inc(ctxT_out, 1)
            weights_high(4)
            for c in range(2):
                straight_out(c, 0)
            weights_high(5)
            for c in range(2, QCH + 1):
                straight_out(c, 0)
            v_out(0)
            for t in range(NT):
                qkT_out(t, 0)
            for u in range(2):
                weights_high(NCH + 2 * u)
                weights_high(NCH + 2 * u + 1)
                exps(u, u)
            with act.Fori(0, B - 1) as b:
                body(b, True)
            body(B - 1, False)

        @block.tensor
        def _(pe):
            def turn_x(b):
                pe.wait_ge(xn_ready, b + 1)
                for k in range(KD):
                    mm = nc.tensor.transpose(ps[:, O_BANK, k * S:(k + 1) * S], xn[:, k * P:(k + 1) * P], g.ident)
                mm.then_inc(xT_mm, 1)

            def project(c, n, first=False):
                if first:
                    pe.wait_ge(w_split, c + 1)
                if c == 0:
                    pe.wait_ge(xT_split, n + 1)
                elif c == 1 and not first:
                    pe.wait_ge(x_added, n - 1)
                elif c in (2, 4, 5):
                    pe.wait_ge(straight, (QCH + 1) * n + {2: 1, 4: 2, 5: 4}[c] + 1)
                if not first and c in (0, 3):
                    pe.wait_ge(probT_ready, 2 * (UNITS * (n - 1) + c // 3) + 2)
                terms = [(x[:, k], w[:, c, k]) for k in range(KD)
                         for x, w in ((xT_hi, wqkv_hi), (xT_hi, wqkv_lo), (xT_lo, wqkv_hi))]
                for i, (x, w) in enumerate(terms):
                    mm = nc.tensor.matmul(ps[:, chunk_bank(c), :], x, w, start=(i == 0), stop=(i == len(terms) - 1))
                mm.then_inc(proj_mm, 1)

            def turn_qk(t, n):
                kind, i0 = TURNED[t][0], int(TURNED[t][1])
                chunk = i0 + 1 if kind == "q" else 0
                pe.wait_ge(rope_done, (QCH + 1) * n + chunk + 1)
                pe.wait_ge(straight, (QCH + 1) * n + chunk + 1)
                if t >= 4:
                    pe.wait_ge(qkT_ready, NT * n + t - 1)
                for i in range(4):
                    tile = 4 * i0 + i if kind == "q" else PAIRS + 4 * i0 + i
                    mm = nc.tensor.transpose(ps[:, turned_bank(t), i * S:(i + 1) * S],
                                             qk_tok[:, tile * P:(tile + 1) * P], g.ident)
                mm.then_inc(qkT_mm, 1)

            def score(u, b):
                if u < 2:
                    pe.wait_ge(qkT_ready, NT * b + (2 if u == 0 else NT))
                else:
                    pe.wait_ge(shifted, UNITS * b + u - 1)
                for p in range(2):
                    nc.tensor.matmul(ps[:, S_BANK + 2 * (u % 2) + p, :], g.ident_bf,
                                     g.swa_bf.unsqueeze(1).to_broadcast([P, 4, S]), start=True, stop=False,
                                     skip_group_check=True)
                for i in range(4):
                    for p in range(2):
                        mm = nc.tensor.matmul(ps[:, S_BANK + 2 * (u % 2) + p, i * S:(i + 1) * S],
                                              qT[HD * p:HD * (p + 1), 4 * u + i, :],
                                              kT[HD * p:HD * (p + 1), 2 * u + i // 2, :],
                                              start=False, stop=True, skip_group_check=True)
                mm.then_inc(score_mm, 1)

            def turn_prob(u, n, first, b, has_next):
                pe.wait_ge(prob_ready, n + 1)
                if not first:
                    pe.wait_ge(probT_ready, 2 * n)
                for p in range(2):
                    if p == 1 and has_next and u in (1, 2):
                        pe.wait_ge(straight, (QCH + 1) * (b + 1) + (1 if u == 1 else 4))
                    for i in range(4):
                        mm = nc.tensor.transpose(ps[:, PT_BANK + p, i * S:(i + 1) * S], prob[:, u % 2, 4 * p + i, :], g.ident)
                    mm.then_inc(probT_mm, 1)

            def attend(u, n, b, first):
                pe.wait_ge(probT_ready, 2 * n + 2)
                if u == 0:
                    pe.wait_ge(v_ready, b + 1)
                if not first:
                    pe.wait_ge(oT_split, n)
                for kv in range(2):
                    for p in range(2):
                        mm = nc.tensor.matmul(ps[HD * p:HD * (p + 1), O_BANK, kv * 2 * S:(kv + 1) * 2 * S],
                                              v_tok[:, (2 * u + kv) * HD:(2 * u + kv + 1) * HD],
                                              probT[:, u % 2, p, kv * 2 * S:(kv + 1) * 2 * S], start=True, stop=True,
                                              skip_group_check=True)
                mm.then_inc(av_mm, 1)

            def output(b):
                pe.wait_ge(oT_split, UNITS * (b + 1))
                pe.wait_ge(w_split, PIECES)
                terms = [(o[:, t], w[:, t]) for t in range(PAIRS)
                         for o, w in ((oT_hi, wout_hi), (oT_hi, wout_lo), (oT_lo, wout_hi))]
                for i, (o, w) in enumerate(terms):
                    mm = nc.tensor.matmul(ps[:, M_BANK, 0:D], o, w, start=(i == 0), stop=(i == len(terms) - 1))
                mm.then_inc(y_mm, 1)

            def body(b, has_next, first):
                steps = "P0 x S2 c0 c1 A0 P1 S3 c2 c3 A1 c4 P2 T0 T1 T2 T3 A2 T4 T5 P3 N0 A3 c5 N1 Y"
                for step in steps.split():
                    k = int(step[1]) if len(step) > 1 else 0
                    n = UNITS * b + k
                    if step[0] == "S":
                        score(k, b)
                    elif step[0] == "P":
                        turn_prob(k, n, first and k == 0, b, has_next)
                    elif step[0] == "A":
                        attend(k, n, b, first and k == 0)
                    elif step[0] == "Y":
                        if has_next:
                            pe.wait_ge(v_ready, b + 2)
                        else:
                            pe.wait_ge(x_added, b)
                        output(b)
                    elif has_next:
                        if step[0] == "x":
                            turn_x(b + 1)
                        elif step[0] == "c":
                            project(k, b + 1)
                        elif step[0] == "N":
                            score(k, b + 1)
                        elif step[0] == "T":
                            if k == 0:
                                pe.wait_ge(shifted, UNITS * b + 3)
                            if k == 2:
                                pe.wait_ge(shifted, UNITS * b + 4)
                            turn_qk(k, b + 1)

            pe.wait_ge(const_in, 16)
            pe.wait_ge(ctx_in, 16)
            for h in range(4):
                for k in range(KD):
                    for j in range(2):
                        mm = nc.tensor.transpose(ps[:, h, (2 * k + j) * S:(2 * k + j + 1) * S],
                                                 ctx_tok[:, 2 * h + j, k * P:(k + 1) * P], g.ident)
                mm.then_inc(ctxT_mm, 1)
            turn_x(0)
            for c in range(NCH):
                project(c, 0, first=True)
            pe.wait_ge(ctxT_out, 4)
            for t in range(NT):
                turn_qk(t, 0)
            pe.wait_ge(masks_ready, 3)
            for u in range(2):
                score(u, 0)
            body(0, True, True)
            with pe.Fori(1, B - 1) as b:
                body(b, True, False)
            body(B - 1, False, False)

        @block.vector
        def _(dve):
            def normalise(b):
                nc.vector.tensor_scalar(xn[:, :], g.x_sb[:, b, :], mv[:, b, 0:1], rstd[:, b, :],
                                        ALU.subtract, ALU.mult).then_inc(xn_ready, 1)

            cos = g.const[:, C_ROPE:C_ROPE + ROT]
            sin = g.const[:, C_ROPE + ROT:C_ROPE + 2 * ROT]

            def turn(c, n, first=False):
                dve.wait_ge(proj_mm, NCH * n + c + 1)
                if not (first and c < 2):
                    dve.wait_ge(rope_done, (QCH + 1) * n + c - 1)
                s = c % 2
                bank = ps[:, chunk_bank(c), :].rearrange("p (h a r) -> p h a r", h=8, a=2)[:, :, :, 0:ROT]
                nc.vector.tensor_tensor(rot_a[:, s], bank,
                                        cos.unsqueeze(1).unsqueeze(1).to_broadcast([P, 8, 2, ROT]), ALU.mult)
                wide = sin.unsqueeze(1).to_broadcast([P, 8, ROT])
                nc.vector.tensor_tensor(rot_b[:, s, :, 0, :], bank[:, :, 1, :], wide, ALU.mult)
                nc.vector.scalar_tensor_tensor(out=rot_b[:, s, :, 1, :], in0=bank[:, :, 0, :], scalar=-1.0, in1=wide,
                                               op0=ALU.mult, op1=ALU.mult).then_inc(turned, 1)

            def shift(u, n):
                s = u % 2
                dve.wait_ge(score_mm, n + 1)
                nc.vector.tensor_reduce(rmax[:, s, :], scores(s).rearrange("p c (i k) -> p (c i) k", i=4),
                                        AX.X, ALU.max).then_inc(rmax_done, 1)
                dve.wait_ge(rmax_done, n + 1)
                nc.vector.tensor_tensor(rowm[:, s, :], rmax[:, s, :], sink8[:, u, :], ALU.max).then_inc(rowm_done, 1)
                dve.wait_ge(rowm_done, n + 1)
                nc.vector.tensor_tensor(prob[:, s], scores(s).rearrange("p c (i k) -> p (c i) k", i=4),
                                        rowm[:, s, :].unsqueeze(2).to_broadcast([P, HU, S]), ALU.subtract).then_inc(shifted, 1)
                nc.vector.tensor_tensor(sinke[:, s, :], sink8[:, u, :], rowm[:, s, :], ALU.subtract).then_inc(sinkd, 1)

            def total(u, n):
                s = u % 2
                dve.wait_ge(exp_done, 2 * n + 2)
                nc.vector.tensor_reduce(psum_p[:, s, :], prob[:, s], AX.X, ALU.add).then_inc(sum_done, 1)
                dve.wait_ge(sum_done, n + 1)
                nc.vector.tensor_tensor(den[:, s, :], psum_p[:, s, :], sinke[:, s, :], ALU.add).then_inc(den_done, 1)
                dve.wait_ge(den_done, n + 1)
                nc.vector.reciprocal(rden[:, s, :], den[:, s, :]).then_inc(rden_done, 1)

            def add(b):
                dve.wait_ge(y_mm, b + 1)
                nc.vector.tensor_tensor(g.x_sb[:, b, :], g.x_sb[:, b, :], ps[:, M_BANK, 0:D], ALU.add).then_inc(x_added, 1)

            def weights_low(i):
                hi, lo, whole_piece = piece(i)
                dve.wait_ge(w_hi_done, i + 1)
                nc.vector.tensor_tensor(lo, whole_piece, hi, ALU.subtract).then_inc(w_split, 1)

            def xT_low(b):
                dve.wait_ge(xT_hi_done, b + 1)
                nc.vector.tensor_tensor(xT_lo[:, :, :], ps[:, O_BANK, 0:KD * S].rearrange("p (k s) -> p k s", k=KD), xT_hi[:, :, :],
                                        ALU.subtract).then_inc(xT_split, 1)

            def oT_low(u, n):
                dve.wait_ge(oT_hi_done, n + 1)
                nc.vector.tensor_tensor(oT_lo[:, 4 * u:4 * u + 4, :], ps[:, O_BANK, :].rearrange("p (t s) -> p t s", t=4),
                                        oT_hi[:, 4 * u:4 * u + 4, :], ALU.subtract).then_inc(oT_split, 1)

            def body(b, has_next, first):
                steps = "x Y L D1 S2 R0 R1 D2 o0 S3 R2 R3 D3 o1 R4 o2 N0 o3 M0 N1"
                for step in steps.split():
                    k = int(step[1]) if len(step) > 1 else 0
                    n = UNITS * b + k
                    if step[0] == "S":
                        shift(k, n)
                    elif step[0] == "D":
                        total(k, n)
                    elif step[0] == "Y":
                        if not first:
                            add(b - 1)
                    elif step[0] == "o":
                        oT_low(k, n)
                    elif has_next:
                        if step[0] == "x":
                            normalise(b + 1)
                        elif step[0] == "L":
                            xT_low(b + 1)
                        elif step[0] == "N":
                            shift(k, UNITS * (b + 1) + k)
                        elif step[0] == "M":
                            total(k, UNITS * (b + 1) + k)
                        else:
                            turn(k, b + 1)

            nc.vector.memset(g.neg_half[:, :], -0.5).then_inc(g.half_ready, 1)
            dve.wait_ge(x_in, 16)
            for b in range(B):
                nc.vector.bn_stats(stats[:, b, :], g.x_sb[:, b, :]).then_inc(stats_done, 1)
            for b in range(B):
                dve.wait_ge(stats_done, b + 1)
                nc.vector.bn_aggr(mv[:, b, :], stats[:, b, :]).then_inc(mv_done, 1)
            dve.wait_ge(const_in, 16)
            nc.vector.tensor_copy(g.ident_bf, g.const[:, C_ID:C_ID + P]).then_inc(masks_ready, 1)
            nc.vector.tensor_copy(g.swa_bf, g.const[:, C_SWA:C_SWA + P]).then_inc(masks_ready, 1)
            nc.vector.tensor_copy(g.causal_bf, g.const[:, C_CAUSAL:C_CAUSAL + P]).then_inc(masks_ready, 1)
            dve.wait_ge(sink_in, 16)
            nc.vector.tensor_scalar(sink8.rearrange("p u (a v j) -> p u a v j", a=2, v=2)[:, :, 0],
                                    sink_raw.rearrange("p (u v j a) -> p u v j a", u=UNITS, v=2, j=2)[:, :, :, :, 0],
                                    HD ** 0.5, None, ALU.mult)
            nc.vector.tensor_scalar(sink8.rearrange("p u (a v j) -> p u a v j", a=2, v=2)[:, :, 1],
                                    sink_raw.rearrange("p (u v j a) -> p u v j a", u=UNITS, v=2, j=2)[:, :, :, :, 1],
                                    HD ** 0.5, None, ALU.mult).then_inc(sink_ready, 1)
            dve.wait_ge(rstd_done, 1)
            normalise(0)
            weights_low(0)
            weights_low(1)
            xT_low(0)
            weights_low(2)
            weights_low(3)
            for c in range(QCH + 1):
                turn(c, 0, first=True)
                if c == 1:
                    weights_low(4)
                    weights_low(5)
            dve.wait_ge(sink_ready, 1)
            shift(0, 0)
            weights_low(NCH)
            weights_low(NCH + 1)
            total(0, 0)
            shift(1, 1)
            weights_low(NCH + 2)
            weights_low(NCH + 3)
            body(0, True, True)
            with dve.Fori(1, B - 1) as b:
                body(b, True, False)
            body(B - 1, False, False)
            add(B - 1)



class LayerNorm:

    def __init__(self, nc, g, ctx):
        self.nc, self.g = nc, g
        self.stats = ctx.enter_context(nc.sbuf_tensor("ln_stats", [P, B, 6], F32))
        self.mv = ctx.enter_context(nc.sbuf_tensor("ln_mv", [P, B, 2], F32))
        self.veps = ctx.enter_context(nc.sbuf_tensor("ln_veps", [P, B], F32))
        self.rstd = ctx.enter_context(nc.sbuf_tensor("ln_rstd", [P, B, 1], F32))
        self.stats_done = ctx.enter_context(nc.semaphore("ln_stats_done"))
        self.mv_done = ctx.enter_context(nc.semaphore("ln_mv_done"))
        self.veps_done = ctx.enter_context(nc.semaphore("ln_veps_done"))
        self.rstd_done = ctx.enter_context(nc.semaphore("ln_rstd_done"))
        self.xn_ready = ctx.enter_context(nc.semaphore("ln_xn_ready"))
        self.turned_mm = ctx.enter_context(nc.semaphore("ln_turned_mm"))
        self.turned_out = ctx.enter_context(nc.semaphore("ln_turned_out"))

    def vector(self, dve, r):
        nc, g = self.nc, self.g
        for b in range(B):
            nc.vector.bn_stats(self.stats[:, b, :], g.x_sb[:, b, :]).then_inc(self.stats_done, 1)
        for b in range(B):
            dve.wait_ge(self.stats_done, B * r + b + 1)
            nc.vector.bn_aggr(self.mv[:, b, :], self.stats[:, b, :]).then_inc(self.mv_done, 1)
        dve.wait_ge(self.rstd_done, r + 1)
        for b in range(B):
            nc.vector.tensor_scalar(g.xn[:, b, :], g.x_sb[:, b, :], self.mv[:, b, 0:1], self.rstd[:, b, :],
                                    ALU.subtract, ALU.mult).then_inc(self.xn_ready, 1)

    def gpsimd(self, pool, r):
        nc, g = self.nc, self.g
        pool.wait_ge(self.mv_done, B * (r + 1))
        nc.gpsimd.tensor_scalar_add(self.veps[:, :], self.mv[:, :, 1], LN_EPS).then_inc(self.veps_done, 1)
        pool.wait_ge(self.veps_done, r + 1)
        nc.gpsimd.tensor_tensor(self.rstd[:, :, 0], self.veps[:, :], g.neg_half[:, 0:B], ALU.pow).then_inc(self.rstd_done, 1)

    def tensor(self, pe, r):
        nc, g = self.nc, self.g
        for h in range(B // 2):
            pe.wait_ge(self.xn_ready, B * r + 2 * h + 2)
            for k in range(KD):
                for j in range(2):
                    mm = nc.tensor.transpose(g.ps[:, h, (2 * k + j) * S:(2 * k + j + 1) * S],
                                             g.xn[:, 2 * h + j, k * P:(k + 1) * P], g.ident)
            mm.then_inc(self.turned_mm, 1)

    def scalar(self, act, r, dst):
        nc, g = self.nc, self.g
        for h in range(B // 2):
            act.wait_ge(self.turned_mm, B // 2 * r + h + 1)
            nc.scalar.copy(dst(h), g.ps[:, h, :].rearrange("p (k j s) -> p k j s", k=KD, j=2)).then_inc(self.turned_out, 1)

    def out(self, r, h=B // 2):
        return B // 2 * r + h


def pair_of(t):
    return lambda h: t[:, :, 2 * h * S:2 * (h + 1) * S].rearrange("p k (j s) -> p k j s", j=2)


NH0 = 16
NI = 8


def layer0_convolution(nc, g):
    with ExitStack() as ctx:
        def sb(name, shape, dt=F32):
            return whole(ctx.enter_context(nc.sbuf_tensor(name, shape, dt)), shape)

        def sem(name):
            return ctx.enter_context(nc.semaphore(name))

        ln = g.ln
        N = B * NI * NI
        toep = sb("b_toep", [P, 2, 2 * P])
        kv = sb("b_kv", [P, 2, KD * N])
        z = sb("b_z", [P, 2, KD * N])
        oT = sb("b_oT", [P, KD * B, P])
        skip = sb("b_skip", [P, P])
        vx = g.xn.rearrange("p b (k s) -> p (b k) s", k=KD)
        skips = sb("b_skips", [P, KD * B, NH0])
        zero = sb("b_zero", [P, D])
        zero_ready = sem("zero_ready")
        toep_ready = sem("toep_ready")
        skip_in = sem("skip_in")
        kv_ready, conv_mm, z_ready, head_out = sem("kv_ready"), sem("conv_mm"), sem("z_ready"), sem("head_out")
        vx_done, skips_done, skip_term, oT_done = sem("vx_done"), sem("skips_done"), sem("skip_term"), sem("b_oT_done")
        back_mm, back_added = sem("back_mm"), sem("back_added")

        def channels(t, h):
            return t.rearrange("p c (h i) -> p c h i", h=NH0)[:, :, h, :]

        vT = g.xnT.rearrange("p k (b s) -> p (k b) s", b=B)
        xT = g.ctxT.rearrange("p k (b s) -> p (k b) s", b=B)
        wide = [P, KD * B, NI, NI]

        block = ctx.enter_context(nc.Block())

        @block.sync
        def _(sp):
            sp.dma_start(skip[:, :], g.skip.unsqueeze(0).to_broadcast([P, P])).then_inc(skip_in, 16)
            sp.dma_start(g.base_gu, g.w_gu[NE].rearrange("(k p) n -> p k n", k=KD)).then_inc(g.base_in, 16)
            sp.dma_start(g.base_dn, g.w_dn[NE].rearrange("(f p) n -> p f n", f=4)).then_inc(g.base_in, 16)
            sp.dma_start(g.wqkv1_raw, g.w_qkv1.rearrange("(k p) n -> p k n", k=KD)).then_inc(g.wqkv1_in, 16)
            sp.dma_start(g.wproj1_raw, g.w_proj1.rearrange("(k p) n -> p k n", k=KD)).then_inc(g.wproj1_in, 16)
            sp.wait_ge(zero_ready, 1)
            sp.dma_start(g.slots_x.rearrange("(t p) d -> p t d", p=P), zero.unsqueeze(1).to_broadcast([P, TILES, D])).then_inc(g.slots_clear, 16)

        @block.gpsimd
        def _(pool):
            nc.gpsimd.memset(zero[:, :], 0.0).then_inc(zero_ready, 1)
            ln.gpsimd(pool, 0)
            pool.wait_ge(ln.turned_out, ln.out(0))

            def products(n, s, first):
                if not first:
                    pool.wait_ge(conv_mm, n - 1)
                nc.gpsimd.tensor_tensor(kv[:, s, :].rearrange("p (c i j) -> p c i j", i=NI, j=NI),
                                        channels(vT, n).unsqueeze(3).to_broadcast(wide),
                                        channels(xT, n).unsqueeze(2).to_broadcast(wide), ALU.mult).then_inc(kv_ready, 1)

            products(0, 0, True)
            products(1, 1, True)
            with pool.Fori(1, NH0 // 2) as i:
                for s in range(2):
                    products(2 * i + s, s, False)
            pool.wait_ge(skips_done, 1)
            nc.gpsimd.tensor_tensor(vx.rearrange("p c (h j) -> p c h j", h=NH0), xT.rearrange("p c (h j) -> p c h j", h=NH0),
                                    skips.unsqueeze(3).to_broadcast([P, KD * B, NH0, NI]), ALU.mult).then_inc(skip_term, 1)

        @block.tensor
        def _(pe):
            ln.tensor(pe, 0)
            pe.wait_ge(ln.turned_out, ln.out(0))

            def convolve(n, s, i, first):
                pe.wait_ge(toep_ready, n + 1)
                pe.wait_ge(kv_ready, n + 1)
                if not first:
                    pe.wait_ge(z_ready, n - 1)
                near, far = toep[:, s, 0:P], toep[:, s, P:2 * P]
                nc.tensor.matmul(g.ps[:, 2 * s, :], near, kv[:, s, 0:N], start=True, stop=True)
                nc.tensor.matmul(g.ps[:, 2 * s + 1, :], near, kv[:, s, N:2 * N], start=True, stop=False)
                nc.tensor.matmul(g.ps[:, 2 * s + 1, :], far, kv[:, s, 0:N], start=False, stop=True).then_inc(conv_mm, 1)

            convolve(0, 0, 0, True)
            convolve(1, 1, 0, True)
            with pe.Fori(1, NH0 // 2) as i:
                for s in range(2):
                    convolve(2 * i + s, s, i, False)
            pe.wait_ge(oT_done, 1)
            for h in range(B // 2):
                for j in range(2):
                    for k in range(KD):
                        mm = nc.tensor.transpose(g.ps[:, 4 + h, (2 * j + k) * P:(2 * j + k + 1) * P],
                                                 oT[:, k * B + 2 * h + j, :], g.ident)
                mm.then_inc(back_mm, 1)

        @block.scalar
        def _(act):
            for e in range(NE):
                act.dma_start(g.ex_gu[:, e], g.w_gu[e].rearrange("(k p) n -> p k n", k=KD)).then_inc(g.ex_in, 16)
                act.dma_start(g.ex_dn[:, e], g.w_dn[e].rearrange("(f p) n -> p f n", f=4)).then_inc(g.ex_in, 16)

            def filter_of(n, s, first):
                if first:
                    act.wait_ge(g.toep_in, 16)
                else:
                    act.wait_ge(conv_mm, n - 1)
                nc.scalar.copy(toep[:, s, :], g.toep[:, n, :]).then_inc(toep_ready, 1)

            filter_of(0, 0, True)
            filter_of(1, 1, True)
            ln.scalar(act, 0, pair_of(g.xnT))
            with act.Fori(1, NH0 // 2) as i:
                for s in range(2):
                    filter_of(2 * i + s, s, False)

        @block.vector
        def _(dve):
            ln.vector(dve, 0)
            dve.wait_ge(ln.turned_out, ln.out(0))
            dve.wait_ge(skip_in, 16)
            nc.vector.tensor_tensor(vx[:, :, :], vT, xT, ALU.mult).then_inc(vx_done, 1)
            dve.wait_ge(vx_done, 1)
            nc.vector.tensor_tensor(vx[:, :, :], vx[:, :, :], skip[:, :].unsqueeze(1).to_broadcast([P, KD * B, P]),
                                    ALU.mult).then_inc(vx_done, 1)
            dve.wait_ge(vx_done, 2)
            nc.vector.tensor_reduce(skips[:, :, :], vx.rearrange("p c (h i) -> p c h i", h=NH0), AX.X, ALU.add).then_inc(skips_done, 1)

            def gather(n, s):
                dve.wait_ge(conv_mm, n + 1)
                nc.vector.tensor_tensor(z[:, s, :].rearrange("p (c i j) -> p c i j", i=NI, j=NI),
                                        g.ps[:, 2 * s:2 * s + 2, :].rearrange("p k (b i j) -> p (k b) i j", i=NI, j=NI),
                                        channels(xT, n).unsqueeze(3).to_broadcast(wide), ALU.mult).then_inc(z_ready, 1)
                dve.wait_ge(z_ready, n + 1)
                nc.vector.tensor_reduce(channels(oT, n), z[:, s, :].rearrange("p (c i j) -> p c j i", i=NI, j=NI),
                                        AX.X, ALU.add).then_inc(head_out, 1)

            with dve.Fori(0, NH0 // 2) as i:
                for s in range(2):
                    gather(2 * i + s, s)
            dve.wait_ge(head_out, NH0)
            dve.wait_ge(skip_term, 1)
            nc.vector.tensor_tensor(oT[:, :, :], oT[:, :, :], vx[:, :, :], ALU.add).then_inc(oT_done, 1)
            for h in range(B // 2):
                dve.wait_ge(back_mm, h + 1)
                dst = g.x_sb[:, 2 * h:2 * h + 2, :]
                nc.vector.tensor_tensor(dst, dst, g.ps[:, 4 + h, :].rearrange("p (j l) -> p j l", j=2), ALU.add).then_inc(back_added, 1)
            dve.wait_ge(back_added, B // 2)


ROUND = 1.5 * 2.0 ** 23


class GatedExpert:

    def __init__(self, nc, g, tag, ctx, nf, kept):
        self.nc, self.g, self.nf, self.kept = nc, g, nf, kept
        self.sg = ctx.enter_context(nc.sbuf_tensor(tag + "_sg", [P, 2, 512], F32))
        self.h = ctx.enter_context(nc.sbuf_tensor(tag + "_h", [P, kept, nf, 512], F32))
        self.gu_mm = ctx.enter_context(nc.semaphore(tag + "_gu_mm"))
        self.silu_done = ctx.enter_context(nc.semaphore(tag + "_silu_done"))
        self.h_ready = ctx.enter_context(nc.semaphore(tag + "_h_ready"))
        self.y_mm = ctx.enter_context(nc.semaphore(tag + "_y_mm"))
        self.y_added = ctx.enter_context(nc.semaphore(tag + "_y_added"))

    def tensor_block(self, half, f, gu):
        nc, g, nf = self.nc, self.g, self.nf
        n = nf * half + f
        if n >= 2:
            nc.tensor.wait_ge(self.h_ready, n - 1)
        for a in range(2):
            col = (a * nf + f) * P
            for k in range(KD):
                mm = nc.tensor.matmul(g.ps[:, 2 * (f % 2) + a, :], gu[:, k, col:col + P],
                                      g.xnT[:, k, half * 512:(half + 1) * 512], start=(k == 0), stop=(k == KD - 1))
        mm.then_inc(self.gu_mm, 1)

    def tensor_down(self, half, dn):
        nc, g, nf = self.nc, self.g, self.nf
        nc.tensor.wait_ge(self.h_ready, nf * (half + 1))
        for q in (2 * half, 2 * half + 1):
            for j in range(2):
                t = 2 * (q % 2) + j
                for f in range(nf):
                    mm = nc.tensor.matmul(g.ps[:, 4 + q, j * D:(j + 1) * D], self.h[:, half % self.kept, f, t * P:(t + 1) * P],
                                          dn[:, f, :], start=(f == 0), stop=(f == nf - 1))
            mm.then_inc(self.y_mm, 1)

    def scalar_block(self, act, half, f):
        nc, g, nf = self.nc, self.g, self.nf
        n = nf * half + f
        act.wait_ge(self.gu_mm, n + 1)
        if n >= 2:
            act.wait_ge(self.h_ready, n - 1)
        nc.scalar.activation(self.sg[:, n % 2, :], g.ps[:, 2 * (n % 2), :], ACT.Silu).then_inc(self.silu_done, 1)

    def vector_block(self, dve, half, f):
        nc, g, nf = self.nc, self.g, self.nf
        n = nf * half + f
        dve.wait_ge(self.silu_done, n + 1)
        nc.vector.tensor_tensor(self.h[:, half % self.kept, f, :], self.sg[:, n % 2, :], g.ps[:, 2 * (n % 2) + 1, :],
                                ALU.mult).then_inc(self.h_ready, 1)

    def vector_add(self, dve, q):
        nc, g = self.nc, self.g
        dve.wait_ge(self.y_mm, q + 1)
        dst = g.x_sb[:, 2 * q:2 * q + 2, :]
        nc.vector.tensor_tensor(dst, dst, g.ps[:, 4 + q, :].rearrange("p (j n) -> p j n", j=2), ALU.add).then_inc(self.y_added, 1)


def layer0_experts(nc, g):
    with ExitStack() as ctx:
        def sb(name, shape, dt=F32):
            return whole(ctx.enter_context(nc.sbuf_tensor(name, shape, dt)), shape)

        def sem(name):
            return ctx.enter_context(nc.semaphore(name))

        ln = g.ln
        ex = GatedExpert(nc, g, "c", ctx, 4, 1)
        gate_w = sb("c_gate_w", [P, KD, NE])
        lmax, lsum, lrec = sb("c_lmax", [P, B]), sb("c_lsum", [P, B]), sb("c_lrec", [P, B])
        prob = sb("c_prob", [P, B, NE])
        above = sb("c_above", [P, B, NE, NE])
        tied = sb("c_tied", [P, B, NE, NE])
        rank = sb("c_rank", [P, B, NE])
        chosen = sb("c_chosen", [P, B, NE])
        weight = sb("c_weight", [P, TOP, B])
        tiles_of = sb("c_tiles_of", [P, NE])
        tiles_to = sb("c_tiles_to", [P, NE])
        tiles_from = sb("c_tiles_from", [P, NE])
        place = sb("c_place", [P, B, NE])
        mine_at = sb("c_mine_at", [P, B, NE])
        slot = sb("c_slot", [P, TOP, B], mybir.dt.uint32)
        past = sb("c_past", [P, TILES, NE])
        expert_f = sb("c_expert_f", [P, TILES])
        expert_of = sb("c_expert_of", [P, TILES], mybir.dt.int32)
        HID = 4 * P
        rows = sb("c_rows", [P, 2, D])
        rowsT = sb("c_rowsT", [P, 2, KD, P])
        sg = g.xn[:, 0:B // 2, :].rearrange("p (s b) d -> p s (b d)", s=2)
        hid = g.xn[:, B // 2:B, :].rearrange("p (s b) d -> p s (b d)", s=2)
        hidT = sb("c_tile_hT", [P, 2, 4, P])
        y = sb("c_tile_y", [P, 2, D])
        back = g.expert_back
        gate_in, logit_mm, expd = sem("gate_in"), sem("logit_mm"), sem("c_expd")
        step = sem("router_step")
        chosen_ready, place_mm, slots_ready, tiles_ready = sem("chosen_ready"), sem("place_mm"), sem("slots_ready"), sem("tiles_ready")
        scattered = sem("scattered")
        rows_in = [sem("rows_in0"), sem("rows_in1")]
        rows_mm, rowsT_out, tile_mm, tile_silu, tile_h = sem("rows_mm"), sem("rowsT_out"), sem("tile_mm"), sem("tile_silu"), sem("tile_h")
        hT_mm, hT_out, tile_y_mm, tile_y_out = sem("hT_mm"), sem("hT_out"), sem("tile_y_mm"), sem("tile_y_out")
        y_stored = [sem("y_stored0"), sem("y_stored1")]
        gathered, back_added = sem("gathered"), sem("c_back_added")
        quant = Ternary(nc, g, ctx)
        X_BANK, H_BANK, Y_BANK = 4, 5, 6
        LOOP = (TILES - 3) // 2
        assert 2 + 2 * LOOP == TILES - 1

        block = ctx.enter_context(nc.Block())

        @block.sync
        def _(sp):
            sp.dma_start(gate_w[:, :, :], g.gate_w.rearrange("(k p) n -> p k n", k=KD)).then_inc(gate_in, 16)

            def load(n, s):
                sp.dma_start(rows[:, s, :], g.slots_x[bass.ds(n * P, P), :]).then_inc(rows_in[s], 16)

            def store(n, s):
                sp.wait_ge(tile_y_out, n + 1)
                sp.dma_start(g.slots_y[bass.ds(n * P, P), :], y[:, s, :]).then_inc(y_stored[s], 16)

            sp.wait_ge(scattered, 16 * TOP * B)
            load(0, 0)
            load(1, 1)
            sp.wait_ge(rows_mm, 1)
            load(2, 0)
            sp.wait_ge(rows_mm, 2)
            load(3, 1)
            with sp.Fori(0, LOOP - 1) as i:
                for s in range(2):
                    store(2 * i + s, s)
                    sp.wait_ge(rows_mm, 2 * i + s + 3)
                    load(2 * i + s + 4, s)
            last = 2 * LOOP - 2
            store(last, 0)
            sp.wait_ge(rows_mm, last + 3)
            load(last + 4, 0)
            for n in range(last + 1, TILES):
                store(n, n % 2)

        @block.gpsimd
        def _(pool):
            ln.gpsimd(pool, 1)
            pool.wait_ge(g.slots_clear, 16)
            pool.wait_ge(slots_ready, 1)
            for r in range(TOP):
                for b in range(B):
                    nc.gpsimd.indirect_dma_start(g.slots_x[:, :], bass.IndirectOffsetOnAxis(ap=slot[:, r, b:b + 1], axis=0),
                                                 g.xn[:, b, :], None).then_inc(scattered, 16)
            quant.gpsimd(pool)
            for s in range(2):
                pool.wait_ge(y_stored[s], 16 * ((TILES + 1 - s) // 2))
            for b in range(B):
                for r in range(TOP):
                    nc.gpsimd.indirect_dma_start(back[:, r, b, :], None, g.slots_y[:, :],
                                                 bass.IndirectOffsetOnAxis(ap=slot[:, r, b:b + 1], axis=0)).then_inc(gathered, 16)

        @block.tensor
        def _(pe):
            ln.tensor(pe, 1)
            pe.wait_ge(gate_in, 16)
            for b in range(B):
                if b % 2 == 0:
                    pe.wait_ge(ln.turned_out, ln.out(1, b // 2 + 1))
                for k in range(KD):
                    mm = nc.tensor.matmul(g.ps[:, 7, b * NE:(b + 1) * NE], g.xnT[:, k, b * S:(b + 1) * S], gate_w[:, k, :],
                                          start=(k == 0), stop=(k == KD - 1))
            mm.then_inc(logit_mm, 1)
            pe.wait_ge(g.base_in, 32)
            ex.tensor_block(0, 0, g.base_gu)
            ex.tensor_block(0, 1, g.base_gu)
            pe.wait_ge(chosen_ready, 1)
            earlier, ones = g.const[:, C_EARLIER:C_EARLIER + P], g.const[:, C_ONES:C_ONES + P]
            flat = chosen.rearrange("p b e -> p (b e)")
            nc.tensor.matmul(g.ps[:, 7, 64:128], earlier, flat, start=True, stop=False, skip_group_check=True)
            for b in range(B - 1):
                nc.tensor.matmul(g.ps[:, 7, 64 + NE * (b + 1):128], ones, chosen[:, b, :].unsqueeze(1).to_broadcast([P, B - 1 - b, NE]),
                                 start=False, stop=False, skip_group_check=True)
            for b in range(B):
                mm = nc.tensor.matmul(g.ps[:, 7, 128:128 + NE], ones, chosen[:, b, :], start=False, stop=True, skip_group_check=True)
            mm.then_inc(place_mm, 1)
            ex.tensor_block(0, 2, g.base_gu)
            ex.tensor_block(0, 3, g.base_gu)
            ex.tensor_down(0, g.base_dn)

            def turn_rows(n, s, i, first=False):
                pe.wait_ge(rows_in[s], 16 * (i + 1))
                if not first:
                    pe.wait_ge(rowsT_out, n)
                for k in range(KD):
                    mm = nc.tensor.transpose(g.ps[:, X_BANK, k * P:(k + 1) * P], rows[:, s, k * P:(k + 1) * P], g.ident)
                mm.then_inc(rows_mm, 1)

            def up(n, s, first=False):
                pe.wait_ge(rowsT_out, n + 1)
                if not first:
                    pe.wait_ge(tile_h, n - 1)
                e = pe.value_load(expert_of[0:1, bass.ds(n, 1)], min_val=0, max_val=NE - 1)
                for a in range(2):
                    for k in range(KD):
                        mm = nc.tensor.matmul(g.ps[:, 2 * s + a, :], rowsT[:, s, k, :], g.ex_gu[:, e, k, a * HID:(a + 1) * HID],
                                              start=(k == 0), stop=(k == KD - 1))
                mm.then_inc(tile_mm, 1)

            def turn_h(n, s, first=False):
                pe.wait_ge(tile_h, n + 1)
                if not first:
                    pe.wait_ge(hT_out, n)
                for f in range(4):
                    mm = nc.tensor.transpose(g.ps[:, H_BANK, f * P:(f + 1) * P], hid[:, s, f * P:(f + 1) * P], g.ident)
                mm.then_inc(hT_mm, 1)

            def down(n, s, first=False):
                pe.wait_ge(hT_out, n + 1)
                if not first:
                    pe.wait_ge(tile_y_out, n - 1)
                e = pe.value_load(expert_of[0:1, bass.ds(n, 1)], min_val=0, max_val=NE - 1)
                for f in range(4):
                    mm = nc.tensor.matmul(g.ps[:, Y_BANK + s, 0:D], hidT[:, s, f, :], g.ex_dn[:, e, f, :],
                                          start=(f == 0), stop=(f == 3))
                mm.then_inc(tile_y_mm, 1)

            pe.wait_ge(g.ex_in, 32 * NE)
            pe.wait_ge(tiles_ready, 1)
            pe.wait_ge(ex.y_added, 2)
            turn_rows(0, 0, 0, True)
            turn_rows(1, 1, 0)
            up(0, 0, True)
            up(1, 1, True)
            turn_h(0, 0, True)
            turn_rows(2, 0, 1)

            def pair(i, first):
                for s in range(2):
                    n = 2 * i + s
                    up(n, s)
                    turn_h(n - 1, 1 - s)
                    turn_rows(n + 1, 1 - s, i + s)
                    down(n - 2, s, first)

            pair(1, True)
            with pe.Fori(2, LOOP + 1) as i:
                pair(i, False)
            last = TILES - 1
            up(last, 0)
            turn_h(last - 1, 1)
            down(last - 2, 0)
            turn_h(last, 0)
            down(last - 1, 1)
            down(last, 0)
            for f in range(4):
                ex.tensor_block(1, f, g.base_gu)
            pe.wait_ge(tile_y_out, TILES)
            ex.tensor_down(1, g.base_dn)

        @block.scalar
        def _(act):
            ln.scalar(act, 1, pair_of(g.xnT))
            act.wait_ge(step, 2)
            nc.scalar.activation(prob[:, :, :], prob[:, :, :], ACT.Exp).then_inc(expd, 1)
            for f in range(4):
                ex.scalar_block(act, 0, f)

            def rows_out(n, s):
                act.wait_ge(rows_mm, n + 1)
                nc.scalar.copy(rowsT[:, s], g.ps[:, X_BANK, 0:D].rearrange("p (k t) -> p k t", k=KD)).then_inc(rowsT_out, 1)

            def silu(n, s):
                act.wait_ge(tile_mm, n + 1)
                nc.scalar.activation(sg[:, s, :], g.ps[:, 2 * s, :], ACT.Silu).then_inc(tile_silu, 1)

            def h_out(n, s):
                act.wait_ge(hT_mm, n + 1)
                nc.scalar.copy(hidT[:, s], g.ps[:, H_BANK, :].rearrange("p (f t) -> p f t", f=4)).then_inc(hT_out, 1)

            rows_out(0, 0)
            rows_out(1, 1)
            silu(0, 0)
            silu(1, 1)
            h_out(0, 0)
            rows_out(2, 0)
            with act.Fori(1, LOOP + 1) as i:
                for s in range(2):
                    n = 2 * i + s
                    silu(n, s)
                    h_out(n - 1, 1 - s)
                    rows_out(n + 1, 1 - s)
            last = TILES - 1
            silu(last, 0)
            h_out(last - 1, 1)
            h_out(last, 0)
            for f in range(4):
                ex.scalar_block(act, 1, f)

        @block.vector
        def _(dve):
            ln.vector(dve, 1)
            wide = [P, B, NE, NE]
            mine, other = prob.unsqueeze(3).to_broadcast(wide), prob.unsqueeze(2).to_broadcast(wide)
            per_token = [P, B, NE]
            done = 0

            def stepped(ins):
                nonlocal done
                done += 1
                ins.then_inc(step, 1)
                dve.wait_ge(step, done)

            dve.wait_ge(logit_mm, 1)
            logits = g.ps[:, 7, 0:B * NE].rearrange("p (b e) -> p b e", b=B)
            stepped(nc.vector.tensor_reduce(lmax[:, :], logits, AX.X, ALU.max))
            stepped(nc.vector.tensor_tensor(prob[:, :, :], logits, lmax.unsqueeze(2).to_broadcast(per_token), ALU.subtract))
            dve.wait_ge(expd, 1)
            stepped(nc.vector.tensor_reduce(lsum[:, :], prob[:, :, :], AX.X, ALU.add))
            stepped(nc.vector.reciprocal(lrec[:, :], lsum[:, :]))
            stepped(nc.vector.tensor_tensor(prob[:, :, :], prob[:, :, :], lrec.unsqueeze(2).to_broadcast(per_token), ALU.mult))
            stepped(nc.vector.tensor_tensor(above[:, :, :, :], other, mine, ALU.is_gt))
            stepped(nc.vector.tensor_tensor(tied[:, :, :, :], other, mine, ALU.is_equal))
            lower = g.const[:, C_LOWER:C_LOWER + NE * NE].rearrange("p (e j) -> p e j", e=NE).unsqueeze(1).to_broadcast(wide)
            stepped(nc.vector.tensor_tensor(tied[:, :, :, :], tied[:, :, :, :], lower, ALU.mult))
            stepped(nc.vector.tensor_tensor(above[:, :, :, :], above[:, :, :, :], tied[:, :, :, :], ALU.add))
            stepped(nc.vector.tensor_reduce(rank[:, :, :], above[:, :, :, :], AX.X, ALU.add))
            nc.vector.tensor_scalar(chosen[:, :, :], rank[:, :, :], float(TOP), None, ALU.is_lt).then_inc(chosen_ready, 1)
            ex.vector_block(dve, 0, 0)
            ex.vector_block(dve, 0, 1)
            dve.wait_ge(place_mm, 1)
            places = g.ps[:, 7, 64:128].rearrange("p (b e) -> p b e", b=B)
            stepped(nc.vector.tensor_scalar(tiles_of[:, :], g.ps[:, 7, 128:128 + NE], 1.0 / P, (P - 1) / P - 0.5 + 0.5 / P, ALU.mult, ALU.add))
            stepped(nc.vector.tensor_scalar(tiles_of[:, :], tiles_of[:, :], ROUND, None, ALU.add))
            stepped(nc.vector.tensor_scalar(tiles_of[:, :], tiles_of[:, :], ROUND, None, ALU.subtract))
            stepped(nc.vector.tensor_tensor_scan(tiles_to[:, :], g.const[:, C_ONES:C_ONES + NE], tiles_of[:, :], 0.0, ALU.mult, ALU.add))
            stepped(nc.vector.tensor_tensor(tiles_from[:, :], tiles_to[:, :], tiles_of[:, :], ALU.subtract))
            stepped(nc.vector.scalar_tensor_tensor(out=place[:, :, :], in0=tiles_from.unsqueeze(1).to_broadcast(per_token), scalar=float(P),
                                                   in1=places, op0=ALU.mult, op1=ALU.add))
            for r in range(TOP):
                stepped(nc.vector.scalar_tensor_tensor(out=mine_at[:, :, :], in0=rank[:, :, :], scalar=float(r), in1=place[:, :, :],
                                                       op0=ALU.is_equal, op1=ALU.mult))
                stepped(nc.vector.tensor_reduce(lmax[:, :], mine_at[:, :, :], AX.X, ALU.add))
                stepped(nc.vector.tensor_copy(slot[:, r, :], lmax[:, :]))
            dve.sem_inc(slots_ready, 1)
            stepped(nc.vector.tensor_tensor(past[:, :, :], tiles_to.unsqueeze(1).to_broadcast([P, TILES, NE]),
                                            g.const[:, C_COUNT:C_COUNT + TILES].unsqueeze(2).to_broadcast([P, TILES, NE]), ALU.is_le))
            stepped(nc.vector.tensor_reduce(expert_f[:, :], past[:, :, :], AX.X, ALU.add))
            stepped(nc.vector.tensor_scalar(expert_f[:, :], expert_f[:, :], float(NE - 1), None, ALU.min))
            nc.vector.tensor_copy(expert_of[:, :], expert_f[:, :]).then_inc(tiles_ready, 1)
            ex.vector_block(dve, 0, 2)
            ex.vector_block(dve, 0, 3)
            for r in range(TOP):
                stepped(nc.vector.scalar_tensor_tensor(out=mine_at[:, :, :], in0=rank[:, :, :], scalar=float(r), in1=prob[:, :, :],
                                                       op0=ALU.is_equal, op1=ALU.mult))
                stepped(nc.vector.tensor_reduce(weight[:, r, :], mine_at[:, :, :], AX.X, ALU.add))
            stepped(nc.vector.tensor_tensor(lsum[:, :], weight[:, 0, :], weight[:, 1, :], ALU.add))
            stepped(nc.vector.reciprocal(lrec[:, :], lsum[:, :]))
            stepped(nc.vector.tensor_tensor(weight[:, :, :], weight[:, :, :], lrec.unsqueeze(1).to_broadcast([P, TOP, B]), ALU.mult))
            ex.vector_add(dve, 0)
            ex.vector_add(dve, 1)
            quant.vector(dve)

            def hidden(n, s, first=False):
                dve.wait_ge(tile_silu, n + 1)
                if not first:
                    dve.wait_ge(hT_mm, n - 1)
                nc.vector.tensor_tensor(hid[:, s, :], sg[:, s, :], g.ps[:, 2 * s + 1, :], ALU.mult).then_inc(tile_h, 1)

            def y_out(n, s, i, first=False):
                dve.wait_ge(tile_y_mm, n + 1)
                if not first:
                    dve.wait_ge(y_stored[s], 16 * i)
                nc.vector.tensor_copy(y[:, s, :], g.ps[:, Y_BANK + s, 0:D]).then_inc(tile_y_out, 1)

            hidden(0, 0, True)
            hidden(1, 1, True)
            for s in range(2):
                hidden(2 + s, s)
                y_out(s, s, 0, True)
            with dve.Fori(2, LOOP + 1) as i:
                for s in range(2):
                    hidden(2 * i + s, s)
                    y_out(2 * i + s - 2, s, i - 1)
            last = TILES - 1
            hidden(last, 0)
            for n in range(last - 2, TILES):
                y_out(n, n % 2, n // 2)
            for f in range(4):
                ex.vector_block(dve, 1, f)
            for b in range(B):
                dve.wait_ge(gathered, 16 * TOP * B)
                for r in range(TOP):
                    if r > 0:
                        dve.wait_ge(back_added, TOP * b + r)
                    nc.vector.scalar_tensor_tensor(out=g.x_sb[:, b, :], in0=back[:, r, b, :], scalar=weight[:, r, b:b + 1],
                                                   in1=g.x_sb[:, b, :], op0=ALU.mult, op1=ALU.add).then_inc(back_added, 1)
            dve.wait_ge(back_added, TOP * B)
            ex.vector_add(dve, 2)
            ex.vector_add(dve, 3)
            dve.wait_ge(ex.y_added, 4)


class Ternary:

    def __init__(self, nc, g, ctx):
        self.nc, self.g = nc, g
        self.asum = ctx.enter_context(nc.sbuf_tensor("t_asum", [P, 2], F32))
        self.total = ctx.enter_context(nc.sbuf_tensor("t_total", [P, 2], F32))
        self.inv = ctx.enter_context(nc.sbuf_tensor("t_inv", [P, 2], F32))
        self.asum_done = ctx.enter_context(nc.semaphore("ternary_asum_done"))
        self.total_done = ctx.enter_context(nc.semaphore("ternary_total_done"))
        self.step = ctx.enter_context(nc.semaphore("ternary_step"))

    def gpsimd(self, pool):
        pool.wait_ge(self.asum_done, 2)
        self.nc.gpsimd.partition_all_reduce(self.total[:, :], self.asum[:, :], P,
                                            bass.bass_isa.ReduceOp.add).then_inc(self.total_done, 1)

    def vector(self, dve):
        nc, g = self.nc, self.g
        raws, outs = (g.wqkv1_raw, g.wproj1_raw), (g.wqkv1, g.wproj1)
        dve.wait_ge(g.wqkv1_in, 16)
        dve.wait_ge(g.wproj1_in, 16)
        for i, raw in enumerate(raws):
            nc.vector.tensor_reduce(self.asum[:, i:i + 1], raw.rearrange("p k n -> p (k n)"), AX.X, ALU.add,
                                    apply_absolute_value=True).then_inc(self.asum_done, 1)
        dve.wait_ge(self.total_done, 1)
        done = 0
        for i, raw in enumerate(raws):
            n = P * raw.shape[1] * raw.shape[2]
            nc.vector.tensor_scalar(g.wmean[:, i:i + 1], self.total[:, i:i + 1], 1.0 / n, 1e-5, ALU.mult, ALU.max).then_inc(self.step, 1)
            done += 1
            dve.wait_ge(self.step, done)
            nc.vector.reciprocal(self.inv[:, i:i + 1], g.wmean[:, i:i + 1]).then_inc(self.step, 1)
            done += 1
            dve.wait_ge(self.step, done)
            nc.vector.tensor_scalar(raw[:, :, :], raw[:, :, :], self.inv[:, i:i + 1], ROUND, ALU.mult, ALU.add).then_inc(self.step, 1)
            done += 1
            dve.wait_ge(self.step, done)
            nc.vector.tensor_scalar(raw[:, :, :], raw[:, :, :], ROUND, 1.0, ALU.subtract, ALU.min).then_inc(self.step, 1)
            done += 1
            dve.wait_ge(self.step, done)
            nc.vector.tensor_scalar(outs[i][:, :, :], raw[:, :, :], -1.0, None, ALU.max).then_inc(self.step, 1)
            done += 1
        dve.wait_ge(self.step, done)


NH1, HD1 = 16, 16
SLOT = 32
QUADS = NH1 * SLOT // P


class QuantizedTokens:

    def __init__(self, nc, g, tag, ctx, which):
        self.nc, self.g, self.which = nc, g, which
        def sb(name, shape, dt=F32):
            return whole(ctx.enter_context(nc.sbuf_tensor(tag + name, shape, dt)), shape)
        self.amax = sb("_amax", [P, B])
        self.inv = sb("_inv", [P, B])
        self.scale = sb("_scale", [P, B, 1])
        self.ints = sb("_ints", [P, B, D], BF16)
        self.intsT = sb("_intsT", [P, KD, B * S], BF16)
        self.step = ctx.enter_context(nc.semaphore(tag + "_q_step"))
        self.ints_ready = ctx.enter_context(nc.semaphore(tag + "_q_ints_ready"))
        self.turned_mm = ctx.enter_context(nc.semaphore(tag + "_q_turned_mm"))
        self.turned_out = ctx.enter_context(nc.semaphore(tag + "_q_turned_out"))

    def vector(self, dve, src):
        nc, g = self.nc, self.g
        def step(ins, n):
            ins.then_inc(self.step, 1)
            dve.wait_ge(self.step, n)
        step(nc.vector.tensor_reduce(self.amax[:, :], src, AX.X, ALU.max, apply_absolute_value=True), 1)
        step(nc.vector.tensor_scalar(self.amax[:, :], self.amax[:, :], 1e-5, None, ALU.max), 2)
        step(nc.vector.reciprocal(self.inv[:, :], self.amax[:, :]), 3)
        step(nc.vector.tensor_scalar(self.inv[:, :], self.inv[:, :], 127.0, None, ALU.mult), 4)
        step(nc.vector.tensor_scalar(self.scale[:, :, 0], self.amax[:, :], 1.0 / 127.0, g.wmean[:, self.which:self.which + 1],
                                     ALU.mult, ALU.mult), 5)
        for h in range(B // 2):
            for b in (2 * h, 2 * h + 1):
                ins = nc.vector.tensor_scalar(src[:, b, :], src[:, b, :], self.inv[:, b:b + 1], ROUND, ALU.mult, ALU.add)
            step(ins, 6 + 2 * h)
            two = src[:, 2 * h:2 * h + 2, :]
            step(nc.vector.tensor_scalar(two, two, ROUND, 127.0, ALU.subtract, ALU.min), 7 + 2 * h)
            nc.vector.tensor_scalar(self.ints[:, 2 * h:2 * h + 2, :], two, -128.0, None, ALU.max).then_inc(self.ints_ready, 1)

    def tensor(self, pe):
        nc, g = self.nc, self.g
        for h in range(B // 2):
            pe.wait_ge(self.ints_ready, h + 1)
            for k in range(KD):
                for j in range(2):
                    mm = nc.tensor.matmul(g.ps[:, h, (2 * k + j) * S:(2 * k + j + 1) * S],
                                          self.ints[:, 2 * h + j, k * P:(k + 1) * P], g.ident_bf, start=True, stop=True)
            mm.then_inc(self.turned_mm, 1)

    def scalar(self, act):
        nc, g = self.nc, self.g
        for h in range(B // 2):
            act.wait_ge(self.turned_mm, h + 1)
            nc.scalar.copy(self.intsT[:, :, 2 * h * S:2 * (h + 1) * S],
                           g.ps[:, h, :].rearrange("p (k s) -> p k s", k=KD)).then_inc(self.turned_out, 1)


def layer1_attention(nc, g):
    with ExitStack() as ctx:
        def sb(name, shape, dt=F32):
            return whole(ctx.enter_context(nc.sbuf_tensor(name, shape, dt)), shape)

        def sem(name):
            return ctx.enter_context(nc.semaphore(name))

        ln = g.ln
        qin = QuantizedTokens(nc, g, "d_in", ctx, 0)
        qout = QuantizedTokens(nc, g, "d_out", ctx, 1)
        qk_pad = sb("d_qk_pad", [P, 2 * NH1, SLOT])
        qkT = sb("d_qkT", [P, 2 * QUADS, S])
        v1 = sb("d_v1", [P, 2, NH1, SLOT])
        prob = sb("d_prob", [P, 2, 8, S])
        probT = sb("d_probT", [P, 2, 2, 4 * S])
        headT = sb("d_headT", [P, QUADS, S])
        rmax = sb("d_rmax", [P, 2, 8])
        rden = sb("d_rden", [P, NH1])
        att = sb("d_att", [P, B, D])
        ffn_gu, ffn_dn = sb("d_ffn_gu", [P, KD, 2048]), sb("d_ffn_dn", [P, 8, D])
        ffn_in, weights_hi, weights_lo = sem("ffn_in"), sem("weights_hi"), sem("weights_lo")
        cleared = sem("d_cleared")
        qk_mm, qk_out, v_mm, v_out = sem("d_qk_mm"), sem("d_qk_out"), sem("d_v_mm"), sem("d_v_out")
        qkT_mm, qkT_out = sem("d_qkT_mm"), sem("d_qkT_out")
        score_mm, rmax_done, shifted, expd = sem("d_score_mm"), sem("d_rmax_done"), sem("d_shifted"), sem("d_expd")
        probT_mm, probT_out, av_mm, rden_done, att_out = (
            sem("d_probT_mm"), sem("d_probT_out"), sem("d_av_mm"), sem("d_rden_done"), sem("d_att_out"))
        headT_out, back_mm = sem("d_headT_out"), sem("d_back_mm")
        y_mm, y_added = sem("d_y_mm"), sem("d_y_added")
        ps = g.ps
        T_BANK, PT_BANK, V_BANK, BACK_BANK, QK_BANK, AV_BANK = 0, 4, 4, 5, 6, 7
        U = 2
        LOOP = (B - 2) // 2

        block = ctx.enter_context(nc.Block())

        @block.sync
        def _(sp):
            sp.dma_start(ffn_gu[:, :, :], g.w_gu1.rearrange("(k p) n -> p k n", k=KD)).then_inc(ffn_in, 16)
            sp.dma_start(ffn_dn[:, :, :], g.w_dn1.rearrange("(k p) n -> p k n", p=P)).then_inc(ffn_in, 16)

        @block.gpsimd
        def _(pool):
            nc.gpsimd.memset(qk_pad[:, :, :], 0.0).then_inc(cleared, 1)
            nc.gpsimd.memset(v1[:, :, :, :], 0.0).then_inc(cleared, 1)
            pool.wait_ge(cleared, 2)
            nc.gpsimd.memset(v1[:, :, :, HD1:HD1 + 1], 1.0).then_inc(cleared, 1)
            ln.gpsimd(pool, 2)
            pool.wait_ge(ffn_in, 32)
            pieces = [(ffn_gu[:, k], g.gu_hi[:, k], g.gu_lo[:, k]) for k in range(KD)] + [(ffn_dn, g.dn_hi, g.dn_lo)]
            for i, (w, hi, lo) in enumerate(pieces):
                nc.gpsimd.tensor_copy(hi, w).then_inc(weights_hi, 1)
                pool.wait_ge(weights_hi, i + 1)
                nc.gpsimd.tensor_tensor(lo, w, hi, ALU.subtract).then_inc(weights_lo, 1)
            pool.wait_ge(weights_lo, len(pieces))

        @block.scalar
        def _(act):
            qin.scalar(act)

            def qkT_copy(b):
                for t in range(2):
                    act.wait_ge(qkT_mm, 2 * b + t + 1)
                    nc.scalar.copy(qkT[:, 4 * t:4 * t + 4, :], ps[:, T_BANK + t, :].rearrange("p (c s) -> p c s", c=4)).then_inc(qkT_out, 1)

            def exp(u, b):
                act.wait_ge(shifted, U * b + u + 1)
                nc.scalar.activation(prob[:, u], prob[:, u], ACT.Exp, scale=HD1 ** -0.5).then_inc(expd, 1)

            def probT_copy(u, b):
                for p in range(2):
                    act.wait_ge(probT_mm, 2 * (U * b + u) + p + 1)
                    nc.scalar.copy(probT[:, u, p, :], ps[:, PT_BANK + p, :]).then_inc(probT_out, 1)

            def headT_copy(b):
                act.wait_ge(av_mm, b + 1)
                nc.scalar.copy(headT[:, :, :], ps[:, AV_BANK, :].rearrange("p (c s) -> p c s", c=QUADS)).then_inc(headT_out, 1)

            def body(b, first, last):
                exp(0, b)
                if not first:
                    headT_copy(b - 1)
                exp(1, b)
                if not last:
                    qkT_copy(b + 1)
                probT_copy(0, b)
                probT_copy(1, b)

            qkT_copy(0)
            body(0, True, False)
            with act.Fori(1, B - 1) as b:
                body(b, False, False)
            body(B - 1, False, True)
            headT_copy(B - 1)
            qout.scalar(act)

        @block.tensor
        def _(pe):
            qin.tensor(pe)
            pe.wait_ge(qin.turned_out, B // 2)

            def project(b, bank, cols, done):
                for k in range(KD):
                    mm = nc.tensor.matmul(ps[:, bank, 0:cols.stop - cols.start], qin.intsT[:, k, bass.ds(b * S, S)],
                                          g.wqkv1[:, k, cols], start=(k == 0), stop=(k == KD - 1))
                mm.then_inc(done, 1)

            def project_qk(b):
                project(b, QK_BANK, slice(0, 2 * D), qk_mm)

            def project_v(b):
                project(b, V_BANK, slice(2 * D, 3 * D), v_mm)

            def turn_qk(b):
                pe.wait_ge(qk_out, b + 1)
                for t in range(2):
                    for c in range(4):
                        mm = nc.tensor.transpose(ps[:, T_BANK + t, c * S:(c + 1) * S],
                                                 qk_pad[:, 16 * t + 4 * c:16 * t + 4 * c + 4, :].rearrange("p h d -> p (h d)"), g.ident)
                    mm.then_inc(qkT_mm, 1)

            def score(u, b):
                for p in range(2):
                    nc.tensor.matmul(ps[:, 2 * u + p, :], g.ident_bf, g.causal_bf.unsqueeze(1).to_broadcast([P, 4, S]),
                                     start=True, stop=False, skip_group_check=True)
                for c in range(QUADS):
                    for p in range(2):
                        rows = slice(SLOT * (2 * u + p), SLOT * (2 * u + p) + HD1)
                        mm = nc.tensor.matmul(ps[:, 2 * u + p, c * S:(c + 1) * S], qkT[rows, c, :], qkT[rows, QUADS + c, :],
                                              start=False, stop=True, skip_group_check=True,
                                              tile_position=(SLOT * (2 * u + p), 0))
                mm.then_inc(score_mm, 1)

            def turn_prob(u, b):
                pe.wait_ge(expd, U * b + u + 1)
                if u == 1:
                    pe.wait_ge(probT_out, 2 * U * b + 2)
                for p in range(2):
                    for i in range(4):
                        mm = nc.tensor.transpose(ps[:, PT_BANK + p, i * S:(i + 1) * S], prob[:, u, 4 * p + i, :], g.ident)
                    mm.then_inc(probT_mm, 1)

            def attend(b, s):
                pe.wait_ge(probT_out, 2 * U * (b + 1))
                for c in range(QUADS):
                    for r in range(4):
                        mm = nc.tensor.matmul(ps[SLOT * r:SLOT * (r + 1), AV_BANK, c * S:(c + 1) * S], v1[:, s, 4 * c + r, :],
                                              probT[:, r // 2, r % 2, c * S:(c + 1) * S], start=True, stop=True,
                                              skip_group_check=True)
                mm.then_inc(av_mm, 1)

            def turn_back(b):
                pe.wait_ge(headT_out, b + 1)
                for c in range(QUADS):
                    mm = nc.tensor.transpose(ps[:, BACK_BANK, c * P:(c + 1) * P], headT[:, c, :], g.ident)
                mm.then_inc(back_mm, 1)

            def body(b, s, first, last):
                pe.wait_ge(qkT_out, 2 * b + 2)
                score(0, b)
                if not first:
                    pe.wait_ge(shifted, U * b)
                score(1, b)
                if not first:
                    pe.wait_ge(v_out, b)
                    attend(b - 1, 1 - s)
                if not last:
                    project_qk(b + 1)
                    if not first:
                        pe.wait_ge(probT_out, 2 * U * b)
                    project_v(b + 1)
                if not first:
                    turn_back(b - 1)
                if not last:
                    pe.wait_ge(shifted, U * b + 1)
                    turn_qk(b + 1)
                    pe.wait_ge(v_out, b + 2)
                if not first:
                    pe.wait_ge(att_out, b)
                turn_prob(0, b)
                turn_prob(1, b)

            project_qk(0)
            project_v(0)
            turn_qk(0)
            pe.wait_ge(v_out, 1)
            body(0, 0, True, False)
            with pe.Fori(0, LOOP) as i:
                for s in (1, 0):
                    body(2 * i + 2 - s, s, False, False)
            body(B - 1, 1, False, True)
            attend(B - 1, 1)
            turn_back(B - 1)
            qout.tensor(pe)
            for h in range(B // 2):
                pe.wait_ge(qout.turned_out, h + 1)
                for j in range(2):
                    b = 2 * h + j
                    for k in range(KD):
                        mm = nc.tensor.matmul(ps[:, 4 + h, j * D:(j + 1) * D], qout.intsT[:, k, b * S:(b + 1) * S],
                                              g.wproj1[:, k, :], start=(k == 0), stop=(k == KD - 1))
                mm.then_inc(y_mm, 1)

        @block.vector
        def _(dve):
            ln.vector(dve, 2)
            dve.wait_ge(ln.xn_ready, B * 3)
            qin.vector(dve, g.xn)
            dve.wait_ge(cleared, 3)

            def out_qk(b):
                dve.wait_ge(qk_mm, b + 1)
                if not isinstance(b, int) or b > 0:
                    dve.wait_ge(qkT_mm, 2 * b)
                nc.vector.tensor_scalar(qk_pad[:, :, 0:HD1], ps[:, QK_BANK, :].rearrange("p (h d) -> p h d", d=HD1),
                                        qin.scale[:, b, :], None, ALU.mult).then_inc(qk_out, 1)

            def out_v(b, s):
                dve.wait_ge(v_mm, b + 1)
                nc.vector.tensor_scalar(v1[:, s, :, 0:HD1], ps[:, V_BANK, 0:D].rearrange("p (h d) -> p h d", d=HD1),
                                        qin.scale[:, b, :], None, ALU.mult).then_inc(v_out, 1)

            def shift(u, b):
                n = U * b + u
                dve.wait_ge(score_mm, n + 1)
                s = ps[:, 2 * u:2 * u + 2, :].rearrange("p a (i k) -> p (a i) k", i=4)
                nc.vector.tensor_reduce(rmax[:, u, :], s, AX.X, ALU.max).then_inc(rmax_done, 1)
                dve.wait_ge(rmax_done, n + 1)
                nc.vector.tensor_tensor(prob[:, u], s, rmax[:, u, :].unsqueeze(2).to_broadcast([P, 8, S]),
                                        ALU.subtract).then_inc(shifted, 1)

            def normalise(b):
                dve.wait_ge(back_mm, b + 1)
                o = ps[:, BACK_BANK, :].rearrange("p (h d) -> p h d", h=NH1)
                nc.vector.reciprocal(rden[:, :], o[:, :, HD1]).then_inc(rden_done, 1)
                dve.wait_ge(rden_done, b + 1)
                nc.vector.tensor_tensor(att[:, b, :].rearrange("p (h d) -> p h d", h=NH1), o[:, :, 0:HD1],
                                        rden.unsqueeze(2).to_broadcast([P, NH1, HD1]), ALU.mult).then_inc(att_out, 1)

            def body(b, s, first, last):
                shift(0, b)
                shift(1, b)
                if not last:
                    out_qk(b + 1)
                    out_v(b + 1, 1 - s)
                if not first:
                    normalise(b - 1)

            out_qk(0)
            out_v(0, 0)
            body(0, 0, True, False)
            with dve.Fori(0, LOOP) as i:
                for s in (1, 0):
                    body(2 * i + 2 - s, s, False, False)
            body(B - 1, 1, False, True)
            normalise(B - 1)
            dve.wait_ge(att_out, B)
            qout.vector(dve, att)
            for h in range(B // 2):
                dve.wait_ge(y_mm, h + 1)
                for j in range(2):
                    b = 2 * h + j
                    nc.vector.scalar_tensor_tensor(out=g.x_sb[:, b, :], in0=ps[:, 4 + h, j * D:(j + 1) * D],
                                                   scalar=qout.scale[:, b, :], in1=g.x_sb[:, b, :],
                                                   op0=ALU.mult, op1=ALU.add).then_inc(y_added, 1)
            dve.wait_ge(y_added, B)


NEVER = -1e38


def layer1_wkv(nc, g):
    with ExitStack() as ctx:
        def sb(name, shape, dt=F32):
            return whole(ctx.enter_context(nc.sbuf_tensor(name, shape, dt)), shape)

        def sem(name):
            return ctx.enter_context(nc.semaphore(name))

        T = S + 1
        k_pad = sb("e_k", [P, KD, B, T])
        ln = g.ln
        decay, first = sb("e_decay", [P, KD]), sb("e_first", [P, KD])
        w = sb("e_w", [P, KD])
        steps = sb("e_steps", [P, KD, B, T])
        run = {n: sb("e_" + n, [P, KD, B, T]) for n in ("pp", "aa", "bb", "keep", "new", "new_v")}
        now_gap, old, now, num = (sb("e_" + n, [P, KD, B, S]) for n in ("now_gap", "old", "now", "num"))
        carry_gap, now_v = num, now_gap
        den = g.xnT.rearrange("p k (b s) -> p k b s", b=B)
        params_in, w_ready, padded, steps_ready = sem("e_params_in"), sem("e_w_ready"), sem("e_padded"), sem("e_steps_ready")
        pp_done, run_diff, now_diff, clipped = sem("e_pp_done"), sem("e_run_diff"), sem("e_now_diff"), sem("e_clipped")
        den_done, den_inv = sem("e_den_done"), sem("e_den_inv")
        exp_done, new_v_done, aa_done, bb_done = sem("e_exp_done"), sem("e_new_v_done"), sem("e_aa_done"), sem("e_bb_done")
        now_v_done, carried_done, den_step, num_done, y_done, back_mm, y_added = (
            sem("e_now_v_done"), sem("e_carried_done"), sem("e_den_step"), sem("e_num_done"), sem("e_y_done"), sem("e_back_mm"), sem("e_y_added"))

        def flat(t, k):
            return t[:, k].rearrange("p b t -> p (b t)")

        def at(n, k):
            return run[n][:, k, :, 1:T]

        def before(n, k):
            return run[n][:, k, :, 0:S]

        v = g.ctxT.rearrange("p k (b s) -> p k b s", b=B)
        block = ctx.enter_context(nc.Block())

        @block.sync
        def _(sp):
            sp.dma_start(decay[:, :], g.decay.rearrange("(k p) -> p k", k=KD), allow_slow_non_contiguous=True).then_inc(params_in, 16)
            sp.dma_start(first[:, :], g.first.rearrange("(k p) -> p k", k=KD), allow_slow_non_contiguous=True).then_inc(params_in, 16)

        @block.gpsimd
        def _(pool):
            nc.gpsimd.memset(k_pad[:, :, :, 0:1], NEVER).then_inc(padded, 1)
            nc.gpsimd.memset(run["keep"][:, :, :, 0:1], 0.0).then_inc(padded, 1)
            nc.gpsimd.memset(run["new"][:, :, :, 0:1], 0.0).then_inc(padded, 1)
            nc.gpsimd.memset(run["new_v"][:, :, :, 0:1], 0.0).then_inc(padded, 1)
            nc.gpsimd.memset(steps[:, :, :, :], 0.0).then_inc(steps_ready, 1)
            ln.gpsimd(pool, 3)
            pool.wait_ge(w_ready, 1)
            nc.gpsimd.tensor_scalar(w[:, :], w[:, :], -1.0, None, ALU.mult).then_inc(w_ready, 1)

            def inputs(k):
                pool.wait_ge(exp_done, 4 * k + 2)
                nc.gpsimd.tensor_tensor(at("new_v", k), at("new", k), v[:, k], ALU.mult).then_inc(new_v_done, 1)

            def own(k):
                pool.wait_ge(exp_done, 4 * k + 4)
                nc.gpsimd.tensor_tensor(now_v[:, k], now[:, k], v[:, k], ALU.mult).then_inc(now_v_done, 1)

            def carried(k):
                pool.wait_ge(aa_done, k + 1)
                nc.gpsimd.tensor_tensor(num[:, k], old[:, k], before("aa", k), ALU.mult).then_inc(carried_done, 1)

            def numerator(k):
                pool.wait_ge(now_v_done, k + 1)
                pool.wait_ge(carried_done, k + 1)
                nc.gpsimd.tensor_tensor(num[:, k], num[:, k], now_v[:, k], ALU.add).then_inc(num_done, 1)

            inputs(0)
            own(0)
            inputs(1)
            carried(0)
            numerator(0)
            own(1)
            carried(1)
            numerator(1)

        @block.scalar
        def _(act):
            act.wait_ge(params_in, 32)
            nc.scalar.activation(w[:, :], decay[:, :], ACT.Exp).then_inc(w_ready, 1)
            ln.scalar(act, 2, lambda h: k_pad[:, :, 2 * h:2 * h + 2, 1:T])
            n = 0
            for k in range(KD):
                for ready, diff, first_of, second_of in ((run_diff, carry_gap[:, k], at("keep", k), at("new", k)),
                                                         (now_diff, now_gap[:, k], now[:, k], old[:, k])):
                    act.wait_ge(ready, k + 1)
                    nc.scalar.activation(first_of, diff, ACT.Relu, scale=-1.0).then_inc(clipped, 1)
                    nc.scalar.activation(second_of, diff, ACT.Relu).then_inc(clipped, 1)
                    act.wait_ge(clipped, n + 1)
                    nc.scalar.activation(first_of, first_of, ACT.Exp, scale=-1.0).then_inc(exp_done, 1)
                    act.wait_ge(clipped, n + 2)
                    nc.scalar.activation(second_of, second_of, ACT.Exp, scale=-1.0).then_inc(exp_done, 1)
                    n += 2

        @block.tensor
        def _(pe):
            ln.tensor(pe, 3)
            for k in range(KD):
                pe.wait_ge(y_done, k + 1)
                for h in range(2):
                    for j in range(4):
                        mm = nc.tensor.transpose(g.ps[:, 4 + 2 * k + h, j * P:(j + 1) * P], num[:, k, 4 * h + j, :], g.ident)
                    mm.then_inc(back_mm, 1)

        @block.vector
        def _(dve):
            ln.vector(dve, 3)
            dve.wait_ge(w_ready, 2)
            dve.wait_ge(steps_ready, 1)
            for k in range(KD):
                nc.vector.tensor_scalar(steps[:, k], steps[:, k], w[:, k:k + 1], None, ALU.add).then_inc(steps_ready, 1)
            dve.wait_ge(steps_ready, 3)
            nc.vector.memset(steps[:, :, :, 0:1], NEVER).then_inc(steps_ready, 1)
            dve.wait_ge(steps_ready, 4)
            dve.wait_ge(padded, 4)

            def quotient(k):
                dve.wait_ge(den_inv, k + 1)
                dve.wait_ge(num_done, k + 1)
                nc.vector.tensor_tensor(num[:, k], num[:, k], den[:, k], ALU.mult).then_inc(y_done, 1)

            dve.wait_ge(ln.turned_out, ln.out(2))
            for k in range(KD):
                nc.vector.tensor_tensor_scan(flat(run["pp"], k), flat(steps, k), flat(k_pad, k), NEVER, ALU.add, ALU.max).then_inc(pp_done, 1)
                dve.wait_ge(pp_done, k + 1)
                k_now = k_pad[:, k, :, 1:T]
                nc.vector.scalar_tensor_tensor(out=carry_gap[:, k], in0=before("pp", k), scalar=w[:, k:k + 1], in1=k_now,
                                               op0=ALU.add, op1=ALU.subtract).then_inc(run_diff, 1)
                nc.vector.scalar_tensor_tensor(out=now_gap[:, k], in0=k_now, scalar=first[:, k:k + 1], in1=before("pp", k),
                                               op0=ALU.add, op1=ALU.subtract).then_inc(now_diff, 1)
            for k in range(KD):
                dve.wait_ge(exp_done, 4 * k + 2)
                nc.vector.tensor_tensor_scan(flat(run["bb"], k), flat(run["keep"], k), flat(run["new"], k), 0.0,
                                             ALU.mult, ALU.add).then_inc(bb_done, 1)
                dve.wait_ge(bb_done, k + 1)
                dve.wait_ge(exp_done, 4 * k + 4)
                nc.vector.tensor_tensor(den[:, k], old[:, k], before("bb", k), ALU.mult).then_inc(den_step, 1)
                dve.wait_ge(new_v_done, k + 1)
                nc.vector.tensor_tensor_scan(flat(run["aa"], k), flat(run["keep"], k), flat(run["new_v"], k), 0.0,
                                             ALU.mult, ALU.add).then_inc(aa_done, 1)
                dve.wait_ge(den_step, k + 1)
                nc.vector.tensor_tensor(den[:, k], den[:, k], now[:, k], ALU.add).then_inc(den_done, 1)
                if k > 0:
                    quotient(k - 1)
                dve.wait_ge(den_done, k + 1)
                nc.vector.reciprocal(den[:, k], den[:, k]).then_inc(den_inv, 1)
            quotient(KD - 1)
            for k in range(KD):
                for h in range(2):
                    dve.wait_ge(back_mm, 2 * k + h + 1)
                    dst = g.x_sb[:, 4 * h:4 * h + 4, k * P:(k + 1) * P]
                    nc.vector.tensor_tensor(dst, dst, g.ps[:, 4 + 2 * k + h, :].rearrange("p (j c) -> p j c", j=4),
                                            ALU.add).then_inc(y_added, 1)
            dve.wait_ge(y_added, 2 * KD)


def layer1_ffn(nc, g):
    with ExitStack() as ctx:
        def sb(name, shape, dt=F32):
            return whole(ctx.enter_context(nc.sbuf_tensor(name, shape, dt)), shape)

        def sem(name):
            return ctx.enter_context(nc.semaphore(name))

        NF, HALF = 8, B * S // 2
        BLOCKS = 2 * NF
        ln = g.ln
        x_hi, x_lo = sb("f_x_hi", [P, KD, B * S], F32R), sb("f_x_lo", [P, KD, B * S], F32R)
        h_hi, h_lo = sb("f_h_hi", [P, 2, NF, HALF], F32R), sb("f_h_lo", [P, 2, NF, HALF], F32R)
        silu = sb("f_silu", [P, 2, HALF])
        h = sb("f_h", [P, 3, HALF])
        x_split, gu_mm, silu_done, h_done = sem("f_x_split"), sem("f_gu_mm"), sem("f_silu_done"), sem("f_h_done")
        h_hi_done, h_split, y_mm, y_added, stored = (
            sem("f_h_hi_done"), sem("f_h_split"), sem("f_y_mm"), sem("f_y_added"), sem("stored"))
        block = ctx.enter_context(nc.Block())

        def parts(a_hi, a_lo, b_hi, b_lo):
            return (a_hi, b_hi), (a_hi, b_lo), (a_lo, b_hi)

        @block.gpsimd
        def _(pool):
            ln.gpsimd(pool, 4)

        @block.scalar
        def _(act):
            ln.scalar(act, 3, pair_of(x_hi))

            def high(n):
                act.wait_ge(h_done, n + 1)
                nc.scalar.copy(h_hi[:, n // NF, n % NF, :], h[:, n % 3, :]).then_inc(h_hi_done, 1)

            for n in range(BLOCKS):
                act.wait_ge(gu_mm, n + 1)
                if n >= 2:
                    act.wait_ge(h_done, n - 1)
                nc.scalar.activation(silu[:, n % 2, :], g.ps[:, 2 * (n % 2), :], ACT.Silu).then_inc(silu_done, 1)
                if n >= 1:
                    high(n - 1)
            high(BLOCKS - 1)

        @block.tensor
        def _(pe):
            ln.tensor(pe, 4)
            for n in range(BLOCKS):
                half, f = divmod(n, NF)
                if n == 0:
                    pe.wait_ge(x_split, 4)
                if n >= 2:
                    pe.wait_ge(h_done, n - 1)
                for a in range(2):
                    cols = slice((a * NF + f) * P, (a * NF + f + 1) * P)
                    toks = slice(half * HALF, (half + 1) * HALF)
                    terms = [(w[:, k, cols], x[:, k, toks]) for k in range(KD)
                             for w, x in parts(g.gu_hi, g.gu_lo, x_hi, x_lo)]
                    for i, (w, x) in enumerate(terms):
                        mm = nc.tensor.matmul(g.ps[:, 2 * (n % 2) + a, :], w, x, start=(i == 0), stop=(i == len(terms) - 1))
                mm.then_inc(gu_mm, 1)
            for q in range(4):
                half = q // 2
                if q == 0:
                    pe.wait_ge(h_split, NF)
                if q == 2:
                    pe.wait_ge(h_split, BLOCKS)
                for j in range(2):
                    t = 2 * (q % 2) + j
                    terms = [(hh[:, half, f, t * P:(t + 1) * P], w[:, f, :]) for f in range(NF)
                             for hh, w in parts(h_hi, h_lo, g.dn_hi, g.dn_lo)]
                    for i, (hh, w) in enumerate(terms):
                        mm = nc.tensor.matmul(g.ps[:, 4 + q, j * D:(j + 1) * D], hh, w, start=(i == 0), stop=(i == len(terms) - 1))
                mm.then_inc(y_mm, 1)

        @block.vector
        def _(dve):
            ln.vector(dve, 4)
            for q in range(4):
                dve.wait_ge(ln.turned_out, ln.out(3, q + 1))
                toks = slice(2 * q * S, 2 * (q + 1) * S)
                nc.vector.tensor_tensor(x_lo[:, :, toks], g.ps[:, q, :].rearrange("p (k s) -> p k s", k=KD), x_hi[:, :, toks],
                                        ALU.subtract).then_inc(x_split, 1)

            def low(n):
                dve.wait_ge(h_hi_done, n + 1)
                nc.vector.tensor_tensor(h_lo[:, n // NF, n % NF, :], h[:, n % 3, :], h_hi[:, n // NF, n % NF, :],
                                        ALU.subtract).then_inc(h_split, 1)

            for n in range(BLOCKS):
                dve.wait_ge(silu_done, n + 1)
                if n >= 3:
                    dve.wait_ge(h_split, n - 2)
                nc.vector.tensor_tensor(h[:, n % 3, :], silu[:, n % 2, :], g.ps[:, 2 * (n % 2) + 1, :], ALU.mult).then_inc(h_done, 1)
                if n >= 1:
                    low(n - 1)
            low(BLOCKS - 1)
            for q in range(4):
                dve.wait_ge(y_mm, q + 1)
                dst = g.x_sb[:, 2 * q:2 * q + 2, :]
                nc.vector.tensor_tensor(dst, dst, g.ps[:, 4 + q, :].rearrange("p (j n) -> p j n", j=2), ALU.add).then_inc(y_added, 1)

        @block.sync
        def _(sp):
            for q in range(4):
                sp.wait_ge(y_added, q + 1)
                sp.dma_start(g.out.rearrange("b s d -> s b d")[:, 2 * q:2 * q + 2, :], g.x_sb[:, 2 * q:2 * q + 2, :]).then_inc(stored, 16)
            sp.wait_ge(stored, 4 * 16)


LAYER0 = (layer0_attention, layer0_convolution, layer0_experts)
LAYER1 = (layer1_attention, layer1_wkv, layer1_ffn)


def clear(nc, g):
    with nc.Block() as block:
        @block.sync
        def _(sp):
            if g.stage_sems:
                numbers = [s.num for s in g.stage_sems]
                assert numbers == list(range(numbers[0], numbers[0] + len(numbers)))
                sp.sem_clear(range(numbers[0], numbers[0] + len(numbers)))
    g.stage_sems = []


class Shared:
    pass


def build(nc, args, out):
    g = Shared()
    g.out = out
    g.stage_sems = []
    (g.x, g.ctx, g.sink, g.w_qkv, g.w_out, g.table, g.skip, g.toeplitz, g.gate_w, g.w_gu, g.w_dn, g.w_qkv1, g.w_proj1,
     g.decay, g.first, g.w_gu1, g.w_dn1) = args
    with ExitStack() as ctx:
        def sb(name, shape, dt=F32):
            return whole(ctx.enter_context(nc.sbuf_tensor(name, shape, dt)), shape)

        def sem(name):
            return ctx.enter_context(nc.semaphore(name))

        g.ps = ctx.enter_context(nc.psum_tensor("ps", [P, 8, 512], F32))
        g.x_sb = sb("x_sb", [P, B, D])
        g.xn = sb("xn", [P, B, D])
        g.xnT = sb("xnT", [P, KD, B * S])
        g.ctxT = sb("ctxT", [P, KD, B * S])
        g.const = sb("const", [P, C_END])
        g.ident = g.const[:, C_ID:C_ID + P]
        masks = sb("masks", [P, 3, P], BF16)
        g.ident_bf, g.swa_bf, g.causal_bf = (masks[:, i, :] for i in range(3))
        g.neg_half = sb("neg_half", [P, 8])
        g.half_ready = sem("half_ready")
        g.ln = LayerNorm(nc, g, ctx)

        g.toep, g.toep_in = sb("toep_all", [P, NH0, 2 * P]), sem("toep_in")
        g.expert_back = g.toep.rearrange("p (r b) n -> p r b n", r=TOP)
        g.base_in, g.ex_in, g.slots_clear = sem("base_in"), sem("ex_in"), sem("slots_clear")
        g.wqkv1, g.wproj1 = sb("wqkv1", [P, KD, 3 * D], BF16), sb("wproj1", [P, KD, D], BF16)
        g.wmean = sb("wmean", [P, 2])
        g.wqkv1_in, g.wproj1_in = sem("wqkv1_in"), sem("wproj1_in")
        g.slots_x = nc.dram_tensor("slots_x", (TILES * P, D), F32, kind="Internal").ap()
        g.slots_y = nc.dram_tensor("slots_y", (TILES * P, D), F32, kind="Internal").ap()
        LAYER0[0](nc, g)
        clear(nc, g)
        with ExitStack() as experts:
            g.ex_gu = whole(experts.enter_context(nc.sbuf_tensor("ex_gu", [P, NE, KD, 1024], F32)), [P, NE, KD, 1024])
            g.ex_dn = whole(experts.enter_context(nc.sbuf_tensor("ex_dn", [P, NE, 4, D], F32)), [P, NE, 4, D])
            GU, DN = KD * 1024, 4 * D
            g.big_w = whole(experts.enter_context(nc.sbuf_tensor("big_w", [P, GU + DN + KD * 4 * D], F32)), [P, GU + DN + KD * 4 * D])
            at = 0
            g.base_gu = g.big_w[:, at:at + GU].rearrange("p (k n) -> p k n", k=KD)
            at += GU
            g.base_dn = g.big_w[:, at:at + DN].rearrange("p (f n) -> p f n", f=4)
            at += DN
            g.wqkv1_raw = g.big_w[:, at:at + KD * 3 * D].rearrange("p (k n) -> p k n", k=KD)
            at += KD * 3 * D
            g.wproj1_raw = g.big_w[:, at:at + KD * D].rearrange("p (k n) -> p k n", k=KD)
            for stage in LAYER0[1:]:
                stage(nc, g)
        g.gu_hi, g.gu_lo = sb("gu_hi", [P, KD, 2048], F32R), sb("gu_lo", [P, KD, 2048], F32R)
        g.dn_hi, g.dn_lo = sb("dn_hi", [P, 8, D], F32R), sb("dn_lo", [P, 8, D], F32R)
        for stage in LAYER1:
            stage(nc, g)


def kernel(**inputs):
    import concourse.bacc as _bacc
    from concourse import mybir as _mybir
    from concourse.bass_utils import run_bass_kernel_spmd as _run

    f = {k: np.ascontiguousarray(v) for k, v in inputs.items()}
    k = np.concatenate([np.zeros((16, P), np.float32), f["L0_xattn_k"]], axis=1)
    toeplitz = np.ascontiguousarray(k[:, P + np.arange(2 * P)[None, :] - np.arange(P)[:, None]])
    arrays = {
        "x": f["x"], "ctx": f["ctx_2048"], "sink": f["L0_attn_s"],
        "w_qkv": f["L0_attn_W_qkv"], "w_out": f["L0_attn_W_out"], "table": constants(),
        "skip": f["fside_S2_0"], "toeplitz": toeplitz, "gate_w": f["L0_ffn_gate_w"],
        "w_gu": np.concatenate([f["L0_ffn_expert_gate_up"], f["L0_ffn_base_gate_up"][None]]),
        "w_dn": np.concatenate([f["L0_ffn_expert_down"], f["L0_ffn_base_down"][None]]),
        "w_qkv1": np.ascontiguousarray(f["L1_attn_w_qkv"].T), "w_proj1": np.ascontiguousarray(f["L1_attn_w_proj"].T),
        "decay": f["L1_xattn_time_decay"], "first": f["L1_xattn_time_first"],
        "w_gu1": np.ascontiguousarray(f["L1_ffn_w_gate_up"].T), "w_dn1": np.ascontiguousarray(f["L1_ffn_w_down"].T),
    }
    nc = _bacc.Bacc("TRN2", target_bir_lowering=False, num_devices=1)
    args = [nc.dram_tensor(f"in_{n}_dram", a.shape, _mybir.dt.from_np(a.dtype), kind="ExternalInput").ap()
            for n, a in arrays.items()]
    out = nc.dram_tensor("out_0_dram", (B, S, D), F32, kind="ExternalOutput").ap()
    build(nc, args, out)
    r = _run(nc, [{f"in_{n}_dram": a for n, a in arrays.items()}], core_ids=[0])
    return r.results[0]["out_0_dram"]
```
